# Optimizing a Trainium2 kernel written in Bass

```python
import numpy as np
import jax
import jax.numpy as jnp

def _softmax(x, axis=-1):
    return jax.nn.softmax(x, axis=axis)

def _gelu(x):
    return jax.nn.gelu(x, approximate=True)

def _silu(x):
    return jax.nn.silu(x)

def _sigmoid(x):
    return jax.nn.sigmoid(x)

def _layernorm(x, axis=-1, eps=1e-05):
    m = jnp.mean(x, axis=axis, keepdims=True)
    v = jnp.var(x, axis=axis, keepdims=True)
    return (x - m) / jnp.sqrt(v + eps)

def _scatter_add(tgt, idx, src, axis=0):
    return tgt.at[idx].add(src)

def _segment_sum(src, seg, n):
    return jax.ops.segment_sum(src, seg, n)
kernel_name = 'mk_perceiver_d2_seqx_r4_be23e5'

def setup_inputs(seed: int=0):
    np.random.seed(seed)
    _w = jnp.asarray

    def _rec_inputs():
        import jax
        import jax.numpy as jnp
        _rk = jax.random.key(seed)
        x = -0.0002928 + 1 * jax.random.normal(jax.random.fold_in(_rk, 1), (32, 32, 256), jnp.float32)
        _lenS = 32 - jax.random.randint(jax.random.fold_in(_rk, 7), (32,), 0, max(1, 32 // 4) + 1, jnp.int32)
        _lenS2 = 257 - jax.random.randint(jax.random.fold_in(_rk, 8), (32,), 0, max(1, 257 // 4) + 1, jnp.int32)
        _ctx_1024P = jax.random.normal(jax.random.fold_in(_rk, 11), (32, 16, 256), jnp.float32)
        _ctx_1024c = jax.random.dirichlet(jax.random.fold_in(_rk, 511), 0.3 * jnp.ones((16,), jnp.float32), (32, 257))
        _ctx_1024t = jnp.einsum('bsk,bkd->bsd', _ctx_1024c, _ctx_1024P)
        _ctx_1024t = _ctx_1024t * jax.lax.rsqrt(jnp.mean(jnp.square(_ctx_1024t)) + 1e-12) * 0.953939
        ctx_1024 = -1.39393e-06 + 0.999914 * (_ctx_1024t + 0.3 * jax.random.normal(jax.random.fold_in(_rk, 611), (32, 257, 256), jnp.float32))
        return (x, ctx_1024)
    x, ctx_1024 = _rec_inputs()

    def _L0_xattn_setup():
        import jax, jax.numpy as jnp
        import numpy as np
        import math
        D_MODEL = 256
        NUM_HEADS = 16
        D_K = D_MODEL // NUM_HEADS
        B, SQ, SK = (2, 512, 512)

        def _alibi_bias(seq_len_q: int, seq_len_k: int, dtype) -> jnp.ndarray:
            slopes = jnp.asarray([2.0 ** (-8.0 * (i + 1) / NUM_HEADS) for i in range(NUM_HEADS)], dtype=dtype)
            q_pos = jnp.arange(seq_len_q, dtype=dtype)[:, None]
            k_pos = jnp.arange(seq_len_k, dtype=dtype)[None, :]
            distance = k_pos - q_pos
            return slopes[:, None, None] * distance[None]
        key = jax.random.key(seed)
        ks = jax.random.split(key, 8)
        bound = math.sqrt(6.0 / (D_MODEL + D_MODEL))
        mk = lambda k: jax.random.uniform(k, (D_MODEL, D_MODEL), jnp.float32, -bound, bound)
        return {'query': jax.random.normal(ks[0], (B, SQ, D_MODEL), jnp.float32), 'key': jax.random.normal(ks[1], (B, SK, D_MODEL), jnp.float32), 'value': jax.random.normal(ks[2], (B, SK, D_MODEL), jnp.float32), 'w_q': mk(ks[3]), 'w_k': mk(ks[4]), 'w_v': mk(ks[5]), 'w_o': mk(ks[6]), 'b_o': jnp.zeros((D_MODEL,), jnp.float32)}
    _L0_xattn_all = _L0_xattn_setup()
    _L0_xattn_in = {k: v for k, v in _L0_xattn_all.items() if k in ('w_q', 'w_k', 'w_v', 'w_o', 'b_o')}
    del _L0_xattn_all

    def _L0_attn_setup():
        import jax, jax.numpy as jnp
        import numpy as np
        B_, L_, D_MODEL = (4, 512, 256)
        D_INNER, D_STATE, D_CONV, DT_RANK = (512, 64, 4, 64)

        def _rmsnorm(x, w):
            eps = jnp.finfo(x.dtype).eps
            var = jnp.mean(jnp.square(x), axis=-1, keepdims=True)
            return x * jax.lax.rsqrt(var + eps) * w

        def _selective_scan(u, delta, A, Bm, Cm, Dp):
            du = jnp.swapaxes(delta, 0, 1)
            uu = jnp.swapaxes(u, 0, 1)
            Bu = jnp.swapaxes(Bm, 0, 1)
            Cu = jnp.swapaxes(Cm, 0, 1)

            def step(h, inp):
                d_t, u_t, B_t, C_t = inp
                dA = jnp.exp(d_t[..., None] * A)
                dBu = (d_t * u_t)[..., None] * B_t[:, None, :]
                h = dA * h + dBu
                y = jnp.einsum('bdn,bn->bd', h, C_t)
                return (h, y)
            h0 = jnp.zeros((u.shape[0], u.shape[2], A.shape[1]), u.dtype)
            _, ys = jax.lax.scan(step, h0, (du, uu, Bu, Cu))
            return jnp.swapaxes(ys, 0, 1) + u * Dp
        key = jax.random.key(seed)
        ks = jax.random.split(key, 8)
        s = 0.02
        x = jax.random.normal(ks[0], (B_, L_, D_MODEL), jnp.float32)
        W_in = jax.random.normal(ks[1], (2 * D_INNER, D_MODEL), jnp.float32) * s
        conv_w = jax.random.normal(ks[2], (D_INNER, 1, D_CONV), jnp.float32) * s
        conv_b = jnp.zeros((D_INNER,), jnp.float32)
        W_x = jax.random.normal(ks[3], (DT_RANK + 2 * D_STATE, D_INNER), jnp.float32) * s
        W_dt = jax.random.normal(ks[4], (D_INNER, DT_RANK), jnp.float32) * s
        b_dt = jax.random.uniform(ks[5], (D_INNER,), jnp.float32, minval=-4.6, maxval=-2.3)
        A_log = jnp.log(jnp.tile(jnp.arange(1, D_STATE + 1, dtype=jnp.float32), (D_INNER, 1)))
        Dp = jnp.ones((D_INNER,), jnp.float32)
        W_out = jax.random.normal(ks[6], (D_MODEL, D_INNER), jnp.float32) * s
        norm_w = jnp.ones((D_MODEL,), jnp.float32)
        return dict(x=x, norm_w=norm_w, W_in=W_in, conv_w=conv_w, conv_b=conv_b, W_x=W_x, W_dt=W_dt, b_dt=b_dt, A_log=A_log, Dp=Dp, W_out=W_out)
    _L0_attn_all = _L0_attn_setup()
    _L0_attn_in = {k: v for k, v in _L0_attn_all.items() if k in ('norm_w', 'W_in', 'conv_w', 'conv_b', 'W_x', 'W_dt', 'b_dt', 'A_log', 'Dp', 'W_out')}
    del _L0_attn_all

    def _L0_ffn_setup():
        import jax, jax.numpy as jnp
        import numpy as np
        D_MODEL = 256
        NUM_HEADS = 4
        NUM_EXPERTS = 8
        TOP_K = 2
        D_FF = 256
        EPS = 1e-06

        def _rmsnorm(x, g):
            return x * jax.lax.rsqrt(jnp.mean(x * x, axis=-1, keepdims=True) + EPS) * g

        def _swiglu(x, w1, w2, w3):
            return jax.nn.silu(x @ w1.T) * (x @ w3.T) @ w2.T
        key = jax.random.key(seed)
        ks = jax.random.split(key, 16)
        d, e, f = (D_MODEL, NUM_EXPERTS, D_FF)
        dc = d // 4
        s = 0.02
        return {'X': jax.random.normal(ks[0], (2, 256, d), dtype=jnp.float32), 'g1': jnp.ones((d,), jnp.float32), 'g2': jnp.ones((d,), jnp.float32), 'Wq': jax.random.normal(ks[1], (d, d), jnp.float32) * s, 'Wkc': jax.random.normal(ks[2], (dc, d), jnp.float32) * s, 'Wvc': jax.random.normal(ks[3], (dc, d), jnp.float32) * s, 'Wo': jax.random.normal(ks[4], (d, d), jnp.float32) * s, 'Wr': jax.random.normal(ks[5], (e, d), jnp.float32) * s, 'expert_bias': jnp.zeros((e,), jnp.float32), 'sW1': jax.random.normal(ks[6], (f, d), jnp.float32) * s, 'sW2': jax.random.normal(ks[7], (d, f), jnp.float32) * s, 'sW3': jax.random.normal(ks[8], (f, d), jnp.float32) * s, 'eW1': jax.random.normal(ks[9], (e, f, d), jnp.float32) * s, 'eW2': jax.random.normal(ks[10], (e, d, f), jnp.float32) * s, 'eW3': jax.random.normal(ks[11], (e, f, d), jnp.float32) * s}
    _L0_ffn_all = _L0_ffn_setup()
    _L0_ffn_in = {k: v for k, v in _L0_ffn_all.items() if k in ('g1', 'g2', 'Wq', 'Wkc', 'Wvc', 'Wo', 'Wr', 'expert_bias', 'sW1', 'sW2', 'sW3', 'eW1', 'eW2', 'eW3')}
    del _L0_ffn_all

    def _L1_xattn_setup():
        import jax, jax.numpy as jnp
        import numpy as np
        from jax import lax
        BIG = jnp.float32(1e+30)

        def _pairwise_euclidean(a, b):
            aa = jnp.sum(a * a, axis=-1)[:, None]
            bb = jnp.sum(b * b, axis=-1)[None, :]
            ab = a @ b.T
            return jnp.sqrt(jnp.maximum(aa + bb - 2.0 * ab, 0.0))

        def _dtw_cost(D):
            row0 = jnp.cumsum(D[0])

            def row_step(prev_row, d_row):
                first = d_row[0] + prev_row[0]

                def col_step(left, inp):
                    d_ij, up, diag = inp
                    r = d_ij + jnp.minimum(jnp.minimum(up, left), diag)
                    return (r, r)
                _, rest = lax.scan(col_step, first, (d_row[1:], prev_row[1:], prev_row[:-1]))
                row = jnp.concatenate([first[None], rest])
                return (row, row)
            _, rows = lax.scan(row_step, row0, D[1:])
            return jnp.concatenate([row0[None], rows], axis=0)

        def _backtrack(R, T1, T2):
            L = T1 + T2 - 1

            def step(carry, _):
                i, j, done = carry
                valid = jnp.logical_not(done)
                cd = jnp.where((i > 0) & (j > 0), R[jnp.maximum(i - 1, 0), jnp.maximum(j - 1, 0)], BIG)
                cu = jnp.where(i > 0, R[jnp.maximum(i - 1, 0), j], BIG)
                cl = jnp.where(j > 0, R[i, jnp.maximum(j - 1, 0)], BIG)
                choice = jnp.argmin(jnp.stack([cd, cu, cl]))
                ni = jnp.where(choice <= 1, i - 1, i)
                nj = jnp.where((choice == 0) | (choice == 2), j - 1, j)
                at_origin = (i == 0) & (j == 0)
                ni = jnp.where(at_origin, 0, ni)
                nj = jnp.where(at_origin, 0, nj)
                return ((ni, nj, done | at_origin), (i, j, valid))
            init = (jnp.int32(T1 - 1), jnp.int32(T2 - 1), jnp.bool_(False))
            _, (i_idx, j_idx, valid) = lax.scan(step, init, None, length=L)
            return (i_idx, j_idx, valid)

        def _align_one(small, large):
            T_small, d = small.shape
            T_large = large.shape[0]
            D = _pairwise_euclidean(small, large)
            R = _dtw_cost(D)
            i_idx, j_idx, valid = _backtrack(R, T_small, T_large)
            contrib = small[i_idx] * valid[:, None].astype(small.dtype)
            expanded = jnp.zeros((T_large, d), dtype=small.dtype).at[j_idx].add(contrib)
            return expanded
        key = jax.random.key(seed)
        k1, k2 = jax.random.split(key)
        teacher = jax.random.normal(k1, (16, 100, 256), dtype=jnp.float32)
        student = jax.random.normal(k2, (16, 150, 256), dtype=jnp.float32)
        return {'teacher_features': teacher, 'student_features': student}
    _L1_xattn_all = _L1_xattn_setup()
    _L1_xattn_in = {k: v for k, v in _L1_xattn_all.items() if k in ()}
    del _L1_xattn_all

    def _L1_attn_setup():
        import jax, jax.numpy as jnp
        import numpy as np
        import math
        KSIZE = 4
        EPS_NORM = 1e-12
        EPS_LN = 1e-05

        def short_conv(x, w):
            b, l, c = x.shape
            K = w.shape[1]
            xp = jnp.pad(x, ((0, 0), (K - 1, 0), (0, 0)))
            y = x
            for j in range(K):
                y = y + xp[:, j:j + l, :] * w[:, j]
            return y

        def l2norm(x):
            return x * jax.lax.rsqrt(jnp.sum(x * x, axis=-1, keepdims=True) + EPS_NORM)

        def titans_forward(hidden_states, Wq, Wk, Wv, conv_q, conv_k, conv_v, W_init, ln_gamma, ln_beta, Wg, Wo, num_heads=16, chunk_size=16):
            b, l, dim = hidden_states.shape
            h = num_heads
            dk = dim // h
            cs = chunk_size
            nc = l // cs
            q = l2norm(jax.nn.silu(short_conv(hidden_states @ Wq.T, conv_q)).reshape(b, l, h, dk))
            k = l2norm(jax.nn.silu(short_conv(hidden_states @ Wk.T, conv_k)).reshape(b, l, h, dk))
            v = jax.nn.silu(short_conv(hidden_states @ Wv.T, conv_v)).reshape(b, l, h, dk)
            qc = q.reshape(b, nc, cs, h, dk).transpose(1, 0, 2, 3, 4)
            kc = k.reshape(b, nc, cs, h, dk).transpose(1, 0, 2, 3, 4)
            vc = v.reshape(b, nc, cs, h, dk).transpose(1, 0, 2, 3, 4)
            mask = jnp.tril(jnp.ones((cs, cs), q.dtype))
            W0 = jnp.broadcast_to(W_init, (b, h, dk, dk))

            def step(W, chunk):
                q_c, k_c, v_c = chunk
                inter = jnp.einsum('bqhk,bhkv->bqhv', q_c, W)
                qk = jnp.einsum('bqhd,bkhd->bhqk', q_c, k_c) * mask
                intra = jnp.einsum('bhqk,bkhv->bqhv', qk, v_c)
                W_new = W + jnp.einsum('bchk,bchv->bhkv', k_c, v_c)
                return (W_new, inter + intra)
            _, o = jax.lax.scan(step, W0, (qc, kc, vc))
            o = o.transpose(1, 0, 2, 3, 4).reshape(b, l, h, dk)
            mu = jnp.mean(o, axis=-1, keepdims=True)
            var = jnp.mean((o - mu) ** 2, axis=-1, keepdims=True)
            o = (o - mu) * jax.lax.rsqrt(var + EPS_LN) * ln_gamma + ln_beta
            o = o.reshape(b, l, dim)
            gate = hidden_states @ Wg.T
            return o * gate @ Wo.T
        key = jax.random.key(seed)
        ks = jax.random.split(key, 12)
        b, l, dim = (4, 512, 256)
        h = 16
        dk = dim // h
        s = 1.0 / math.sqrt(dim)
        inp = {'hidden_states': jax.random.normal(ks[0], (b, l, dim), jnp.float32), 'Wq': jax.random.normal(ks[1], (dim, dim), jnp.float32) * s, 'Wk': jax.random.normal(ks[2], (dim, dim), jnp.float32) * s, 'Wv': jax.random.normal(ks[3], (dim, dim), jnp.float32) * s, 'conv_q': jax.random.normal(ks[4], (dim, KSIZE), jnp.float32) * 0.1, 'conv_k': jax.random.normal(ks[5], (dim, KSIZE), jnp.float32) * 0.1, 'conv_v': jax.random.normal(ks[6], (dim, KSIZE), jnp.float32) * 0.1, 'W_init': jax.random.normal(ks[7], (1, h, dk, dk), jnp.float32) / math.sqrt(dk), 'ln_gamma': jnp.ones((dk,), jnp.float32), 'ln_beta': jnp.zeros((dk,), jnp.float32), 'Wg': jax.random.normal(ks[8], (dim, dim), jnp.float32) * s, 'Wo': jax.random.normal(ks[9], (dim, dim), jnp.float32) * s}
        return inp
    _L1_attn_all = _L1_attn_setup()
    _L1_attn_in = {k: v for k, v in _L1_attn_all.items() if k in ('Wq', 'Wk', 'Wv', 'conv_q', 'conv_k', 'conv_v', 'W_init', 'ln_gamma', 'ln_beta', 'Wg', 'Wo')}
    del _L1_attn_all

    def _L1_ffn_setup():
        import jax, jax.numpy as jnp
        import numpy as np
        B, T, C = (4, 512, 256)
        E, H, K = (8, 512, 2)
        key = jax.random.key(seed)
        ks = jax.random.split(key, 7)
        s_in = 1.0 / np.sqrt(C)
        s_hid = 1.0 / np.sqrt(H)
        return {'x': jax.random.normal(ks[0], (B, T, C), dtype=jnp.float32), 'gate_w': jax.random.uniform(ks[1], (C, E), jnp.float32, -s_in, s_in), 'gate_b': jnp.zeros((E,), jnp.float32), 'w1': jax.random.uniform(ks[2], (E, C, H), jnp.float32, -s_in, s_in), 'b1': jax.random.uniform(ks[3], (E, H), jnp.float32, -s_in, s_in), 'w2': jax.random.uniform(ks[4], (E, H, C), jnp.float32, -s_hid, s_hid), 'b2': jax.random.uniform(ks[5], (E, C), jnp.float32, -s_hid, s_hid)}
    _L1_ffn_all = _L1_ffn_setup()
    _L1_ffn_in = {k: v for k, v in _L1_ffn_all.items() if k in ('gate_w', 'gate_b', 'w1', 'b1', 'w2', 'b2')}
    del _L1_ffn_all
    return {'x': x, 'ctx_1024': ctx_1024, 'L0_xattn_w_q': _L0_xattn_in['w_q'], 'L0_xattn_w_k': _L0_xattn_in['w_k'], 'L0_xattn_w_v': _L0_xattn_in['w_v'], 'L0_xattn_w_o': _L0_xattn_in['w_o'], 'L0_xattn_b_o': _L0_xattn_in['b_o'], 'L0_attn_norm_w': _L0_attn_in['norm_w'], 'L0_attn_W_in': _L0_attn_in['W_in'], 'L0_attn_conv_w': _L0_attn_in['conv_w'], 'L0_attn_conv_b': _L0_attn_in['conv_b'], 'L0_attn_W_x': _L0_attn_in['W_x'], 'L0_attn_W_dt': _L0_attn_in['W_dt'], 'L0_attn_b_dt': _L0_attn_in['b_dt'], 'L0_attn_A_log': _L0_attn_in['A_log'], 'L0_attn_Dp': _L0_attn_in['Dp'], 'L0_attn_W_out': _L0_attn_in['W_out'], 'L0_ffn_g1': _L0_ffn_in['g1'], 'L0_ffn_g2': _L0_ffn_in['g2'], 'L0_ffn_Wq': _L0_ffn_in['Wq'], 'L0_ffn_Wkc': _L0_ffn_in['Wkc'], 'L0_ffn_Wvc': _L0_ffn_in['Wvc'], 'L0_ffn_Wo': _L0_ffn_in['Wo'], 'L0_ffn_Wr': _L0_ffn_in['Wr'], 'L0_ffn_expert_bias': _L0_ffn_in['expert_bias'], 'L0_ffn_sW1': _L0_ffn_in['sW1'], 'L0_ffn_sW2': _L0_ffn_in['sW2'], 'L0_ffn_sW3': _L0_ffn_in['sW3'], 'L0_ffn_eW1': _L0_ffn_in['eW1'], 'L0_ffn_eW2': _L0_ffn_in['eW2'], 'L0_ffn_eW3': _L0_ffn_in['eW3'], 'L1_attn_Wq': _L1_attn_in['Wq'], 'L1_attn_Wk': _L1_attn_in['Wk'], 'L1_attn_Wv': _L1_attn_in['Wv'], 'L1_attn_conv_q': _L1_attn_in['conv_q'], 'L1_attn_conv_k': _L1_attn_in['conv_k'], 'L1_attn_conv_v': _L1_attn_in['conv_v'], 'L1_attn_W_init': _L1_attn_in['W_init'], 'L1_attn_ln_gamma': _L1_attn_in['ln_gamma'], 'L1_attn_ln_beta': _L1_attn_in['ln_beta'], 'L1_attn_Wg': _L1_attn_in['Wg'], 'L1_attn_Wo': _L1_attn_in['Wo'], 'L1_ffn_gate_w': _L1_ffn_in['gate_w'], 'L1_ffn_gate_b': _L1_ffn_in['gate_b'], 'L1_ffn_w1': _L1_ffn_in['w1'], 'L1_ffn_b1': _L1_ffn_in['b1'], 'L1_ffn_w2': _L1_ffn_in['w2'], 'L1_ffn_b2': _L1_ffn_in['b2']}

def reference(x, ctx_1024, L0_xattn_w_q, L0_xattn_w_k, L0_xattn_w_v, L0_xattn_w_o, L0_xattn_b_o, L0_attn_norm_w, L0_attn_W_in, L0_attn_conv_w, L0_attn_conv_b, L0_attn_W_x, L0_attn_W_dt, L0_attn_b_dt, L0_attn_A_log, L0_attn_Dp, L0_attn_W_out, L0_ffn_g1, L0_ffn_g2, L0_ffn_Wq, L0_ffn_Wkc, L0_ffn_Wvc, L0_ffn_Wo, L0_ffn_Wr, L0_ffn_expert_bias, L0_ffn_sW1, L0_ffn_sW2, L0_ffn_sW3, L0_ffn_eW1, L0_ffn_eW2, L0_ffn_eW3, L1_attn_Wq, L1_attn_Wk, L1_attn_Wv, L1_attn_conv_q, L1_attn_conv_k, L1_attn_conv_v, L1_attn_W_init, L1_attn_ln_gamma, L1_attn_ln_beta, L1_attn_Wg, L1_attn_Wo, L1_ffn_gate_w, L1_ffn_gate_b, L1_ffn_w1, L1_ffn_b1, L1_ffn_w2, L1_ffn_b2):
    import jax
    import jax.numpy as jnp

    def _L0_xattn_ref(query, key, value, w_q, w_k, w_v, w_o, b_o):
        import jax, jax.numpy as jnp
        import numpy as np
        import math
        D_MODEL = 256
        NUM_HEADS = 16
        D_K = D_MODEL // NUM_HEADS
        B, SQ, SK = (2, 512, 512)

        def _alibi_bias(seq_len_q: int, seq_len_k: int, dtype) -> jnp.ndarray:
            slopes = jnp.asarray([2.0 ** (-8.0 * (i + 1) / NUM_HEADS) for i in range(NUM_HEADS)], dtype=dtype)
            q_pos = jnp.arange(seq_len_q, dtype=dtype)[:, None]
            k_pos = jnp.arange(seq_len_k, dtype=dtype)[None, :]
            distance = k_pos - q_pos
            return slopes[:, None, None] * distance[None]
        b, sq, _ = query.shape
        sk = key.shape[1]
        Q = (query @ w_q.T).reshape(b, sq, NUM_HEADS, D_K).transpose(0, 2, 1, 3)
        K = (key @ w_k.T).reshape(b, sk, NUM_HEADS, D_K).transpose(0, 2, 1, 3)
        V = (value @ w_v.T).reshape(b, sk, NUM_HEADS, D_K).transpose(0, 2, 1, 3)
        scale = math.sqrt(D_K)
        scores = jnp.einsum('bhqd,bhkd->bhqk', Q, K) / scale
        scores = scores + _alibi_bias(sq, sk, scores.dtype)[None]
        attn = jax.nn.softmax(scores, axis=-1)
        ctx = jnp.einsum('bhqk,bhkd->bqhd', attn, V).reshape(b, sq, D_MODEL)
        return ctx @ w_o.T + b_o

    def _L0_attn_ref(x, norm_w, W_in, conv_w, conv_b, W_x, W_dt, b_dt, A_log, Dp, W_out):
        import jax, jax.numpy as jnp
        import numpy as np
        B_, L_, D_MODEL = (4, 512, 256)
        D_INNER, D_STATE, D_CONV, DT_RANK = (512, 64, 4, 64)

        def _rmsnorm(x, w):
            eps = jnp.finfo(x.dtype).eps
            var = jnp.mean(jnp.square(x), axis=-1, keepdims=True)
            return x * jax.lax.rsqrt(var + eps) * w

        def _selective_scan(u, delta, A, Bm, Cm, Dp):
            du = jnp.swapaxes(delta, 0, 1)
            uu = jnp.swapaxes(u, 0, 1)
            Bu = jnp.swapaxes(Bm, 0, 1)
            Cu = jnp.swapaxes(Cm, 0, 1)

            def step(h, inp):
                d_t, u_t, B_t, C_t = inp
                dA = jnp.exp(d_t[..., None] * A)
                dBu = (d_t * u_t)[..., None] * B_t[:, None, :]
                h = dA * h + dBu
                y = jnp.einsum('bdn,bn->bd', h, C_t)
                return (h, y)
            h0 = jnp.zeros((u.shape[0], u.shape[2], A.shape[1]), u.dtype)
            _, ys = jax.lax.scan(step, h0, (du, uu, Bu, Cu))
            return jnp.swapaxes(ys, 0, 1) + u * Dp
        xn = _rmsnorm(x, norm_w)
        xz = xn @ W_in.T
        xm, z = jnp.split(xz, 2, axis=-1)
        xc = jnp.swapaxes(xm, 1, 2)
        xc = jax.lax.conv_general_dilated(xc, conv_w, window_strides=(1,), padding=[(D_CONV - 1, 0)], feature_group_count=D_INNER, dimension_numbers=('NCH', 'OIH', 'NCH'))
        xc = jax.nn.silu(xc + conv_b[None, :, None])
        u = jnp.swapaxes(xc, 1, 2)
        x_dbl = u @ W_x.T
        dt, Bm, Cm = jnp.split(x_dbl, [DT_RANK, DT_RANK + D_STATE], axis=-1)
        delta = jax.nn.softplus(dt @ W_dt.T + b_dt)
        A = -jnp.exp(A_log)
        y = _selective_scan(u, delta, A, Bm, Cm, Dp)
        y = y * jax.nn.silu(z)
        out = y @ W_out.T
        return out + x

    def _L0_ffn_ref(X, g1, g2, Wq, Wkc, Wvc, Wo, Wr, expert_bias, sW1, sW2, sW3, eW1, eW2, eW3):
        import jax, jax.numpy as jnp
        import numpy as np
        D_MODEL = 256
        NUM_HEADS = 4
        NUM_EXPERTS = 8
        TOP_K = 2
        D_FF = 256
        EPS = 1e-06

        def _rmsnorm(x, g):
            return x * jax.lax.rsqrt(jnp.mean(x * x, axis=-1, keepdims=True) + EPS) * g

        def _swiglu(x, w1, w2, w3):
            return jax.nn.silu(x @ w1.T) * (x @ w3.T) @ w2.T
        B, S, d = X.shape
        H = NUM_HEADS
        dk = d // H
        scale = 1.0 / jnp.sqrt(jnp.float32(dk))
        nx = _rmsnorm(X, g1)
        Q = (nx @ Wq.T).reshape(B, S, H, dk).transpose(0, 2, 1, 3)
        Kc = nx @ Wkc.T
        Vc = nx @ Wvc.T
        scores = jnp.einsum('bhsd,btd->bhst', Q, Kc) * scale
        attn = jax.nn.softmax(scores, axis=-1)
        out = jnp.einsum('bhst,btd->bhsd', attn, Vc)
        out = out.transpose(0, 2, 1, 3).reshape(B, S, d) @ Wo.T
        X = X + out
        nx = _rmsnorm(X, g2)
        xf = nx.reshape(-1, d)
        logits = xf @ Wr.T + expert_bias
        rw = jax.nn.softmax(logits, axis=-1)
        topw, topi = jax.lax.top_k(rw, TOP_K)
        topw = jax.nn.softmax(topw, axis=-1)
        combine = jnp.sum(jax.nn.one_hot(topi, NUM_EXPERTS, dtype=xf.dtype) * topw[..., None], axis=1)
        shared = _swiglu(xf, sW1, sW2, sW3)
        h = jax.nn.silu(jnp.einsum('td,efd->etf', xf, eW1)) * jnp.einsum('td,efd->etf', xf, eW3)
        eo = jnp.einsum('etf,edf->etd', h, eW2)
        specialist = jnp.einsum('te,etd->td', combine, eo)
        moe_out = (shared + specialist).reshape(B, S, d)
        return X + moe_out

    def _L1_xattn_ref(teacher_features, student_features):
        import jax, jax.numpy as jnp
        import numpy as np
        from jax import lax
        BIG = jnp.float32(1e+30)

        def _pairwise_euclidean(a, b):
            aa = jnp.sum(a * a, axis=-1)[:, None]
            bb = jnp.sum(b * b, axis=-1)[None, :]
            ab = a @ b.T
            return jnp.sqrt(jnp.maximum(aa + bb - 2.0 * ab, 0.0))

        def _dtw_cost(D):
            row0 = jnp.cumsum(D[0])

            def row_step(prev_row, d_row):
                first = d_row[0] + prev_row[0]

                def col_step(left, inp):
                    d_ij, up, diag = inp
                    r = d_ij + jnp.minimum(jnp.minimum(up, left), diag)
                    return (r, r)
                _, rest = lax.scan(col_step, first, (d_row[1:], prev_row[1:], prev_row[:-1]))
                row = jnp.concatenate([first[None], rest])
                return (row, row)
            _, rows = lax.scan(row_step, row0, D[1:])
            return jnp.concatenate([row0[None], rows], axis=0)

        def _backtrack(R, T1, T2):
            L = T1 + T2 - 1

            def step(carry, _):
                i, j, done = carry
                valid = jnp.logical_not(done)
                cd = jnp.where((i > 0) & (j > 0), R[jnp.maximum(i - 1, 0), jnp.maximum(j - 1, 0)], BIG)
                cu = jnp.where(i > 0, R[jnp.maximum(i - 1, 0), j], BIG)
                cl = jnp.where(j > 0, R[i, jnp.maximum(j - 1, 0)], BIG)
                choice = jnp.argmin(jnp.stack([cd, cu, cl]))
                ni = jnp.where(choice <= 1, i - 1, i)
                nj = jnp.where((choice == 0) | (choice == 2), j - 1, j)
                at_origin = (i == 0) & (j == 0)
                ni = jnp.where(at_origin, 0, ni)
                nj = jnp.where(at_origin, 0, nj)
                return ((ni, nj, done | at_origin), (i, j, valid))
            init = (jnp.int32(T1 - 1), jnp.int32(T2 - 1), jnp.bool_(False))
            _, (i_idx, j_idx, valid) = lax.scan(step, init, None, length=L)
            return (i_idx, j_idx, valid)

        def _align_one(small, large):
            T_small, d = small.shape
            T_large = large.shape[0]
            D = _pairwise_euclidean(small, large)
            R = _dtw_cost(D)
            i_idx, j_idx, valid = _backtrack(R, T_small, T_large)
            contrib = small[i_idx] * valid[:, None].astype(small.dtype)
            expanded = jnp.zeros((T_large, d), dtype=small.dtype).at[j_idx].add(contrib)
            return expanded
        return jax.vmap(_align_one)(teacher_features, student_features)

    def _L1_attn_ref(hidden_states, Wq, Wk, Wv, conv_q, conv_k, conv_v, W_init, ln_gamma, ln_beta, Wg, Wo):
        import jax, jax.numpy as jnp
        import numpy as np
        import math
        KSIZE = 4
        EPS_NORM = 1e-12
        EPS_LN = 1e-05

        def short_conv(x, w):
            b, l, c = x.shape
            K = w.shape[1]
            xp = jnp.pad(x, ((0, 0), (K - 1, 0), (0, 0)))
            y = x
            for j in range(K):
                y = y + xp[:, j:j + l, :] * w[:, j]
            return y

        def l2norm(x):
            return x * jax.lax.rsqrt(jnp.sum(x * x, axis=-1, keepdims=True) + EPS_NORM)

        def titans_forward(hidden_states, Wq, Wk, Wv, conv_q, conv_k, conv_v, W_init, ln_gamma, ln_beta, Wg, Wo, num_heads=16, chunk_size=16):
            b, l, dim = hidden_states.shape
            h = num_heads
            dk = dim // h
            cs = chunk_size
            nc = l // cs
            q = l2norm(jax.nn.silu(short_conv(hidden_states @ Wq.T, conv_q)).reshape(b, l, h, dk))
            k = l2norm(jax.nn.silu(short_conv(hidden_states @ Wk.T, conv_k)).reshape(b, l, h, dk))
            v = jax.nn.silu(short_conv(hidden_states @ Wv.T, conv_v)).reshape(b, l, h, dk)
            qc = q.reshape(b, nc, cs, h, dk).transpose(1, 0, 2, 3, 4)
            kc = k.reshape(b, nc, cs, h, dk).transpose(1, 0, 2, 3, 4)
            vc = v.reshape(b, nc, cs, h, dk).transpose(1, 0, 2, 3, 4)
            mask = jnp.tril(jnp.ones((cs, cs), q.dtype))
            W0 = jnp.broadcast_to(W_init, (b, h, dk, dk))

            def step(W, chunk):
                q_c, k_c, v_c = chunk
                inter = jnp.einsum('bqhk,bhkv->bqhv', q_c, W)
                qk = jnp.einsum('bqhd,bkhd->bhqk', q_c, k_c) * mask
                intra = jnp.einsum('bhqk,bkhv->bqhv', qk, v_c)
                W_new = W + jnp.einsum('bchk,bchv->bhkv', k_c, v_c)
                return (W_new, inter + intra)
            _, o = jax.lax.scan(step, W0, (qc, kc, vc))
            o = o.transpose(1, 0, 2, 3, 4).reshape(b, l, h, dk)
            mu = jnp.mean(o, axis=-1, keepdims=True)
            var = jnp.mean((o - mu) ** 2, axis=-1, keepdims=True)
            o = (o - mu) * jax.lax.rsqrt(var + EPS_LN) * ln_gamma + ln_beta
            o = o.reshape(b, l, dim)
            gate = hidden_states @ Wg.T
            return o * gate @ Wo.T
        return titans_forward(hidden_states, Wq, Wk, Wv, conv_q, conv_k, conv_v, W_init, ln_gamma, ln_beta, Wg, Wo)

    def _L1_ffn_ref(x, gate_w, gate_b, w1, b1, w2, b2):
        import jax, jax.numpy as jnp
        import numpy as np
        B, T, C = (4, 512, 256)
        E, H, K = (8, 512, 2)
        b, t, c = x.shape
        xf = x.reshape(b * t, c)
        logits = xf @ gate_w + gate_b
        probs = jax.nn.softmax(logits, axis=-1)
        gates, expert_idx = jax.lax.top_k(probs, K)
        h = jax.nn.relu(jnp.einsum('nc,ech->neh', xf, w1) + b1)
        expert_out = jnp.einsum('neh,ehc->nec', h, w2) + b2
        onehot = jax.nn.one_hot(expert_idx, E, dtype=xf.dtype)
        weights = jnp.einsum('nk,nke->ne', gates, onehot)
        out = jnp.einsum('ne,nec->nc', weights, expert_out)
        return out.reshape(b, t, c)
    x = x + _L0_xattn_ref(_layernorm(x, axis=-1), ctx_1024, ctx_1024, L0_xattn_w_q, L0_xattn_w_k, L0_xattn_w_v, L0_xattn_w_o, L0_xattn_b_o)
    x = x + _L0_attn_ref(_layernorm(x, axis=-1), L0_attn_norm_w, L0_attn_W_in, L0_attn_conv_w, L0_attn_conv_b, L0_attn_W_x, L0_attn_W_dt, L0_attn_b_dt, L0_attn_A_log, L0_attn_Dp, L0_attn_W_out)
    x = x + _L0_ffn_ref(_layernorm(x, axis=-1), L0_ffn_g1, L0_ffn_g2, L0_ffn_Wq, L0_ffn_Wkc, L0_ffn_Wvc, L0_ffn_Wo, L0_ffn_Wr, L0_ffn_expert_bias, L0_ffn_sW1, L0_ffn_sW2, L0_ffn_sW3, L0_ffn_eW1, L0_ffn_eW2, L0_ffn_eW3)
    x = x + _L1_xattn_ref(ctx_1024, _layernorm(x, axis=-1))
    x = x + _L1_attn_ref(_layernorm(x, axis=-1), L1_attn_Wq, L1_attn_Wk, L1_attn_Wv, L1_attn_conv_q, L1_attn_conv_k, L1_attn_conv_v, L1_attn_W_init, L1_attn_ln_gamma, L1_attn_ln_beta, L1_attn_Wg, L1_attn_Wo)
    x = x + _L1_ffn_ref(_layernorm(x, axis=-1), L1_ffn_gate_w, L1_ffn_gate_b, L1_ffn_w1, L1_ffn_b1, L1_ffn_w2, L1_ffn_b2)
    return x

_drawn_inputs = setup_inputs


def setup_inputs(seed=0):
    import zlib

    import numpy as np

    out = dict(_drawn_inputs(seed))
    spreads = {'L0_xattn_b_o': (0.0, 0.364),
     'L0_attn_norm_w': (1.0, 0.6),
     'L0_attn_conv_b': (0.0, 0.8),
     'L0_attn_Dp': (1.0, 0.6),
     'L0_ffn_g1': (1.0, 0.6),
     'L0_ffn_g2': (1.0, 0.6),
     'L0_ffn_expert_bias': (0.0, 0.8),
     'L1_attn_ln_gamma': (1.0, 0.6),
     'L1_attn_ln_beta': (0.0, 2.0),
     'L1_ffn_gate_b': (0.0, 0.8)}
    factors = {'L0_attn_W_in': 8.0,
     'L0_attn_conv_w': 8.0,
     'L0_attn_W_x': 8.0,
     'L0_attn_W_dt': 8.0,
     'L0_attn_b_dt': 8.0,
     'L0_attn_A_log': 8.0,
     'L0_attn_W_out': 8.0,
     'L0_ffn_Wq': 8.0,
     'L0_ffn_Wkc': 8.0,
     'L0_ffn_Wvc': 8.0,
     'L0_ffn_Wo': 8.0,
     'L0_ffn_Wr': 6.188,
     'L0_ffn_eW1': 6.503,
     'L0_ffn_eW2': 8.0,
     'L0_ffn_eW3': 8.0,
     'L1_attn_conv_q': 4.813,
     'L1_attn_conv_k': 6.105,
     'L1_attn_conv_v': 5.263,
     'L1_ffn_gate_w': 8.0,
     'L1_ffn_w1': 8.0,
     'L1_ffn_b1': 8.0,
     'L1_ffn_w2': 8.0,
     'L1_ffn_b2': 64.0,
     'L0_ffn_sW2': 2.739}
    for name, (base, spread) in spreads.items():
        noise = np.random.default_rng([zlib.crc32(name.encode()), seed]).standard_normal(out[name].shape)
        drawn = base * np.exp(spread * noise) if base else spread * noise
        out[name] = jnp.asarray(drawn.astype(out[name].dtype))
    for name, factor in factors.items():
        out[name] = (out[name] * factor).astype(out[name].dtype)
    return out
```

```python
from contextlib import ExitStack

import concourse.bass as bass
import numpy as np
from concourse import mybir

ALU = mybir.AluOpType
ACT = mybir.ActivationFunctionType
AX = mybir.AxisListType
F32 = mybir.dt.float32
BF16 = mybir.dt.bfloat16
U32 = mybir.dt.uint32

P = 128
B = 32
L = 32
T = B * L
D = 256
DC = D // P
HALF = 512
NH = T // HALF
TT = T // P
SK = 257
XH = 16
DK = D // XH
HPC = P // DK
DI = 512
IC = DI // P
NS = 64
KW = 4
E = 8
FH = 512
BIG = 1e30


NORMS = [(0, "xn", 2), (1, "mn", 2), (1, "mr", 0), (2, "fn", 2), (2, "fr", 0), (2, "f2", 0), (3, "dn", 2),
         (4, "tn", 2), (5, "gn", 2)]
DENSE = [(0, "xq", 4, 0, 4), (0, "xw", 4, 0, 0), (1, "mi", 16, 8, 8), (1, "mx", 4, 4, 0), (1, "md", 8, 0, 8),
         (1, "mo", 4, 0, 0), (2, "fq", 6, 0, 6), (2, "fw", 4, 0, 0), (4, "tp", 16, 16, 0), (4, "to", 4, 0, 0)]


class Sems:

    def __init__(self, nc, ctx, first):
        self.nc, self.ctx, self.made, self.base = nc, ctx, {}, {}
        count = {}

        def add(n, kind, events):
            total = count.get(kind, 0)
            self.base[f"{n}_{kind.split('_', 1)[1]}"] = (kind, total)
            count[kind] = total + events
        for stage, n, means in NORMS:
            if stage >= first:
                for kind, events in (("in", 1), ("mean", means), ("xc", means), ("sq", NH), ("var", NH), ("sd", NH),
                                     ("out", NH if means else NH * DC)):
                    add(n, "norm_" + kind, events)
        for stage, n, groups, a, d in DENSE:
            if stage >= first:
                for kind, events in (("mm", groups), ("ev_a", a), ("ev_d", d)):
                    add(n, "dense_" + kind, events)

    def __getitem__(self, name):
        name = self.base.get(name, (name, 0))[0]
        if name not in self.made:
            self.made[name] = self.ctx.enter_context(self.nc.semaphore(name))
        return self.made[name]

    def at(self, name, n):
        return self[name], self.base.get(name, (name, 0))[1] + n


class Chain:

    def __init__(self, eng, sem):
        self.eng, self.sem, self.n = eng, sem, 0

    def link(self, ins):
        self.n += 1
        ins.then_inc(self.sem, 1)
        self.eng.wait_ge(self.sem, self.n)

    def step(self, ins):
        self.n += 1
        ins.then_inc(self.sem, 1)

    def sync(self):
        self.eng.wait_ge(self.sem, self.n)


def build(nc, A, out, first=0, last=5):
    ctx = ExitStack()
    with ctx:
        S = Sems(nc, ctx, first)
        ar = ctx.enter_context(nc.sbuf_tensor("arena", [P, 46 * 1024], F32))
        ps = ctx.enter_context(nc.psum_tensor("ps", [P, 8, HALF], F32))

        dist = nc.dram_tensor("dist", (TT, P, SK), F32, kind="Internal").ap()

        def view(off, *shape):
            n = int(np.prod(shape))
            v = ar[:, off:off + n]
            if len(shape) == 1:
                return v
            names = "abcd"[:len(shape)]
            return v.rearrange(f"p ({' '.join(names)}) -> p {' '.join(names)}", **dict(zip(names, shape)))

        def bview(off, *shape):
            n = int(np.prod(shape))
            v = ar[:, off:off + (n + 1) // 2].bitcast(BF16)
            if len(shape) == 1:
                return v
            names = "abcd"[:len(shape)]
            return v.rearrange(f"p ({' '.join(names)}) -> p {' '.join(names)}", **dict(zip(names, shape)))

        K = 1024
        xT = view(0, DC, T)
        CONST = 44 * K
        ident = view(CONST, P)
        mean_w = view(CONST + 128, P)
        hmask = view(CONST + 256, HPC)
        ones = view(CONST + 264, 32)
        grp = view(CONST + 296, P)
        eps = view(CONST + 424, 4)
        identb = bview(CONST + 428, P)
        iota8 = view(CONST + 492, E)
        U = [view(2 * K * n, DC, T) for n in range(23)]

        dma_n = {}

        def signal(name):
            nc.vector.memset(view(CONST + 500, 1), 0.0).then_inc(S[name], 1)

        def load(sp, name, *pairs):
            for dst, src in pairs:
                sp.dma_start(dst, src).then_inc(S[name], 16)
            dma_n[name] = 16 * len(pairs)

        def half(v, c, h):
            return v[:, c, h * HALF:(h + 1) * HALF]

        def dense_pe(pe, name, groups, owners, banks):
            nb = len(banks)
            for g, (rows, pairs) in enumerate(groups):
                if g >= nb:
                    o = owners[g - nb]
                    pe.wait_ge(*S.at(f"{name}_ev_{o}", owners[:g - nb + 1].count(o)))
                for k, (lhsT, rhs) in enumerate(pairs):
                    dst = ps[0:rows, banks[g % nb], 0:rhs.shape[-1]]
                    last_mm = nc.tensor.matmul(dst, lhsT, rhs, start=(k == 0), stop=(k == len(pairs) - 1))
                last_mm.then_inc(S[f"{name}_mm"], 1)

        def norm_pe(pe, name, src, sq, rms=False):
            if not rms:
                pe.wait_ge(*S.at(f"{name}_in", 1))
                for h in range(NH):
                    for c in range(DC):
                        mm = nc.tensor.matmul(ps[:, h, :], mean_w, half(src, c, h), start=(c == 0), stop=(c == 1))
                    mm.then_inc(S[f"{name}_mean"], 1)
            for h in range(NH):
                pe.wait_ge(*S.at(f"{name}_sq", h + 1))
                for c in range(DC):
                    mm = nc.tensor.matmul(ps[:, 2 + h, :], mean_w, half(sq, c, h), start=(c == 0), stop=(c == 1))
                mm.then_inc(S[f"{name}_var"], 1)

        def norm_act(act, name, src, sq, sd, eps_n, rms=False):
            for h in range(NH):
                if rms:
                    act.wait_ge(*S.at(f"{name}_in", 1))
                else:
                    act.wait_ge(*S.at(f"{name}_xc", h + 1))
                nc.scalar.activation(sq[:, :, h * HALF:(h + 1) * HALF], src[:, :, h * HALF:(h + 1) * HALF],
                                     ACT.Square).then_inc(S[f"{name}_sq"], 1)
            for h in range(NH):
                act.wait_ge(*S.at(f"{name}_var", h + 1))
                nc.scalar.activation(sd[:, h * HALF:(h + 1) * HALF], ps[:, 2 + h, :], ACT.Sqrt,
                                     bias=eps[:, eps_n:eps_n + 1]).then_inc(S[f"{name}_sd"], 1)

        def norm_dve(ch, name, src, xc, sd, dst, rms=False, gain=None):
            dve = ch.eng
            if not rms:
                for h in range(NH):
                    dve.wait_ge(*S.at(f"{name}_mean", h + 1))
                    sl = slice(h * HALF, (h + 1) * HALF)
                    nc.vector.tensor_tensor(xc[:, :, sl], src[:, :, sl],
                                            ps[:, h:h + 1, :].broadcast_to([P, DC, HALF]),
                                            ALU.subtract).then_inc(S[f"{name}_xc"], 1)
                dve.wait_ge(*S.at(f"{name}_xc", NH))
            for h in range(NH):
                dve.wait_ge(*S.at(f"{name}_sd", h + 1))
                sl = slice(h * HALF, (h + 1) * HALF)
                ch.link(nc.vector.reciprocal(sd[:, sl], sd[:, sl]))
                if gain is None:
                    nc.vector.tensor_tensor(dst[:, :, sl], xc[:, :, sl],
                                            sd[:, sl].unsqueeze(1).broadcast_to([P, DC, HALF]),
                                            ALU.mult).then_inc(S[f"{name}_out"], 1)
                else:
                    for c in range(DC):
                        nc.vector.scalar_tensor_tensor(out=dst[:, c, sl], in0=xc[:, c, sl],
                                                       scalar=gain[:, c:c + 1], in1=sd[:, sl],
                                                       op0=ALU.mult, op1=ALU.mult).then_inc(S[f"{name}_out"], 1)
            dve.wait_ge(*S.at(f"{name}_out", NH if gain is None else NH * DC))

        x0 = dict(
            wq=view(20 * K, DC, D), wk=view(20 * K + 512, DC, D), wv=view(21 * K, DC, D), wo=view(21 * K + 512, DC, D),
            bo=view(22 * K, DC),
            slope=bview(22 * K + 16, 4, P), pos=bview(22 * K + 16 + 256, SK + 1),
            slope32=view(36 * K, 4, P), pos32=view(36 * K + 512, SK),
            dmask=view(22 * K + 512, HALF),
            ctx=[view(23 * K + 520 * j, DC, SK) for j in range(2)],
            kT=[view(25 * K + 520 * j, DC, SK) for j in range(2)],
            v=[view(27 * K + 512 * j, 2, D) for j in range(2)],
            v2=[view(28 * K + 256 * j, D) for j in range(2)],
            qb=[view(28 * K + 512 + 512 * j, HALF) for j in range(2)],
            p=[view(30 * K + 1040 * j, 4, SK) for j in range(2)],
            pT=view(33 * K, 2, HALF), pT2=view(34 * K, HALF),
            om=view(34 * K + 512, HALF),
            st=[view(35 * K + 16 * j, 3, 4) for j in range(2)],
        )
        Xn, Xq, Xo = U[1], U[2], U[3]

        def x_load(sp):
            load(sp, "ld_const", (ident, A["c_ident"]), (mean_w, A["c_mean"]), (hmask, A["c_hmask"]),
                 (ones, A["c_ones"]), (grp, A["c_grp"]), (eps, A["c_eps"]),
                 (iota8, A["c_iota8"]), (xT, A["x"]))

        def x_loads(sp):
            load(sp, "ld_x", (x0["wq"], A["L0_xattn_w_q"]), (x0["wk"], A["L0_xattn_w_k"]),
                 (x0["wv"], A["L0_xattn_w_v"]), (x0["wo"], A["L0_xattn_w_o"]), (x0["bo"], A["L0_xattn_b_o"]),
                 (x0["slope32"][0:6], A["c_slope"]), (x0["pos32"][0:6], A["c_pos"]), (x0["dmask"], A["c_dmask"]))

            def ctx_load(b, j):
                sp.dma_start(x0["ctx"][j], A["ctxT"][:, :, bass.ds(b * SK, SK)]).then_inc(S[f"x_ctx{j}"], 16)
            for j in range(2):
                ctx_load(j, j)
            with sp.Fori(1, B // 2) as i:
                for j in range(2):
                    sp.wait_ge(S["x_v"], 2 * i + j - 1)
                    ctx_load(2 * i + j, j)

        def x_pe(pe):
            pe.wait_ge(S["ld_const"], dma_n["ld_const"])
            norm_pe(pe, "xn", xT, Xo)
            pe.wait_ge(S["ld_x"], dma_n["ld_x"])
            pe.wait_ge(*S.at("xn_out", 2))
            dense_pe(pe, "xq", [(P, [(x0["wq"][:, k, m * P:(m + 1) * P], half(Xn, k, h)) for k in range(DC)])
                                for m in range(DC) for h in range(NH)], "dddd", [4, 5, 6, 7])
            pe.wait_ge(*S.at("xq_ev_d", 4))

            def proj(b, j, i):
                if not isinstance(b, int) or b >= 2:
                    pe.wait_ge(S["x_or"], b)
                if not isinstance(b, int) or b >= 1:
                    pe.wait_ge(S["x_vev"], 2 * b)
                    pe.wait_ge(S["x_kev"], b)
                cx = x0["ctx"][j]
                pe.wait_ge(S[f"x_ctx{j}"], 16 * (i + 1))
                for m in range(DC):
                    for k in range(DC):
                        mm = nc.tensor.matmul(ps[:, 4 + m, 0:SK], x0["wk"][:, k, m * P:(m + 1) * P], cx[:, k, :],
                                              start=(k == 0), stop=(k == 1))
                mm.then_inc(S["x_k"], 1)
                for t in range(3):
                    rows = min(P, SK - t * P)
                    dst = ps[0:rows, 6, t * D:(t + 1) * D] if t < 2 else ps[0:rows, 7, 0:D]
                    for k in range(DC):
                        mm = nc.tensor.matmul(dst, cx[:, k, t * P:t * P + rows], x0["wv"][:, k, :],
                                              start=(k == 0), stop=(k == 1))
                mm.then_inc(S["x_v"], 1)

            def scores(b, j):
                pe.wait_ge(S["x_kev"], b + 1)
                pe.wait_ge(S["x_qblk"], 2 * b + 2)
                if not isinstance(b, int) or b >= 1:
                    pe.wait_ge(S["x_exp"], 4 * b)
                for g in range(4):
                    nc.tensor.matmul(ps[:, g, 0:SK], x0["qb"][j][:, g * P:(g + 1) * P], x0["kT"][j][:, g // 2, :],
                                     start=True, stop=False)
                    mm = nc.tensor.matmul(ps[:, g, 0:SK], x0["slope"][0:6, g, :], x0["pos"][0:6, 0:SK],
                                          start=False, stop=True)
                mm.then_inc(S["x_s"], 1)

            def tail(b, j, vev):
                pe.wait_ge(S["x_norm"], b + 1)
                pe.wait_ge(S["x_vev"], vev)
                for t in range(3):
                    rows = min(P, SK - t * P)
                    for g in range(4):
                        mm = nc.tensor.transpose(ps[0:rows, 4 + t, g * P:(g + 1) * P],
                                                 x0["p"][j][:, g, t * P:t * P + rows], ident)
                mm.then_inc(S["x_pt"], 1)
                pe.wait_ge(S["x_ptev"], b + 1)
                pe.wait_ge(S["x_pt2ev"], b + 1)
                for c in range(DC):
                    sl = slice(c * 256, (c + 1) * 256)
                    for t in range(2):
                        nc.tensor.matmul(ps[:, 7, sl], x0["v"][j][:, t, c * P:(c + 1) * P], x0["pT"][:, t, sl],
                                         start=(t == 0), stop=False)
                    mm = nc.tensor.matmul(ps[:, 7, sl], x0["v2"][j][0:1, c * P:(c + 1) * P], x0["pT2"][0:1, sl],
                                          start=False, stop=True)
                mm.then_inc(S["x_o"], 1)

            proj(0, 0, 0)
            pe.wait_ge(S["x_alibi"], 2)
            scores(0, 0)
            with pe.Fori(0, B // 2 - 1) as i:
                b = 2 * i
                proj(b + 1, 1, i)
                scores(b + 1, 1)
                tail(b, 0, 2 * b + 4)
                proj(b + 2, 0, i + 1)
                scores(b + 2, 0)
                tail(b + 1, 1, 2 * b + 6)
            proj(B - 1, 1, B // 2 - 1)
            scores(B - 1, 1)
            tail(B - 2, 0, 2 * B)
            tail(B - 1, 1, 2 * B)
            pe.wait_ge(S["x_or"], B + 1)
            dense_pe(pe, "xw", [(P, [(x0["wo"][:, k, m * P:(m + 1) * P], half(Xo, k, h)) for k in range(DC)])
                                for m in range(DC) for h in range(NH)], "dddd", [0, 1, 2, 3])

        def x_act(act):
            act.wait_ge(S["ld_const"], dma_n["ld_const"])
            norm_act(act, "xn", Xn, Xo, U[4][:, 0, :], 0)

            def keys(b, j):
                act.wait_ge(S["x_k"], b + 1)
                nc.scalar.copy(x0["kT"][j], ps[:, 4:6, 0:SK]).then_inc(S["x_kev"], 1)

            def exps(b, j):
                act.wait_ge(S["x_max"], b + 1)
                for g in range(4):
                    nc.scalar.activation(x0["p"][j][:, g, :], ps[:, g, 0:SK], ACT.Exp,
                                         bias=x0["st"][j][:, 0, g:g + 1],
                                         accum_out=x0["st"][j][:, 1, g:g + 1]).then_inc(S["x_exp"], 1)

            def turned(b):
                act.wait_ge(S["x_pt"], b + 1)
                act.wait_ge(S["x_or"], b + 1)
                nc.scalar.copy(x0["pT"], ps[:, 4:6, :]).then_inc(S["x_ptev"], 1)

            keys(0, 0)
            exps(0, 0)
            with act.Fori(0, B // 2 - 1) as i:
                b = 2 * i
                keys(b + 1, 1)
                turned(b)
                exps(b + 1, 1)
                keys(b + 2, 0)
                turned(b + 1)
                exps(b + 2, 0)
            keys(B - 1, 1)
            turned(B - 2)
            exps(B - 1, 1)
            turned(B - 1)

        def x_dve(ch):
            dve = ch.eng
            dve.wait_ge(S["ld_const"], dma_n["ld_const"])
            norm_dve(ch, "xn", xT, Xn, U[4][:, 0, :], Xn)
            for g in range(4):
                m, h = g // 2, g % 2
                dve.wait_ge(*S.at("xq_mm", g + 1))
                nc.vector.tensor_scalar(half(Xq, m, h), ps[:, 4 + g, :], 1.0 / DK ** 0.5, None,
                                        ALU.mult).then_inc(S["xq_ev_d"], 1)
            dve.wait_ge(S["ld_x"], dma_n["ld_x"])
            nc.vector.tensor_copy(x0["slope"][0:6], x0["slope32"][0:6]).then_inc(S["x_alibi"], 1)
            nc.vector.tensor_copy(x0["pos"][0:6, 0:SK], x0["pos32"][0:6]).then_inc(S["x_alibi"], 1)

            def values(b, j):
                dve.wait_ge(S["x_v"], b + 1)
                nc.vector.tensor_copy(x0["v"][j].rearrange("p a b -> p (a b)"), ps[:, 6, :]).then_inc(S["x_vev"], 1)
                nc.vector.tensor_copy(x0["v2"][j][0:1, :], ps[0:1, 7, 0:D]).then_inc(S["x_vev"], 1)

            def maxima(b, j):
                dve.wait_ge(S["x_s"], b + 1)
                nc.vector.tensor_reduce(x0["st"][j][:, 2, :], ps[:, 0:4, 0:SK], AX.X, ALU.max).then_inc(S["x_mx0"], 1)
                dve.wait_ge(S["x_mx0"], b + 1)
                nc.vector.tensor_scalar(x0["st"][j][:, 0, :], x0["st"][j][:, 2, :], -1.0, None,
                                        ALU.mult).then_inc(S["x_max"], 1)

            def sums(b, j):
                dve.wait_ge(S["x_exp"], 4 * b + 4)
                nc.vector.reciprocal(x0["st"][j][:, 2, :], x0["st"][j][:, 1, :]).then_inc(S["x_rec"], 1)

            def outs(b):
                dve.wait_ge(S["x_pt"], b + 1)
                nc.vector.tensor_copy(x0["pT2"][0:1, :], ps[0:1, 6, :]).then_inc(S["x_pt2ev"], 1)
                dve.wait_ge(S["x_o"], b + 1)
                nc.vector.tensor_tensor(x0["om"], ps[:, 7, :], x0["dmask"], ALU.mult).then_inc(S["x_om"], 1)
                dve.wait_ge(S["x_om"], b + 1)
                nc.vector.tensor_reduce(Xo[:, :, bass.ds(b * L, L)],
                                        x0["om"].rearrange("p (c h q) -> p c q h", c=DC, h=HPC),
                                        AX.X, ALU.add).then_inc(S["x_or"], 1)

            signal("x_or")
            values(0, 0)
            maxima(0, 0)
            sums(0, 0)
            with dve.Fori(0, B // 2 - 1) as i:
                b = 2 * i
                values(b + 1, 1)
                maxima(b + 1, 1)
                outs(b)
                sums(b + 1, 1)
                values(b + 2, 0)
                maxima(b + 2, 0)
                outs(b + 1)
                sums(b + 2, 0)
            values(B - 1, 1)
            maxima(B - 1, 1)
            outs(B - 2)
            sums(B - 1, 1)
            outs(B - 1)
            for g in range(4):
                m, h = g // 2, g % 2
                dve.wait_ge(*S.at("xw_mm", g + 1))
                ch.link(nc.vector.scalar_tensor_tensor(out=half(xT, m, h), in0=ps[:, g, :], scalar=x0["bo"][:, m:m + 1],
                                                       in1=half(xT, m, h), op0=ALU.add, op1=ALU.add))

        def x_pool(pool):
            pool.wait_ge(S["ld_const"], dma_n["ld_const"])
            pool.wait_ge(*S.at("xq_ev_d", 4))

            def qblk(b, j):
                if not isinstance(b, int) or b >= 2:
                    pool.wait_ge(S["x_s"], b - 1)
                for c in range(DC):
                    nc.gpsimd.tensor_tensor(
                        x0["qb"][j][:, c * 256:(c + 1) * 256].rearrange("p (h q) -> p h q", h=HPC),
                        Xq[:, c, bass.ds(b * L, L)].unsqueeze(1).broadcast_to([P, HPC, L]),
                        hmask.unsqueeze(2).broadcast_to([P, HPC, L]), ALU.mult).then_inc(S["x_qblk"], 1)

            def normed(b, j):
                pool.wait_ge(S["x_rec"], b + 1)
                nc.gpsimd.tensor_tensor(x0["p"][j], x0["p"][j],
                                        x0["st"][j][:, 2, :].unsqueeze(2).broadcast_to([P, 4, SK]),
                                        ALU.mult).then_inc(S["x_norm"], 1)

            qblk(0, 0)
            qblk(1, 1)
            normed(0, 0)
            with pool.Fori(0, B // 2 - 1) as i:
                b = 2 * i
                qblk(b + 2, 0)
                normed(b + 1, 1)
                qblk(b + 3, 1)
                normed(b + 2, 0)
            normed(B - 1, 1)

        m_xm = view(6 * K, IC, T)
        m_z = view(10 * K, IC, T)
        m_u = view(14 * K, IC, T)
        m_bc, m_dt = view(18 * K, T), view(19 * K, T)
        m_part = bview(20 * K, 3, T)
        m_delta = view(22 * K, IC, T)
        m_du = view(26 * K, IC, T)
        m_da = view(30 * K, 4, T)
        m_h = view(34 * K, 4, T)
        m_hc = view(38 * K, 2, T)
        m_cb = view(40 * K, 2, T)
        m_win = view(42 * K, DC, 2 * DI)
        m_wx = view(38 * K, IC, 3 * 64)
        m_wdt = view(39 * K, DI)
        m_s = view(34 * K, IC, T)
        m_s2 = view(26 * K, IC, T)
        m_p = view(30 * K, IC, T)
        SM = CONST + 512
        m_wout = view(SM, IC, D)
        m_a = view(SM + 1024, IC, NS)
        m_cw = view(SM + 1280, IC, KW)
        m_cb1, m_dp, m_bdt, m_nw = (view(SM + 1296 + 4 * n, IC) for n in range(4))

        def m_load(sp):
            sp.wait_ge(*S.at("mn_in", 1))
            load(sp, "ld_m1", (m_nw[:, 0:DC], A["L0_attn_norm_w"]), (m_win, A["L0_attn_W_in"]))
            load(sp, "ld_m", (m_cw, A["L0_attn_conv_w"]),
                 (m_cb1, A["L0_attn_conv_b"]), (m_dp, A["L0_attn_Dp"]), (m_bdt, A["L0_attn_b_dt"]),
                 (m_a, A["L0_attn_A_log"]), (m_wx, A["L0_attn_W_x"]),
                 (m_wdt[0:64], A["L0_attn_W_dt"]), (m_wout, A["L0_attn_W_out"]))

        MU = 2 * NS

        def m_pe(pe):
            norm_pe(pe, "mn", xT, U[2])
            norm_pe(pe, "mr", U[1], U[2], rms=True)
            pe.wait_ge(*S.at("mr_out", 4))
            pe.wait_ge(S["ld_m1"], dma_n["ld_m1"])
            dense_pe(pe, "mi", [(P, [(m_win[:, k, m * P:(m + 1) * P], half(U[2], k, h)) for k in range(DC)])
                                for m in range(8) for h in range(NH)], "dddddddd" + "aaaaaaaa", list(range(8)))
            pe.wait_ge(S["ld_m"], dma_n["ld_m"])
            pe.wait_ge(S["mc_act"], IC)
            pe.wait_ge(*S.at("mi_ev_a", 8))
            dense_pe(pe, "mx", [(r, [(m_wx[:, k, o:o + r], half(m_u, k, h)) for k in range(IC)])
                                for o, r in ((0, 64), (64, P)) for h in range(NH)], "aaaa", [0, 1, 2, 3])
            pe.wait_ge(*S.at("mx_ev_a", 4))
            dense_pe(pe, "md", [(P, [(m_wdt[0:64, m * P:(m + 1) * P], m_dt[0:64, h * HALF:(h + 1) * HALF])])
                                for m in range(IC) for h in range(NH)], "d" * 8, list(range(8)))
            pe.wait_ge(S["m_parts"], 3)
            pe.wait_ge(*S.at("md_ev_d", 8))

            def spread(nn, n):
                if not isinstance(nn, int) or nn >= 1:
                    pe.wait_ge(S["m_dbu"], 2 * nn)
                for h in range(NH):
                    for k in range(3):
                        mm = nc.tensor.matmul(ps[:, 4 + h, :], identb[:, bass.ds(n, 1)].broadcast_to([P, P]),
                                              m_part[:, k, h * HALF:(h + 1) * HALF], start=(k == 0), stop=(k == 2))
                mm.then_inc(S["m_b"], 1)
                if not isinstance(nn, int) or nn >= 1:
                    pe.wait_ge(S["m_cc"], nn)
                for h in range(NH):
                    for k in range(3):
                        mm = nc.tensor.matmul(ps[:, 6 + h, :], identb[:, bass.ds(n + NS, 1)].broadcast_to([P, P]),
                                              m_part[:, k, h * HALF:(h + 1) * HALF], start=(k == 0), stop=(k == 2))
                mm.then_inc(S["m_c"], 1)

            def gather(w, par, first_n, last_n):
                for cc in range(2):
                    pe.wait_ge(S["m_hc"], w + cc + 1)
                    for h in range(NH):
                        mm = nc.tensor.matmul(ps[:, 2 * cc + h, :], ident, m_hc[:, cc, h * HALF:(h + 1) * HALF],
                                              start=first_n, stop=last_n, skip_group_check=True)
                    mm.then_inc(S["m_acc"], 1)

            for q in range(2):
                o = NS * q
                if q:
                    pe.wait_ge(S["my_ev"], 4)
                spread(o, 0)
                spread(o + 1, 1)
                gather(2 * o, 0, True, False)
                with pe.Fori(1, NS - 1) as n:
                    spread(o + 1 + n, n + 1)
                    gather(2 * o + 2 * n, 0, False, False)
                gather(2 * o + 2 * (NS - 1), 1, False, True)
            pe.wait_ge(S["m_gate"], IC)
            pe.wait_ge(S["my_ev"], 8)
            dense_pe(pe, "mo", [(P, [(m_wout[:, k, m * P:(m + 1) * P], half(m_xm, k, h)) for k in range(IC)])
                                for m in range(DC) for h in range(NH)], "dddd", [0, 1, 2, 3])

        def m_act(act):
            norm_act(act, "mn", U[1], U[2], U[3][:, 0, :], 0)
            act.wait_ge(*S.at("mn_out", 2))
            norm_act(act, "mr", U[1], U[2], U[3][:, 1, :], 1, rms=True)
            for g in range(8, 16):
                m, h = g // 2 - 4, g % 2
                act.wait_ge(*S.at("mi_mm", g + 1))
                nc.scalar.activation(half(m_z, m, h), ps[:, g % 8, :], ACT.Silu).then_inc(S["mi_ev_a"], 1)
            for c in range(IC):
                act.wait_ge(S["mc_dve"], c + 1)
                nc.scalar.activation(m_u[:, c, :], m_u[:, c, :], ACT.Silu).then_inc(S["mc_act"], 1)
            for g in range(4):
                act.wait_ge(*S.at("mx_mm", g + 1))
                h = g % 2
                if g < 2:
                    ins = nc.scalar.copy(m_dt[0:64, h * HALF:(h + 1) * HALF], ps[0:64, g, :])
                else:
                    ins = nc.scalar.copy(m_bc[:, h * HALF:(h + 1) * HALF], ps[:, g, :])
                ins.then_inc(S["mx_ev_a"], 1)
            for c in range(IC):
                act.wait_ge(*S.at("md_ev_d", 2 * c + 2))
                nc.scalar.activation(m_s[:, c, :], m_delta[:, c, :], ACT.Abs).then_inc(S["m_abs"], 1)
            nc.scalar.activation(m_a, m_a, ACT.Exp).then_inc(S["m_ea"], 1)
            for c in range(IC):
                act.wait_ge(S["m_abs"], c + 1)
                nc.scalar.activation(m_s[:, c, :], m_s[:, c, :], ACT.Exp, scale=-1.0).then_inc(S["m_e"], 1)

            def c_copy(nn, par):
                act.wait_ge(S["m_c"], nn + 1)
                if not isinstance(nn, int) or nn >= 2:
                    act.wait_ge(S["m_hc"], 2 * nn - 2)
                nc.scalar.copy(m_cb[:, par, :], ps[:, 6:8, :].rearrange("p a b -> p (a b)")).then_inc(S["m_cc"], 1)

            def decay(w, slot, c, n):
                if not isinstance(w, int) or w >= 4:
                    act.wait_ge(S["m_hs"], w - 3)
                nc.scalar.activation(
                    m_da[:, slot, :].rearrange("p (b t) -> p b t", t=L)[:, :, 1:L],
                    m_delta[:, c, :].rearrange("p (b t) -> p b t", t=L)[:, :, 1:L], ACT.Exp,
                    scale=m_a[:, c, bass.ds(n, 1)]).then_inc(S["m_dec"], 1)

            act.wait_ge(S["m_ready"], 1)
            for q in range(2):
                o = NS * q
                for n0 in range(2):
                    c_copy(o + n0, n0)
                    for cc in range(2):
                        decay(2 * (o + n0) + cc, 2 * n0 + cc, 2 * q + cc, n0)
                with act.Fori(1, NS // 2) as i:
                    for n0 in range(2):
                        n = 2 * i + n0
                        c_copy(n + o, n0)
                        for cc in range(2):
                            decay(2 * n + (2 * o + cc), 2 * n0 + cc, 2 * q + cc, n)

        def m_dve(ch):
            dve = ch.eng
            norm_dve(ch, "mn", xT, U[1], U[3][:, 0, :], U[1])
            signal("mr_in")
            dve.wait_ge(S["ld_m1"], dma_n["ld_m1"])
            norm_dve(ch, "mr", None, U[1], U[3][:, 1, :], U[2], rms=True, gain=m_nw)
            for g in range(8):
                dve.wait_ge(*S.at("mi_mm", g + 1))
                nc.vector.tensor_copy(half(m_xm, g // 2, g % 2), ps[:, g, :]).then_inc(S["mi_ev_d"], 1)
            dve.wait_ge(S["ld_m"], dma_n["ld_m"])
            for c in range(IC):
                dve.wait_ge(*S.at("mi_ev_d", 2 * c + 2))
                x3 = m_xm[:, c, :].rearrange("p (b t) -> p b t", t=L)
                u3 = m_u[:, c, :].rearrange("p (b t) -> p b t", t=L)
                ch.link(nc.vector.tensor_scalar(m_u[:, c, :], m_xm[:, c, :], m_cw[:, c, KW - 1:KW],
                                                m_cb1[:, c:c + 1], ALU.mult, ALU.add))
                for s in range(1, KW):
                    ins = nc.vector.scalar_tensor_tensor(out=u3[:, :, s:], in0=x3[:, :, :L - s],
                                                         scalar=m_cw[:, c, KW - 1 - s:KW - s], in1=u3[:, :, s:],
                                                         op0=ALU.mult, op1=ALU.add)
                    if s < KW - 1:
                        ch.link(ins)
                ins.then_inc(S["mc_dve"], 1)
            dve.wait_ge(*S.at("mx_ev_a", 4))
            nc.vector.tensor_copy(m_part[:, 0, :], m_bc).then_inc(S["m_parts"], 1)
            dve.wait_ge(S["m_parts"], 1)
            ch.link(nc.vector.tensor_tensor(m_bc, m_bc, m_part[:, 0, :], ALU.subtract))
            nc.vector.tensor_copy(m_part[:, 1, :], m_bc).then_inc(S["m_parts"], 1)
            dve.wait_ge(S["m_parts"], 2)
            ch.link(nc.vector.tensor_tensor(m_bc, m_bc, m_part[:, 1, :], ALU.subtract))
            nc.vector.tensor_copy(m_part[:, 2, :], m_bc).then_inc(S["m_parts"], 1)
            for g in range(8):
                m, h = g // 2, g % 2
                dve.wait_ge(*S.at("md_mm", g + 1))
                nc.vector.tensor_scalar(half(m_delta, m, h), ps[:, g, :], m_bdt[:, m:m + 1], None,
                                        ALU.add).then_inc(S["md_ev_d"], 1)
            dve.wait_ge(S["m_e"], IC)
            dve.wait_ge(S["m_ea"], 1)
            ch.link(nc.vector.tensor_scalar(m_a, m_a, -1.0, None, ALU.mult))
            for c in range(IC):
                s, s2, p = m_s[:, c, :], m_s2[:, c, :], m_p[:, c, :]
                ch.link(nc.vector.tensor_scalar(p, s, 2.0, None, ALU.add))
                ch.link(nc.vector.reciprocal(p, p))
                ch.link(nc.vector.tensor_tensor(s, s, p, ALU.mult))
                ch.link(nc.vector.tensor_tensor(s2, s, s, ALU.mult))
                ch.link(nc.vector.tensor_scalar(p, s2, 1.0 / 15, None, ALU.mult))
                for k in range(6, 0, -1):
                    ch.link(nc.vector.scalar_tensor_tensor(out=p, in0=p, scalar=1.0 / (2 * k + 1), in1=s2,
                                                           op0=ALU.add, op1=ALU.mult))
                ch.link(nc.vector.scalar_tensor_tensor(out=p, in0=p, scalar=1.0, in1=s, op0=ALU.add, op1=ALU.mult))
                ch.link(nc.vector.tensor_scalar(m_delta[:, c, :], m_delta[:, c, :], 0.0, None, ALU.max))
                ch.link(nc.vector.scalar_tensor_tensor(out=m_delta[:, c, :], in0=p, scalar=2.0, in1=m_delta[:, c, :],
                                                       op0=ALU.mult, op1=ALU.add))
                ch.link(nc.vector.tensor_tensor(m_du[:, c, :], m_delta[:, c, :], m_u[:, c, :], ALU.mult))
            nc.vector.memset(m_da.rearrange("p a t -> p (a t)"), 0.0).then_inc(S["m_ready"], 1)

            def inputs_of(nn, w, n0, q):
                dve.wait_ge(S["m_b"], nn + 1)
                for cc in range(2):
                    if not isinstance(w, int) or w >= 4:
                        dve.wait_ge(S["m_hc"], w + cc - 3)
                    nc.vector.tensor_tensor(m_h[:, 2 * n0 + cc, :], m_du[:, 2 * q + cc, :],
                                            ps[:, 4:6, :].rearrange("p a b -> p (a b)"),
                                            ALU.mult).then_inc(S["m_dbu"], 1)

            def scans(w, n0):
                for cc in range(2):
                    sl = 2 * n0 + cc
                    dve.wait_ge(S["m_dec"], w + cc + 1)
                    dve.wait_ge(S["m_dbu"], w + cc + 1)
                    nc.vector.tensor_tensor_scan(m_h[:, sl, :], m_da[:, sl, :], m_h[:, sl, :], 0.0,
                                                 ALU.mult, ALU.add).then_inc(S["m_hs"], 1)

            for q in range(2):
                o = NS * q
                for n0 in range(2):
                    inputs_of(o + n0, 2 * (o + n0), n0, q)
                    scans(2 * (o + n0), n0)
                with dve.Fori(1, NS // 2) as i:
                    for n0 in range(2):
                        n = 2 * i + n0
                        inputs_of(n + o, 2 * n + 2 * o, n0, q)
                        scans(2 * n + 2 * o, n0)
                dve.wait_ge(S["m_acc"], MU * (q + 1))
                for cc in range(2):
                    for h in range(NH):
                        c = 2 * q + cc
                        nc.vector.scalar_tensor_tensor(out=half(m_xm, c, h), in0=half(m_u, c, h),
                                                       scalar=m_dp[:, c:c + 1], in1=ps[:, 2 * cc + h, :],
                                                       op0=ALU.mult, op1=ALU.add).then_inc(S["my_ev"], 1)
            dve.wait_ge(S["m_res"], 1)
            for g in range(4):
                m, h = g // 2, g % 2
                dve.wait_ge(*S.at("mo_mm", g + 1))
                ch.link(nc.vector.tensor_tensor(half(xT, m, h), half(xT, m, h), ps[:, g, :], ALU.add))

        def m_pool(pool):
            def used(nn, w, n0):
                pool.wait_ge(S["m_cc"], nn + 1)
                for cc in range(2):
                    pool.wait_ge(S["m_hs"], w + cc + 1)
                    if not isinstance(w, int) or w >= 2:
                        pool.wait_ge(S["m_acc"], w + cc - 1)
                    nc.gpsimd.tensor_tensor(m_hc[:, cc, :], m_h[:, 2 * n0 + cc, :], m_cb[:, n0, :],
                                            ALU.mult).then_inc(S["m_hc"], 1)

            pool.wait_ge(*S.at("mn_out", 2))
            pool.wait_ge(S["m_ready"], 1)
            nc.gpsimd.tensor_tensor(xT, xT, U[1], ALU.add).then_inc(S["m_res"], 1)
            for q in range(2):
                o = NS * q
                for n0 in range(2):
                    used(o + n0, 2 * (o + n0), n0)
                with pool.Fori(1, NS // 2) as i:
                    for n0 in range(2):
                        n = 2 * i + n0
                        used(n + o, 2 * n + 2 * o, n0)
                pool.wait_ge(S["my_ev"], 4 * (q + 1))
                for cc in range(2):
                    c = 2 * q + cc
                    nc.gpsimd.tensor_tensor(m_xm[:, c, :], m_xm[:, c, :], m_z[:, c, :],
                                            ALU.mult).then_inc(S["m_gate"], 1)

        def router_areas(o):
            return dict(w=view(o, DC, E), b=view(o + 16, E), lg=view(o + 24, TT, E), pr=view(o + 88, TT, E),
                        m8=view(o + 152, TT, E), ix=view(o + 216, TT, E).bitcast(U32), ixf=view(o + 280, TT, E),
                        e1=view(o + 344, TT, E), e2=view(o + 408, TT, E), s=view(o + 472, 4, TT),
                        cT=view(o + 512, T), cS=view(o + 512 + T, T), part=bview(o + 512 + 2 * T, 3, T))

        def route_pe(pe, n, R, xf):
            for t in range(TT):
                for k in range(DC):
                    mm = nc.tensor.matmul(ps[:, 4, t * E:(t + 1) * E], xf[:, k, t * P:(t + 1) * P], R["w"][:, k, :],
                                          start=(k == 0), stop=(k == 1))
            mm.then_inc(S[n + "_lg"], 1)
            pe.wait_ge(S[n + "_cm"], 1)
            for t in range(TT):
                mm = nc.tensor.transpose(ps[0:E, 5 + t // 4, (t % 4) * P:(t % 4 + 1) * P], R["e1"][:, t, :], ident)
            mm.then_inc(S[n + "_cT"], 1)

        def route_act(act, n, R, renorm):
            act.wait_ge(S[n + "_sub"], 1)
            nc.scalar.activation(R["pr"], R["lg"], ACT.Exp).then_inc(S[n + "_exp"], 1)
            if renorm:
                act.wait_ge(S[n + "_d"], 1)
                nc.scalar.activation(R["s"][:, 2, :], R["s"][:, 1, :], ACT.Exp).then_inc(S[n + "_e2"], 1)

        def route_dve(ch, n, R, renorm):
            dve, ln = ch.eng, ch.link
            v = nc.vector

            def over_e(x):
                return x.unsqueeze(2).broadcast_to([P, TT, E])
            dve.wait_ge(S[n + "_lg"], 1)
            ln(v.tensor_tensor(R["lg"], ps[:, 4, 0:TT * E].rearrange("p (t e) -> p t e", e=E),
                               R["b"].unsqueeze(1).broadcast_to([P, TT, E]), ALU.add))
            ln(v.tensor_reduce(R["s"][:, 0, :], R["lg"], AX.X, ALU.max))
            v.tensor_tensor(R["lg"], R["lg"], over_e(R["s"][:, 0, :]), ALU.subtract).then_inc(S[n + "_sub"], 1)
            dve.wait_ge(S[n + "_exp"], 1)
            ln(v.tensor_reduce(R["s"][:, 0, :], R["pr"], AX.X, ALU.add))
            ln(v.reciprocal(R["s"][:, 0, :], R["s"][:, 0, :]))
            ln(v.tensor_tensor(R["pr"], R["pr"], over_e(R["s"][:, 0, :]), ALU.mult))
            for t in range(TT):
                ch.step(v.max(R["m8"][:, t, :], R["pr"][:, t, :]))
            ch.sync()
            for t in range(TT):
                ch.step(v.max_index(R["ix"][:, t, :], R["m8"][:, t, :], R["pr"][:, t, :]))
            ch.sync()
            ln(v.tensor_copy(R["ixf"], R["ix"]))
            w1, w2 = R["m8"][:, :, 0], R["m8"][:, :, 1]
            if renorm:
                v.tensor_tensor(R["s"][:, 1, :], w2, w1, ALU.subtract).then_inc(S[n + "_d"], 1)
                dve.wait_ge(S[n + "_e2"], 1)
                ln(v.tensor_scalar(R["s"][:, 1, :], R["s"][:, 2, :], 1.0, None, ALU.add))
                ln(v.reciprocal(R["s"][:, 0, :], R["s"][:, 1, :]))
                ln(v.tensor_tensor(R["s"][:, 3, :], R["s"][:, 2, :], R["s"][:, 0, :], ALU.mult))
                w1, w2 = R["s"][:, 0, :], R["s"][:, 3, :]
            for k, (w, e) in enumerate(((w1, "e1"), (w2, "e2"))):
                ln(v.tensor_tensor(R[e], iota8.unsqueeze(1).broadcast_to([P, TT, E]), over_e(R["ixf"][:, :, k]),
                                   ALU.is_equal))
                ln(v.tensor_tensor(R[e], R[e], over_e(w), ALU.mult))
            v.tensor_tensor(R["e1"], R["e1"], R["e2"], ALU.add).then_inc(S[n + "_cm"], 1)
            dve.wait_ge(S[n + "_cT"], 1)
            ln(v.tensor_copy(R["cT"][0:E, :], ps[0:E, 5:7, :].rearrange("p a b -> p (a b)")))

        def route_parts(ch, n, R):
            rest, part = R["cT"], R["part"]
            ch.eng.wait_ge(S[n + "_zero"], 1)
            for k in range(3):
                ins = nc.vector.tensor_copy(part[0:E, k, :], rest[0:E, :])
                if k == 2:
                    ins.then_inc(S[n + "_part"], 1)
                    break
                ch.link(ins)
                ch.link(nc.vector.tensor_tensor(R["cS"][0:E, :], rest[0:E, :], part[0:E, k, :], ALU.subtract))
                rest = R["cS"]

        def route_pool(pool, n, R, stage_in):
            pool.wait_ge(*S.at(stage_in, 1))
            nc.gpsimd.memset(R["part"].rearrange("p k t -> p (k t)"), 0.0).then_inc(S[n + "_zero"], 1)

        def weight_pe(R, e, h):
            for k in range(3):
                mm = nc.tensor.matmul(ps[:, 6 + h, :], identb[:, bass.ds(e, 1)].broadcast_to([P, P]),
                                      R["part"][:, k, h * HALF:(h + 1) * HALF], start=(k == 0), stop=(k == 2))
            return mm

        f_q = U[3]
        f_k = view(8 * K, T)
        f_v = view(9 * K, TT, P)
        f_o = U[5]
        f_S = [view(12 * K + 512 * j, 4, P) for j in range(2)]
        f_pT = [view(13 * K + 512 * j, HALF) for j in range(2)]
        f_st = [view(14 * K + 16 * j, 3, 4) for j in range(2)]
        f_neg = view(14 * K + 64, P)
        f_g = view(14 * K + 256, 2, DC)
        f_wq, f_wkv, f_wo = view(15 * K, DC, D), view(15 * K + 512, DC, 2 * P), view(16 * K, DC, D)
        f_R = router_areas(17 * K)
        f_w13 = [view(21 * K + 1024 * j, DC, 2 * D) for j in range(2)]
        f_w2 = [view(23 * K + 512 * j, DC, D) for j in range(2)]
        f_sa = view(24 * K, 2, HALF)
        f_sb = view(25 * K, HALF)
        f_h = [view(26 * K + 1024 * j, 2, HALF) for j in range(2)]

        def f_load(sp):
            sp.wait_ge(*S.at("fn_in", 1))
            load(sp, "ld_f", (f_wq, A["L0_ffn_Wq"]), (f_wkv, A["L0_ffn_Wkv"]), (f_wo, A["L0_ffn_Wo"]),
                 (f_g[:, 0, :], A["L0_ffn_g1"]), (f_g[:, 1, :], A["L0_ffn_g2"]), (f_neg, A["c_neg"]),
                 (f_R["w"], A["L0_ffn_Wr"]), (f_R["b"], A["L0_ffn_expert_bias"]))
            sp.dma_start(f_w13[1], A["L0_ffn_sW13"]).then_inc(S["fe_wt1"], 16)
            sp.dma_start(f_w2[1], A["L0_ffn_sW2"]).then_inc(S["fe_wt1"], 16)

            def expert(e, j):
                sp.dma_start(f_w13[j], A["L0_ffn_eW13"][:, bass.ds(e, 1)].rearrange("p a k f -> p (a k) f"))\
                    .then_inc(S[f"fe_wt{j}"], 16)
                sp.dma_start(f_w2[j], A["L0_ffn_eW2"][:, bass.ds(e, 1)].rearrange("p a k f -> p (a k) f"))\
                    .then_inc(S[f"fe_wt{j}"], 16)
            expert(0, 0)
            sp.wait_ge(S["fe_w2"], 2)
            expert(1, 1)
            with sp.Fori(1, E // 2) as i:
                for j in range(2):
                    sp.wait_ge(S["fe_w2"], 4 * i + 2 * j)
                    expert(2 * i + j, j)

        def f_pe(pe):
            norm_pe(pe, "fn", xT, U[2])
            norm_pe(pe, "fr", U[1], U[2], rms=True)
            pe.wait_ge(*S.at("fr_out", 4))
            pe.wait_ge(S["ld_f"], dma_n["ld_f"])
            dense_pe(pe, "fq", [(P, [(w[:, k, m * P:(m + 1) * P], half(U[2], k, h)) for k in range(DC)])
                                for w, m in ((f_wq, 0), (f_wq, 1), (f_wkv, 0)) for h in range(NH)],
                     "d" * 6, list(range(6)))
            for t in range(TT):
                for k in range(DC):
                    mm = nc.tensor.matmul(ps[:, 6 + t // 4, (t % 4) * P:(t % 4 + 1) * P],
                                          U[2][:, k, t * P:(t + 1) * P], f_wkv[:, k, P:2 * P],
                                          start=(k == 0), stop=(k == 1))
                if t % 4 == 3:
                    mm.then_inc(S["f_v"], 1)
            pe.wait_ge(*S.at("fq_ev_d", 6))

            def sc(t):
                if t >= 2:
                    pe.wait_ge(S["f_sm"], t - 1)
                if t == 0:
                    pe.wait_ge(*S.at("fq_ev_d", 6))
                for hd in range(4):
                    r = slice(64 * (hd % 2), 64 * (hd % 2) + 64)
                    mm = nc.tensor.matmul(ps[:, 2 * (t % 2) + hd % 2, (hd // 2) * P:(hd // 2 + 1) * P],
                                          f_q[r, hd // 2, t * P:(t + 1) * P],
                                          f_k[r, t * P:(t + 1) * P], start=True, stop=True)
                mm.then_inc(S["f_s"], 1)

            def turn(t):
                pe.wait_ge(S["f_norm"], t + 1)
                for hd in range(4):
                    mm = nc.tensor.transpose(ps[:, 4 + t % 2, hd * P:(hd + 1) * P], f_S[t % 2][:, hd, :], ident)
                mm.then_inc(S["f_pt"], 1)
                pe.wait_ge(S["f_ptev"], t + 1)
                if t >= 2:
                    pe.wait_ge(S["f_oev"], 2 * t - 2)
                nc.tensor.matmul(ps[:, 6 + t % 2, :], f_v[:, t, :], f_pT[t % 2], start=True,
                                 stop=True).then_inc(S["f_pv"], 1)

            pe.wait_ge(S["f_vev"], 2)
            sc(0)
            for t in range(TT):
                if t + 1 < TT:
                    sc(t + 1)
                turn(t)
            pe.wait_ge(S["f_oev"], 2 * TT)
            dense_pe(pe, "fw", [(P, [(f_wo[:, k, m * P:(m + 1) * P], half(f_o, k, h)) for k in range(DC)])
                                for m in range(DC) for h in range(NH)], "dddd", [0, 1, 6, 7])
            norm_pe(pe, "f2", U[1], U[2], rms=True)
            pe.wait_ge(*S.at("f2_out", 4))
            route_pe(pe, "fr", f_R, U[2])

            def up(v, h, j, e):
                for f in range(2):
                    for part in range(2):
                        if not isinstance(v, int) or v or f:
                            pe.wait_ge(S[("fe_sa", "fe_sb")[part]], 2 * v + f)
                        for k in range(DC):
                            mm = nc.tensor.matmul(ps[:, 4 + part, :],
                                                  f_w13[j][:, k, part * D + f * P:part * D + (f + 1) * P],
                                                  half(U[2], k, h), start=(k == 0), stop=(k == 1))
                        mm.then_inc(S["fe_ab"], 1)
                    if f == 0 and e is not None:
                        if not isinstance(v, int) or v >= 2:
                            pe.wait_ge(S["fe_h"], 2 * v - 2)
                        weight_pe(f_R, e, h).then_inc(S["fe_c"], 1)

            def down(v, h, j, start, stop):
                pe.wait_ge(S["fe_h"], 2 * v + 2)
                for m in range(DC):
                    for f in range(2):
                        mm = nc.tensor.matmul(ps[:, 2 * m + h, :], f_w2[j][:, f, m * P:(m + 1) * P], f_h[h][:, f, :],
                                              start=start and f == 0, stop=stop and f == 1, skip_group_check=True)
                mm.then_inc(S["fe_w2"], 1)

            pe.wait_ge(S["fr_part"], 1)
            pe.wait_ge(S["fe_wt1"], 32)
            up(0, 0, 1, None)
            up(1, 1, 1, None)
            down(0, 0, 1, True, False)

            def expert_pair(i, first_pair):
                for j in range(2):
                    v = 4 * i + 2 + 2 * j
                    pe.wait_ge(S[f"fe_wt{j}"], 32 * i + 32 + 32 * j)
                    up(v, 0, j, 2 * i + j)
                    down(v - 1, 1, 1 - j, first_pair and j == 0, False)
                    up(v + 1, 1, j, 2 * i + j)
                    down(v, 0, j, False, False)
            expert_pair(0, True)
            with pe.Fori(1, E // 2) as i:
                expert_pair(i, False)
            down(2 * E + 1, 1, 1, False, True)

        def f_act(act):
            norm_act(act, "fn", U[1], U[2], U[3][:, 0, :], 0)
            act.wait_ge(*S.at("fn_out", 2))
            norm_act(act, "fr", U[1], U[2], U[3][:, 1, :], 2, rms=True)
            for n in range(2):
                act.wait_ge(S["f_v"], n + 1)
                nc.scalar.copy(f_v[:, 4 * n:4 * n + 4, :].rearrange("p a b -> p (a b)"), ps[:, 6 + n, :])\
                    .then_inc(S["f_vev"], 1)
            for t in range(TT + 1):
                if t < TT:
                    act.wait_ge(S["f_max"], t + 1)
                    for hd in range(4):
                        nc.scalar.activation(f_S[t % 2][:, hd, :], f_S[t % 2][:, hd, :], ACT.Exp,
                                             bias=f_st[t % 2][:, 0, hd:hd + 1],
                                             accum_out=f_st[t % 2][:, 1, hd:hd + 1]).then_inc(S["f_exp"], 1)
                if t >= 1:
                    act.wait_ge(S["f_pt"], t)
                    if t >= 3:
                        act.wait_ge(S["f_pv"], t - 2)
                    nc.scalar.copy(f_pT[(t - 1) % 2], ps[:, 4 + (t - 1) % 2, :]).then_inc(S["f_ptev"], 1)
            act.wait_ge(*S.at("f2_in", 1))
            norm_act(act, "f2", U[1], U[2], U[3][:, 1, :], 2, rms=True)
            route_act(act, "fr", f_R, True)

            def gate(r, f):
                act.wait_ge(S["fe_ab"], 2 * r + 1)
                if not isinstance(r, int) or r >= 2:
                    act.wait_ge(S["fe_sb"], r - 1)
                nc.scalar.activation(f_sa[:, f, :], ps[:, 4, :], ACT.Silu).then_inc(S["fe_sa"], 1)
            for r in range(4):
                gate(r, r % 2)
            with act.Fori(1, E + 1) as i:
                for r in range(4):
                    gate(4 * i + r, r % 2)

        def f_dve(ch):
            dve = ch.eng
            norm_dve(ch, "fn", xT, U[1], U[3][:, 0, :], U[1])
            signal("fr_in")
            dve.wait_ge(S["ld_f"], dma_n["ld_f"])
            norm_dve(ch, "fr", None, U[1], U[3][:, 1, :], U[2], rms=True, gain=f_g[:, 0, :])
            for g in range(6):
                dve.wait_ge(*S.at("fq_mm", g + 1))
                dst = half(f_q, g // 2, g % 2) if g < 4 else f_k[:, (g - 4) * HALF:(g - 3) * HALF]
                nc.vector.tensor_scalar(dst, ps[:, g, :], 0.125 if g < 4 else 1.0, None,
                                        ALU.mult).then_inc(S["fq_ev_d"], 1)

            def soft(t):
                st = f_st[t % 2]
                dve.wait_ge(S["f_s"], t + 1)
                if t >= 2:
                    dve.wait_ge(S["f_pt"], t - 1)
                nc.vector.tensor_tensor(f_S[t % 2].rearrange("p (o c) k -> p o c k", o=2),
                                        ps[:, 2 * (t % 2):2 * (t % 2) + 2, 0:2 * P].rearrange("p o (c k) -> p o c k", c=2),
                                        f_neg.unsqueeze(1).unsqueeze(1).broadcast_to([P, 2, 2, P]), ALU.add).then_inc(S["f_sm"], 1)
                dve.wait_ge(S["f_sm"], t + 1)
                ch.link(nc.vector.tensor_reduce(st[:, 2, :], f_S[t % 2], AX.X, ALU.max))
                nc.vector.tensor_scalar(st[:, 0, :], st[:, 2, :], -1.0, None, ALU.mult).then_inc(S["f_max"], 1)

            soft(0)
            for t in range(TT):
                if t + 1 < TT:
                    soft(t + 1)
                dve.wait_ge(S["f_exp"], 4 * t + 4)
                nc.vector.reciprocal(f_st[t % 2][:, 2, :], f_st[t % 2][:, 1, :]).then_inc(S["f_rec"], 1)
                if t >= 1:
                    heads_out(dve, t - 1)
            heads_out(dve, TT - 1)
            for g in range(4):
                m, h = g // 2, g % 2
                dve.wait_ge(*S.at("fw_mm", g + 1))
                ch.link(nc.vector.tensor_tensor(half(U[1], m, h), half(U[1], m, h),
                                                ps[:, (0, 1, 6, 7)[g], :], ALU.add))
            signal("f2_in")
            norm_dve(ch, "f2", None, U[1], U[3][:, 1, :], U[2], rms=True, gain=f_g[:, 1, :])
            route_dve(ch, "fr", f_R, True)
            route_parts(ch, "fr", f_R)

            def product(v, r, h, f, e):
                dve.wait_ge(S["fe_sa"], r + 1)
                dve.wait_ge(S["fe_ab"], 2 * r + 2)
                nc.vector.tensor_tensor(f_sb, f_sa[:, f, :], ps[:, 5, :], ALU.mult).then_inc(S["fe_sb"], 1)
                dve.wait_ge(S["fe_sb"], r + 1)
                if not isinstance(v, int) or v >= 2:
                    dve.wait_ge(S["fe_w2"], v - 1)
                if e:
                    dve.wait_ge(S["fe_c"], v - 1)
                    ins = nc.vector.tensor_tensor(f_h[h][:, f, :], f_sb, ps[:, 6 + h, :], ALU.mult)
                else:
                    ins = nc.vector.tensor_copy(f_h[h][:, f, :], f_sb)
                ins.then_inc(S["fe_h"], 1)
                dve.wait_ge(S["fe_h"], r + 1)
            for h in range(NH):
                for f in range(2):
                    product(h, 2 * h + f, h, f, False)
            with dve.Fori(1, E + 1) as i:
                for h in range(NH):
                    for f in range(2):
                        product(2 * i + h, 4 * i + 2 * h + f, h, f, True)
            dve.wait_ge(S["f_res"], 1)
            dve.wait_ge(S["fe_w2"], 2 * E + 2)
            for g in range(4):
                ch.link(nc.vector.tensor_tensor(half(xT, g // 2, g % 2), half(xT, g // 2, g % 2),
                                                ps[:, g, :], ALU.add))

        def heads_out(dve, t):
            dve.wait_ge(S["f_pv"], t + 1)
            for o in range(2):
                r = slice(64 * o, 64 * o + 64)
                nc.vector.tensor_copy(f_o[r, :, t * P:(t + 1) * P],
                                      ps[r, 6 + t % 2, :].rearrange("p (o c q) -> p o c q", c=2, o=2)[:, o, :, :])\
                    .then_inc(S["f_oev"], 1)

        def f_pool(pool):
            route_pool(pool, "fr", f_R, "fn_in")
            for t in range(TT):
                pool.wait_ge(S["f_rec"], t + 1)
                nc.gpsimd.tensor_tensor(f_S[t % 2], f_S[t % 2],
                                        f_st[t % 2][:, 2, :].unsqueeze(2).broadcast_to([P, 4, P]),
                                        ALU.mult).then_inc(S["f_norm"], 1)
            pool.wait_ge(*S.at("f2_in", 1))
            nc.gpsimd.tensor_tensor(xT, xT, U[1], ALU.add).then_inc(S["f_res"], 1)

        IP = SK + 1
        d_m2 = U[3]
        d_xs = [view(34 * K + 256 * j, DC, P) for j in range(2)]
        d_ctx = [view(35 * K + 520 * j, DC, SK) for j in range(2)]
        d_sq = [view(37 * K + 520 * j, DC, SK) for j in range(2)]
        d_dt = [view(39 * K + 260 * j, SK) for j in range(2)]
        d_bb = view(40 * K, TT)
        d_R = view(8 * K, L + 1, IP)
        d_D = view(17 * K, L, SK)
        d_t = view(25 * K + 256, L, SK)
        d_diag = bview(34 * K, L, IP)
        d_left = bview(38 * K + 256, L, IP)
        d_up = bview(17 * K, L, IP)
        d_V = bview(21 * K + 256, L, IP)
        d_min = view(42 * K + 640, SK)
        d_E, d_VD = view(42 * K + 640, IP), view(43 * K, IP)
        d_M = view(8 * K, 3, B, L)
        CT = 4
        d_ct = [view(26 * K + 512 * j, 2, D) for j in range(CT)]
        d_c2 = [view(29 * K + 256 * j, D) for j in range(CT)]

        def d_load(sp):
            sp.wait_ge(*S.at("dn_in", 1))

            def ctx_load(b, j):
                sp.dma_start(d_ctx[j], A["ctxT"][:, :, bass.ds(b * SK, SK)]).then_inc(S[f"d_ctx{j}"], 16)

            def keep(g, j):
                sp.wait_ge(S["d_sqrt"], g + 1)
                sp.dma_start(dist[bass.ds(g, 1)].rearrange("a p i -> (a p) i"), d_dt[j]).then_inc(S[f"d_out{j}"], 16)
            ctx_load(0, 0)
            ctx_load(1, 1)

            def ahead(g, count, j):
                for bi in range(count):
                    b = 4 * g + bi + 2
                    sp.wait_ge(S["d_ab"], b - 1)
                    ctx_load(b, bi % 2)
                if j is not None:
                    keep(g - 1, j)
            ahead(0, 4, None)
            ahead(1, 4, 0)
            with sp.Fori(1, TT // 2 - 1) as i:
                ahead(2 * i, 4, 1)
                ahead(2 * i + 1, 4, 0)
            ahead(TT - 2, 4, 1)
            ahead(TT - 1, 2, 0)
            keep(TT - 1, 1)
            for j in range(2):
                sp.wait_ge(S[f"d_out{j}"], 16 * TT // 2)
            sp.dma_start(d_D[0:B].rearrange("p j i -> p (j i)"),
                         dist.rearrange("g (s j) i -> (g s) (j i)", j=L)).then_inc(S["d_back"], 16)

            def rows(b, j):
                sp.dma_start(d_ct[j], A["ctx_rows"][:, bass.ds(b, 1)].rearrange("p a t d -> p (a t) d"))\
                    .then_inc(S[f"d_rows{j}"], 16)
                sp.dma_start(d_c2[j][0:1], A["ctx_last"][:, bass.ds(b, 1)].rearrange("p a d -> p (a d)"))\
                    .then_inc(S[f"d_rows{j}"], 16)
            sp.wait_ge(S["d_choice"], 3)
            for j in range(CT):
                rows(j, j)
            with sp.Fori(1, B // CT) as i:
                for j in range(CT):
                    sp.wait_ge(S["d_exp"], CT * i + j - CT + 1)
                    rows(CT * i + j, j)

        def d_pe(pe):
            norm_pe(pe, "dn", xT, U[2])
            pe.wait_ge(S["d_tsq"], 1)
            for g in range(TT):
                for k in range(DC):
                    mm = nc.tensor.matmul(ps[:, 4, g:g + 1], U[2][:, k, g * P:(g + 1) * P], ones[:, 0:1],
                                          start=(k == 0), stop=(k == 1))
            mm.then_inc(S["d_bb"], 1)

            def tile(g, j, i):
                pe.wait_ge(S["d_xs"], g + 1)
                if not isinstance(g, int) or g >= 2:
                    pe.wait_ge(S["d_clip"], g - 1)
                for bi in range(4):
                    b = 4 * g + bi
                    pe.wait_ge(S["d_sq"], b + 1)
                    dst = ps[32 * bi:32 * bi + 32, j, 0:SK]
                    for k in range(DC):
                        nc.tensor.matmul(dst, ones, d_sq[bi % 2][:, k, :], start=(k == 0), stop=False)
                    for k in range(DC):
                        mm = nc.tensor.matmul(dst, d_xs[j][:, k, 32 * bi:32 * bi + 32], d_ctx[bi % 2][:, k, :],
                                              start=False, stop=(k == 1))
                    mm.then_inc(S["d_ab"], 1)
            tile(0, 0, 0)
            tile(1, 1, 0)
            with pe.Fori(1, TT // 2) as i:
                for j in range(2):
                    tile(2 * i + j, j, i)
            for n in range(L):
                pe.wait_ge(S["d_v"], n + 1)
                j = L - 1 - n
                for t in range(3):
                    rows = min(P, SK - t * P)
                    mm = nc.tensor.transpose(
                        ps[0:rows, t, :].bitcast(BF16)[:, j * B:(j + 1) * B],
                        d_V[0:B, j, t * P:t * P + rows],
                        identb[0:B, 0:B])
                mm.then_inc(S["d_vT"], 1)
            pe.wait_ge(S["d_mev"], 3)

            def expand(b, j, i):
                pe.wait_ge(S[f"d_rows{j}"], 32 * i + 32)
                if not isinstance(b, int) or b >= 2:
                    pe.wait_ge(S["d_add"], b - 1)
                for c in range(DC):
                    for t in range(3):
                        rows = min(P, SK - t * P)
                        lhsT = d_ct[j][:, t, c * P:(c + 1) * P] if t < 2 else d_c2[j][0:1, c * P:(c + 1) * P]
                        mm = nc.tensor.matmul(ps[:, 4 + j % 2, c * L:(c + 1) * L], lhsT,
                                              d_M[0:rows, t, bass.ds(b, 1), :].rearrange("p a j -> p (a j)"),
                                              start=(t == 0), stop=(t == 2))
                mm.then_inc(S["d_exp"], 1)
            for j in range(CT):
                expand(j, j, 0)
            with pe.Fori(1, B // CT) as i:
                for j in range(CT):
                    expand(CT * i + j, j, i)

        def d_act(act):
            norm_act(act, "dn", U[1], U[2], U[3][:, 0, :], 0)
            act.wait_ge(*S.at("dn_out", 2))
            nc.scalar.activation(U[2], U[1], ACT.Square).then_inc(S["d_tsq"], 1)

            def squares(b, j, i, half_i):
                act.wait_ge(S[f"d_ctx{j}"], 16 * half_i + 16)
                if not isinstance(b, int) or b >= 2:
                    act.wait_ge(S["d_ab"], b - 1)
                nc.scalar.activation(d_sq[j], d_ctx[j], ACT.Square).then_inc(S["d_sq"], 1)

            def root(g, j):
                act.wait_ge(S["d_clip"], g + 1)
                nc.scalar.activation(d_dt[j], d_dt[j], ACT.Sqrt).then_inc(S["d_sqrt"], 1)

            def tile(g, j, i):
                for bi in range(4):
                    squares(4 * g + bi, bi % 2, i, 2 * g + bi // 2)
            tile(0, 0, 0)
            tile(1, 1, 0)
            root(0, 0)
            with act.Fori(1, TT // 2) as i:
                for j in range(2):
                    tile(2 * i + j, j, i)
                    root(2 * i + j - 1, 1 - j)
            root(TT - 1, 1)
            act.wait_ge(S["d_vT"], L)
            for t in range(3):
                rows = min(P, SK - t * P)
                nc.scalar.copy(d_M[0:rows, t].rearrange("p b j -> p j b"),
                               ps[0:rows, t, :].bitcast(BF16).rearrange("p (j b) -> p j b", j=L)).then_inc(S["d_mev"], 1)

        def d_dve(ch):
            dve = ch.eng
            norm_dve(ch, "dn", xT, U[1], U[3][:, 0, :], U[1])
            nc.vector.tensor_scalar(d_m2, U[1], -2.0, None, ALU.mult).then_inc(S["d_m2"], 1)
            dve.wait_ge(S["d_bb"], 1)
            ch.link(nc.vector.tensor_copy(d_bb, ps[:, 4, 0:TT]))

            def clip(g, j):
                dve.wait_ge(S["d_ab"], 4 * g + 4)
                if not isinstance(g, int) or g >= 2:
                    dve.wait_ge(S[f"d_out{j}"], 8 * (g - j))
                nc.vector.tensor_scalar(d_dt[j], ps[:, j, 0:SK], d_bb[:, bass.ds(g, 1)], 0.0, ALU.add,
                                        ALU.max).then_inc(S["d_clip"], 1)
            clip(0, 0)
            clip(1, 1)
            with dve.Fori(1, TT // 2) as i:
                for j in range(2):
                    clip(2 * i + j, j)
            R = d_R[0:B]
            ch.link(nc.vector.memset(R[:, 0, :], BIG))
            ch.link(nc.vector.memset(R[:, 0, 0:1], 0.0))
            ch.link(nc.vector.memset(R[:, 1:L + 1, 0:1], BIG))
            dve.wait_ge(S["d_back"], 16)
            with dve.Fori(0, L) as j:
                prev = R[:, bass.ds(j, 1), :].rearrange("p a i -> p (a i)")
                cur = R[:, bass.ds(j + 1, 1), :].rearrange("p a i -> p (a i)")
                nc.vector.tensor_tensor(d_min[0:B], prev[:, 1:IP], prev[:, 0:SK], ALU.min).then_inc(S["d_fwd"], 1)
                dve.wait_ge(S["d_fwd"], 2 * j + 1)
                nc.vector.tensor_tensor_scan(cur[:, 1:IP], d_min[0:B],
                                             d_D[0:B, bass.ds(j, 1), :].rearrange("p a i -> p (a i)"), BIG,
                                             ALU.min, ALU.add).then_inc(S["d_fwd"], 1)
                dve.wait_ge(S["d_fwd"], 2 * j + 2)
            cd, cu, cl = R[:, 0:L, 0:SK], R[:, 1:L + 1, 0:SK], R[:, 0:L, 1:IP]
            t = d_t[0:B]
            dg, lf, up = d_diag[0:B], d_left[0:B], d_up[0:B]
            ch.link(nc.vector.tensor_tensor(t, cd, cu, ALU.min))
            nc.vector.tensor_tensor(lf[:, :, IP - 1:0:-1], cl, t, ALU.is_lt).then_inc(S["d_choice"], 1)
            dve.wait_ge(S["d_choice"], 1)
            ch.link(nc.vector.tensor_tensor(t, cl, cu, ALU.min))
            nc.vector.tensor_tensor(dg[:, :, IP - 1:0:-1], cd, t, ALU.is_le).then_inc(S["d_choice"], 1)
            dve.wait_ge(S["d_choice"], 2)
            ch.link(nc.vector.memset(up[:, :, 0:1], 0.0))
            nc.vector.scalar_tensor_tensor(out=up[:, :, 1:IP], in0=lf[:, :, 1:IP], scalar=0.0, in1=dg[:, :, 1:IP],
                                           op0=ALU.is_equal, op1=ALU.is_gt).then_inc(S["d_choice"], 1)
            E_, VD = d_E[0:B], d_VD[0:B]
            ch.link(nc.vector.memset(E_, 0.0))
            ch.link(nc.vector.memset(E_[:, 0:1], 1.0))
            dve.wait_ge(S["d_choice"], 3)
            with dve.Fori(0, L) as n:
                j = (L - 1) - n

                def col(x):
                    return x[:, bass.ds(j, 1), :].rearrange("p a i -> p (a i)")
                v = col(d_V[0:B])
                nc.vector.tensor_tensor_scan(v[:, 0:SK], col(up)[:, 0:SK], E_[:, 0:SK], 0.0,
                                             ALU.mult, ALU.add).then_inc(S["d_v"], 1)
                dve.wait_ge(S["d_v"], n + 1)
                nc.vector.tensor_tensor(E_[:, 0:SK], v[:, 0:SK], col(lf)[:, 1:IP], ALU.mult).then_inc(S["d_bw"], 1)
                nc.vector.tensor_tensor(VD[:, 0:SK], v[:, 0:SK], col(dg)[:, 1:IP], ALU.mult).then_inc(S["d_bw"], 1)
                dve.wait_ge(S["d_bw"], 3 * n + 2)
                nc.vector.tensor_tensor(E_[:, 1:SK], E_[:, 1:SK], VD[:, 0:SK - 1], ALU.add).then_inc(S["d_bw"], 1)
                dve.wait_ge(S["d_bw"], 3 * n + 3)

            def add(b, j):
                dve.wait_ge(S["d_exp"], b + 1)
                dst = xT[:, :, bass.ds(b * L, L)]
                nc.vector.tensor_tensor(dst, dst, ps[:, 4 + j, 0:DC * L].rearrange("p (c j) -> p c j", c=DC),
                                        ALU.add).then_inc(S["d_add"], 1)
            with dve.Fori(0, B // 2) as i:
                for j in range(2):
                    add(2 * i + j, j)
            dve.wait_ge(S["d_add"], B)

        def d_pool(pool):
            def slot(g, j):
                if not isinstance(g, int) or g >= 2:
                    pool.wait_ge(S["d_ab"], 4 * g - 4)
                nc.gpsimd.tensor_copy(d_xs[j], d_m2[:, :, bass.ds(g * P, P)]).then_inc(S["d_xs"], 1)
            pool.wait_ge(S["d_m2"], 1)
            slot(0, 0)
            slot(1, 1)
            with pool.Fori(1, TT // 2) as i:
                for j in range(2):
                    slot(2 * i + j, j)

        t_raw = [U[2], U[3], U[4]]
        t_g = U[5]
        t_x = [U[6], U[7], U[8]]
        t_sq = [U[9], U[10]]
        t_v = view(22 * K, TT, D)
        t_o = view(24 * K, TT, D)
        t_osq = view(18 * K, TT, D)
        t_qm = [view(26 * K + 2048 * j, DC, HPC, P) for j in range(2)]
        t_S = [view(30 * K + 2048 * j, XH, P) for j in range(2)]
        t_w = [view(34 * K + 512 * n, DC, D) for n in range(5)]
        t_W0 = view(37 * K, DC, P)
        t_tril = view(37 * K + 256, P)
        t_cw = view(37 * K + 384, 3, DC, KW)
        t_gam, t_bet = view(37 * K + 512, DK), view(37 * K + 528, DK)
        t_st = view(37 * K + 544, 2, TT * XH)

        def t_load(sp):
            sp.wait_ge(*S.at("tn_in", 1))
            load(sp, "ld_t", *((t_w[n], A["L1_attn_W" + x]) for n, x in enumerate("qkvgo")), (t_cw, A["L1_attn_conv"]),
                 (t_W0, A["L1_attn_W_init"]), (t_tril, A["c_tril"]),
                 (t_gam, A["L1_attn_ln_gamma"]), (t_bet, A["L1_attn_ln_beta"]))

        def t_pe(pe):
            norm_pe(pe, "tn", xT, U[2])
            pe.wait_ge(*S.at("tn_out", 2))
            pe.wait_ge(S["ld_t"], dma_n["ld_t"])
            dense_pe(pe, "tp", [(P, [(t_w[n][:, k, m * P:(m + 1) * P], half(U[1], k, h)) for k in range(DC)])
                                for n in range(4) for m in range(DC) for h in range(NH)], "a" * 16, list(range(8)))
            pe.wait_ge(*S.at("tp_ev_a", 16))
            for g in range(8):
                pe.wait_ge(S["t_sq"], g // 2 + 1)
                nc.tensor.matmul(ps[:, g, :], grp, half(t_sq[g // 4], (g // 2) % 2, g % 2),
                                 start=True, stop=True).then_inc(S["t_ss"], 1)
            pe.wait_ge(S["t_nrm"], 8)
            pe.wait_ge(S["t_silu"], 6)
            for t in range(TT):
                for c in range(DC):
                    o = (t % 2) * D + c * P
                    mm = nc.tensor.transpose(ps[:, t // 2, o:o + P], t_x[2][:, c, t * P:(t + 1) * P], ident)
                if t % 2:
                    mm.then_inc(S["t_vT"], 1)
            pe.wait_ge(S["t_vev"], 4)
            pe.wait_ge(S["t_qk"], 8)

            def sc(t):
                for b in range(4):
                    if t:
                        pe.wait_ge(S["t_mask"], 4 * (t - 1) + b + 1)
                    pe.wait_ge(S["t_qm"], 2 * t + b // 2 + 1)
                    nc.tensor.matmul(ps[:, b, :], t_x[1][:, b // 2, t * P:(t + 1) * P],
                                     t_qm[t % 2][:, b // 2, 4 * (b % 2):4 * (b % 2) + 4, :].rearrange("p h q -> p (h q)"),
                                     start=True, stop=True).then_inc(S["t_s"], 1)

            sc(0)
            for t in range(TT):
                if t + 1 < TT:
                    sc(t + 1)
                if t >= 2:
                    pe.wait_ge(S["t_oev"], t - 1)
                for c in range(DC):
                    nc.tensor.matmul(ps[:, 4 + t % 2, c * P:(c + 1) * P], t_x[0][:, c, t * P:(t + 1) * P],
                                     t_W0[:, c, :], start=True, stop=False, skip_group_check=True)
                    for hd in range(HPC * c, HPC * (c + 1)):
                        if hd % 4 == 0:
                            pe.wait_ge(S["t_mask"], 4 * t + hd // 4 + 1)
                        mm = nc.tensor.matmul(ps[:, 4 + t % 2, hd * DK:(hd + 1) * DK], t_S[t % 2][:, hd, :],
                                              t_v[:, t, hd * DK:(hd + 1) * DK], start=False,
                                              stop=True, skip_group_check=True)
                mm.then_inc(S["t_om"], 1)
            pe.wait_ge(S["t_ln"], 1)
            for t in range(TT):
                for c in range(DC):
                    mm = nc.tensor.transpose(ps[:, 2 * c + t // 4, (t % 4) * P:(t % 4 + 1) * P],
                                             t_o[:, t, c * P:(c + 1) * P], ident)
            mm.then_inc(S["t_oT"], 1)
            pe.wait_ge(S["t_gate"], 4)
            dense_pe(pe, "to", [(P, [(t_w[4][:, k, m * P:(m + 1) * P], half(t_x[0], k, h)) for k in range(DC)])
                                for m in range(DC) for h in range(NH)], "dddd", [4, 5, 6, 7])

        def t_act(act):
            norm_act(act, "tn", U[1], U[2], U[3][:, 0, :], 0)
            for g in range(16):
                n, m, h = g // 4, (g // 2) % 2, g % 2
                act.wait_ge(*S.at("tp_mm", g + 1))
                dst = (t_raw + [t_g])[n]
                nc.scalar.copy(half(dst, m, h), ps[:, g % 8, :]).then_inc(S["tp_ev_a"], 1)
            for n in range(6):
                act.wait_ge(S["t_conv"], n + 1)
                x = t_x[n // 2][:, n % 2, :]
                nc.scalar.activation(x, x, ACT.Silu).then_inc(S["t_silu"], 1)
            for n in range(4):
                act.wait_ge(S["t_silu"], n + 1)
                nc.scalar.activation(t_sq[n // 2][:, n % 2, :], t_x[n // 2][:, n % 2, :],
                                     ACT.Square).then_inc(S["t_sq"], 1)
            for g in range(8):
                act.wait_ge(S["t_ss"], g + 1)
                nc.scalar.activation(half(t_sq[g // 4], (g // 2) % 2, g % 2), ps[:, g, :], ACT.Sqrt,
                                     bias=eps[:, 3:4]).then_inc(S["t_nrm"], 1)
            for n in range(4):
                act.wait_ge(S["t_vT"], n + 1)
                nc.scalar.copy(t_v[:, 2 * n:2 * n + 2, :].rearrange("p a b -> p (a b)"), ps[:, n, :])\
                    .then_inc(S["t_vev"], 1)
            for t in range(TT):
                act.wait_ge(S["t_om"], t + 1)
                nc.scalar.copy(t_o[:, t, :], ps[:, 4 + t % 2, 0:D]).then_inc(S["t_oev"], 1)
            act.wait_ge(S["t_cen"], 1)
            nc.scalar.activation(t_osq, t_o, ACT.Square).then_inc(S["t_osq"], 1)
            act.wait_ge(S["t_var"], 1)
            nc.scalar.activation(t_st[:, 1, :], t_st[:, 0, :], ACT.Sqrt, bias=eps[:, 0:1],
                                 scale=1.0 / DK).then_inc(S["t_sd"], 1)

        def t_dve(ch):
            dve, ln = ch.eng, ch.link
            v = nc.vector
            norm_dve(ch, "tn", xT, U[1], U[3][:, 0, :], U[1])
            dve.wait_ge(S["ld_t"], dma_n["ld_t"])
            for n in range(6):
                w, c = n // 2, n % 2
                dve.wait_ge(*S.at("tp_ev_a", 2 * n + 2))
                x, y = t_raw[w][:, c, :], t_x[w][:, c, :]
                x3, y3 = (z.rearrange("p (b t) -> p b t", t=L) for z in (x, y))
                ln(v.scalar_tensor_tensor(out=y, in0=x, scalar=t_cw[:, w, c, KW - 1:KW], in1=x,
                                          op0=ALU.mult, op1=ALU.add))
                for s in range(1, KW):
                    ins = v.scalar_tensor_tensor(out=y3[:, :, s:], in0=x3[:, :, :L - s],
                                                 scalar=t_cw[:, w, c, KW - 1 - s:KW - s], in1=y3[:, :, s:],
                                                 op0=ALU.mult, op1=ALU.add)
                    if s < KW - 1:
                        ln(ins)
                ins.then_inc(S["t_conv"], 1)
            for g in range(8):
                x, r = (half(z[g // 4], (g // 2) % 2, g % 2) for z in (t_x, t_sq))
                dve.wait_ge(S["t_nrm"], g + 1)
                ln(v.reciprocal(r, r))
                v.tensor_tensor(x, x, r, ALU.mult).then_inc(S["t_qk"], 1)
            for t in range(TT):
                if t >= 2:
                    dve.wait_ge(S["t_om"], t - 1)
                for b in range(4):
                    dve.wait_ge(S["t_s"], 4 * t + b + 1)
                    v.tensor_tensor(t_S[t % 2][:, 4 * b:4 * b + 4, :],
                                    ps[:, b, :].rearrange("p (h q) -> p h q", h=4),
                                    t_tril.unsqueeze(1).broadcast_to([P, 4, P]), ALU.mult).then_inc(S["t_mask"], 1)
            dve.wait_ge(S["t_oev"], TT)
            o4 = t_o.rearrange("p t (h d) -> p (t h) d", d=DK)
            q4 = t_osq.rearrange("p t (h d) -> p (t h) d", d=DK)
            G = TT * XH

            def wide(s):
                return s.unsqueeze(2).broadcast_to([P, G, DK])
            ln(v.tensor_reduce(t_st[:, 0, :], o4, AX.X, ALU.add))
            ln(v.tensor_scalar(t_st[:, 1, :], t_st[:, 0, :], 1.0 / DK, None, ALU.mult))
            v.tensor_tensor(o4, o4, wide(t_st[:, 1, :]), ALU.subtract).then_inc(S["t_cen"], 1)
            dve.wait_ge(S["t_osq"], 1)
            v.tensor_reduce(t_st[:, 0, :], q4, AX.X, ALU.add).then_inc(S["t_var"], 1)
            dve.wait_ge(S["t_sd"], 1)
            ln(v.reciprocal(t_st[:, 0, :], t_st[:, 1, :]))
            ln(v.tensor_tensor(o4, o4, wide(t_st[:, 0, :]), ALU.mult))
            ln(v.tensor_tensor(o4, o4, t_gam.unsqueeze(1).broadcast_to([P, G, DK]), ALU.mult))
            v.tensor_tensor(o4, o4, t_bet.unsqueeze(1).broadcast_to([P, G, DK]), ALU.add).then_inc(S["t_ln"], 1)
            dve.wait_ge(S["t_oT"], 1)
            for g in range(4):
                v.tensor_tensor(half(t_x[0], g // 2, g % 2), ps[:, g, :], half(t_g, g // 2, g % 2),
                                ALU.mult).then_inc(S["t_gate"], 1)
            for g in range(4):
                dve.wait_ge(*S.at("to_mm", g + 1))
                ln(v.tensor_tensor(half(xT, g // 2, g % 2), half(xT, g // 2, g % 2), ps[:, 4 + g, :], ALU.add))

        def t_pool(pool):
            pool.wait_ge(S["t_qk"], 4)
            for t in range(TT):
                for c in range(DC):
                    if t >= 2:
                        pool.wait_ge(S["t_s"], 4 * (t - 2) + 2 * c + 2)
                    nc.gpsimd.tensor_tensor(t_qm[t % 2][:, c],
                                            t_x[0][:, c, t * P:(t + 1) * P].unsqueeze(1).broadcast_to([P, HPC, P]),
                                            hmask.unsqueeze(2).broadcast_to([P, HPC, P]),
                                            ALU.mult).then_inc(S["t_qm"], 1)

        FC = FH // P
        g_w1 = [view(21 * K + 1024 * j, DC, FH) for j in range(2)]
        g_w2 = [view(23 * K + 1024 * j, FC, D) for j in range(2)]
        g_b1 = [view(25 * K + 16 * j, FC) for j in range(2)]
        g_b2 = view(25 * K + 64, D)
        g_sa = view(26 * K, 2, HALF)
        g_h = [view(27 * K + 2048 * j, FC, HALF) for j in range(2)]

        def g_load(sp):
            sp.wait_ge(*S.at("gn_in", 1))
            load(sp, "ld_g", (f_R["w"], A["L1_ffn_gate_w"]), (f_R["b"], A["L1_ffn_gate_b"]), (g_b2[0:E], A["L1_ffn_b2"]))

            def expert(e, j):
                for dst, src in ((g_w1[j], "w1"), (g_w2[j], "w2"), (g_b1[j].unsqueeze(1), "b1")):
                    sp.dma_start(dst, A["L1_ffn_" + src][:, bass.ds(e, 1)].rearrange("p a k f -> p (a k) f"))\
                        .then_inc(S[f"ge_wt{j}"], 16)
            expert(0, 0)
            expert(1, 1)
            with sp.Fori(1, E // 2) as i:
                for j in range(2):
                    sp.wait_ge(S["ge_w2"], 4 * i + 2 * j - 2)
                    expert(2 * i + j, j)

        def g_pe(pe):
            norm_pe(pe, "gn", xT, U[2])
            pe.wait_ge(*S.at("gn_out", 2))
            pe.wait_ge(S["ld_g"], dma_n["ld_g"])
            route_pe(pe, "gr", f_R, U[1])

            def up(v, h, j, e):
                for f in range(FC):
                    r = 4 * v + f
                    if not isinstance(v, int) or r >= 2:
                        pe.wait_ge(S["ge_sa"], r - 1)
                    for k in range(DC):
                        mm = nc.tensor.matmul(ps[:, 4 + f % 2, :], g_w1[j][:, k, f * P:(f + 1) * P],
                                              half(U[1], k, h), start=(k == 0), stop=(k == 1))
                    mm.then_inc(S["ge_a"], 1)
                    if f == 0:
                        if not isinstance(v, int) or v >= 2:
                            pe.wait_ge(S["ge_h"], 4 * v - 4)
                        weight_pe(f_R, e, h).then_inc(S["ge_c"], 1)

            def down(v, h, j, stop):
                pe.wait_ge(S["ge_h"], 4 * v + 4)
                for m in range(DC):
                    for f in range(FC):
                        mm = nc.tensor.matmul(ps[:, 2 * m + h, :], g_w2[j][:, f, m * P:(m + 1) * P], g_h[h][:, f, :],
                                              start=False, stop=stop and f == FC - 1, skip_group_check=True)
                mm.then_inc(S["ge_w2"], 1)

            pe.wait_ge(S["gr_part"], 1)
            for m in range(DC):
                for h in range(NH):
                    nc.tensor.matmul(ps[:, 2 * m + h, :], g_b2[0:E, m * P:(m + 1) * P],
                                     f_R["cT"][0:E, h * HALF:(h + 1) * HALF], start=True, stop=False,
                                     skip_group_check=True)

            def expert_pair(i, first_pair):
                for j in range(2):
                    v = 4 * i + 2 * j
                    pe.wait_ge(S[f"ge_wt{j}"], 48 * i + 48)
                    up(v, 0, j, 2 * i + j)
                    if not (first_pair and j == 0):
                        down(v - 1, 1, 1 - j, False)
                    up(v + 1, 1, j, 2 * i + j)
                    down(v, 0, j, False)
            expert_pair(0, True)
            with pe.Fori(1, E // 2) as i:
                expert_pair(i, False)
            down(2 * E - 1, 1, 1, True)

        def g_act(act):
            norm_act(act, "gn", U[1], U[2], U[3][:, 0, :], 0)
            route_act(act, "gr", f_R, False)

            def relu(r, f, j):
                act.wait_ge(S["ge_a"], r + 1)
                if not isinstance(r, int) or r >= 2:
                    act.wait_ge(S["ge_h"], r - 1)
                nc.scalar.activation(g_sa[:, f % 2, :], ps[:, 4 + f % 2, :], ACT.Relu,
                                     bias=g_b1[j][:, f:f + 1]).then_inc(S["ge_sa"], 1)

            def pair(i):
                for j in range(2):
                    act.wait_ge(S[f"ge_wt{j}"], 48 * i + 48)
                    for n in range(2 * FC):
                        relu(16 * i + 8 * j + n, n % FC, j)
            pair(0)
            with act.Fori(1, E // 2) as i:
                pair(i)

        def g_dve(ch):
            dve = ch.eng
            norm_dve(ch, "gn", xT, U[1], U[3][:, 0, :], U[1])
            dve.wait_ge(S["ld_g"], dma_n["ld_g"])
            route_dve(ch, "gr", f_R, False)
            route_parts(ch, "gr", f_R)

            def product(v, h):
                dve.wait_ge(S["ge_c"], v + 1)
                if not isinstance(v, int) or v >= 2:
                    dve.wait_ge(S["ge_w2"], v - 1)
                for f in range(FC):
                    dve.wait_ge(S["ge_sa"], 4 * v + f + 1)
                    nc.vector.tensor_tensor(g_h[h][:, f, :], g_sa[:, f % 2, :], ps[:, 6 + h, :],
                                            ALU.mult).then_inc(S["ge_h"], 1)
            product(0, 0)
            product(1, 1)
            with dve.Fori(1, E) as i:
                for h in range(NH):
                    product(2 * i + h, h)
            dve.wait_ge(S["ge_w2"], 2 * E)
            for g in range(4):
                ch.link(nc.vector.tensor_tensor(half(xT, g // 2, g % 2), half(xT, g // 2, g % 2),
                                                ps[:, g, :], ALU.add))

        def g_pool(pool):
            route_pool(pool, "gr", f_R, "gn_in")


        stages = {0: (x_loads, x_pe, x_act, x_dve, x_pool)}
        stages[1] = (m_load, m_pe, m_act, m_dve, m_pool)
        stages[2] = (f_load, f_pe, f_act, f_dve, f_pool)
        stages[3] = (d_load, d_pe, d_act, d_dve, d_pool)
        stages[4] = (t_load, t_pe, t_act, t_dve, t_pool)
        stages[5] = (g_load, g_pe, g_act, g_dve, g_pool)
        block = ctx.enter_context(nc.Block())

        @block.sync
        def _(sp):
            x_load(sp)
            for s in range(first, last + 1):
                stages[s][0](sp)
            sp.wait_ge(S["all_done"], 1)
            sp.dma_start(out, xT).then_inc(S["stored"], 16)
            sp.wait_ge(S["stored"], 16)

        @block.vector
        def _(dve):
            ch = Chain(dve, S["dve_own"])
            dve.wait_ge(S["ld_const"], dma_n["ld_const"])
            ch.link(nc.vector.tensor_copy(identb, ident))
            for s in range(first, last + 1):
                signal(("xn", "mn", "fn", "dn", "tn", "gn")[s] + "_in")
                stages[s][3](ch)
            signal("all_done")

        @block.scalar
        def _(act):
            for s in range(first, last + 1):
                stages[s][2](act)

        @block.gpsimd
        def _(pool):
            for s in range(first, last + 1):
                stages[s][4](pool)

        @block.tensor
        def _(pe):
            for s in range(first, last + 1):
                stages[s][1](pe)


def feat(w):
    w = np.asarray(w)
    return np.ascontiguousarray(w.T.reshape(w.shape[1] // P, P, w.shape[0]).transpose(1, 0, 2))


def cols(v):
    v = np.asarray(v)
    return np.ascontiguousarray(v.reshape(-1, P).T)


def constants():
    def split(v):
        parts = []
        for _ in range(3):
            parts.append((v.view(np.uint32) & np.uint32(0xFFFF0000)).view(np.float32))
            v = v - parts[-1]
        return parts

    p = np.arange(P)
    c = {
        "c_ident": np.eye(P, dtype=np.float32),
        "c_mean": np.full((P, P), 1.0 / D, np.float32),
        "c_hmask": (p[:, None] // DK == np.arange(HPC)[None]).astype(np.float32),
        "c_ones": np.ones((P, 32), np.float32),
        "c_grp": (p[:, None] // DK == p[None] // DK).astype(np.float32),
        "c_eps": np.tile(np.array([1e-5, np.finfo(np.float32).eps, 1e-6, 1e-12], np.float32), (P, 1)),
        "c_iota8": np.tile(np.arange(E, dtype=np.float32), (P, 1)),
    }
    slopes = np.array([2.0 ** (-8.0 * (i + 1) / XH) for i in range(XH)], np.float32)
    sl = np.repeat(slopes.reshape(4, 4), L, axis=1)
    qs = -(sl * np.tile(np.arange(L, dtype=np.float32), 4)[None])
    c["c_slope"] = np.ascontiguousarray(np.stack(split(sl) + split(qs)))
    pos = np.arange(SK, dtype=np.float32)
    c["c_pos"] = np.stack([pos] * 3 + [np.ones_like(pos)] * 3)
    hq = np.repeat(np.arange(HPC), L)
    c["c_dmask"] = np.tile((p[:, None] // DK == hq[None]).astype(np.float32), (1, DC))
    tok = p // L
    c["c_neg"] = np.where(tok[:, None] == tok[None], 0.0, -BIG).astype(np.float32)
    c["c_tril"] = ((tok[:, None] == tok[None]) & (p[:, None] <= p[None])).astype(np.float32)
    return c


def layout(inputs):
    a = {}
    a["x"] = feat(np.asarray(inputs["x"]).reshape(T, D))
    ctx = np.asarray(inputs["ctx_1024"])
    a["ctxT"] = feat(ctx.reshape(B * SK, D))
    for n in ("w_q", "w_k", "w_v", "w_o"):
        a["L0_xattn_" + n] = feat(inputs["L0_xattn_" + n])
    a["L0_xattn_b_o"] = cols(inputs["L0_xattn_b_o"])
    pre = "L0_attn_"
    a[pre + "norm_w"] = cols(inputs[pre + "norm_w"])
    for n in ("W_in", "W_x", "W_out"):
        a[pre + n] = feat(inputs[pre + n])
    a[pre + "W_dt"] = np.ascontiguousarray(np.asarray(inputs[pre + "W_dt"]).T)
    for n in ("conv_b", "Dp", "b_dt"):
        a[pre + n] = cols(inputs[pre + n])
    a[pre + "conv_w"] = np.ascontiguousarray(np.asarray(inputs[pre + "conv_w"]).reshape(IC, P, KW).transpose(1, 0, 2))
    a[pre + "A_log"] = np.ascontiguousarray(np.asarray(inputs[pre + "A_log"]).reshape(IC, P, NS).transpose(1, 0, 2))
    pre = "L0_ffn_"
    a[pre + "Wq"], a[pre + "Wo"] = feat(inputs[pre + "Wq"]), feat(inputs[pre + "Wo"])
    k, v = feat(inputs[pre + "Wkc"]), feat(inputs[pre + "Wvc"])
    a[pre + "Wkv"] = np.concatenate([k, k, v, v], axis=2)
    a[pre + "g1"], a[pre + "g2"] = cols(inputs[pre + "g1"]), cols(inputs[pre + "g2"])
    a[pre + "Wr"] = feat(inputs[pre + "Wr"])
    a[pre + "expert_bias"] = np.ascontiguousarray(np.broadcast_to(np.asarray(inputs[pre + "expert_bias"]), (P, E)))
    a[pre + "sW13"] = np.concatenate([feat(inputs[pre + "sW1"]), feat(inputs[pre + "sW3"])], axis=2)
    a[pre + "sW2"] = feat(inputs[pre + "sW2"])
    a[pre + "eW13"] = np.stack([np.concatenate([feat(w1), feat(w3)], axis=2) for w1, w3 in
                                zip(np.asarray(inputs[pre + "eW1"]), np.asarray(inputs[pre + "eW3"]))], axis=1)
    a[pre + "eW2"] = np.stack([feat(w) for w in np.asarray(inputs[pre + "eW2"])], axis=1)
    back = ctx[:, ::-1]
    a["ctx_rows"] = np.ascontiguousarray(back[:, :2 * P].reshape(B, 2, P, D).transpose(2, 0, 1, 3))
    a["ctx_last"] = np.ascontiguousarray(back[:, 2 * P][None])
    pre = "L1_attn_"
    for x in "qkvgo":
        a[pre + "W" + x] = feat(inputs[pre + "W" + x])
    a[pre + "conv"] = np.stack([np.asarray(inputs[pre + "conv_" + x]).reshape(DC, P, KW).transpose(1, 0, 2)
                                for x in "qkv"], axis=1)
    w0 = np.zeros((P, DC, P), np.float32)
    for h in range(XH):
        r = DK * (h % HPC)
        w0[r:r + DK, h // HPC, r:r + DK] = np.asarray(inputs[pre + "W_init"])[0, h]
    a[pre + "W_init"] = w0
    for n in ("ln_gamma", "ln_beta"):
        a[pre + n] = np.ascontiguousarray(np.broadcast_to(np.asarray(inputs[pre + n]), (P, DK)))
    pre = "L1_ffn_"
    a[pre + "gate_w"] = feat(np.asarray(inputs[pre + "gate_w"]).T)
    a[pre + "gate_b"] = np.ascontiguousarray(np.broadcast_to(np.asarray(inputs[pre + "gate_b"]), (P, E)))
    a[pre + "w1"] = np.stack([feat(w.T) for w in np.asarray(inputs[pre + "w1"])], axis=1)
    a[pre + "w2"] = np.stack([feat(w.T) for w in np.asarray(inputs[pre + "w2"])], axis=1)
    a[pre + "b1"] = np.ascontiguousarray(np.asarray(inputs[pre + "b1"]).reshape(E, 1, FH // P, P).transpose(3, 0, 1, 2))
    a[pre + "b2"] = np.ascontiguousarray(np.asarray(inputs[pre + "b2"]))
    return a


def kernel(**inputs):
    import concourse.bacc as _bacc
    from concourse.bass_utils import run_bass_kernel_spmd as _run

    nc = _bacc.Bacc("TRN2", target_bir_lowering=False, num_devices=1)
    arrays = {**layout(inputs), **constants()}
    aps = {n: nc.dram_tensor(n, a.shape, mybir.dt.from_np(a.dtype), kind="ExternalInput").ap()
           for n, a in arrays.items()}
    out = nc.dram_tensor("out", (P, DC, T), F32, kind="ExternalOutput").ap()
    build(nc, aps, out)
    r = _run(nc, [arrays], core_ids=[0])
    got = np.asarray(r.results[0]["out"])
    return np.ascontiguousarray(got.transpose(2, 1, 0).reshape(B, L, D))
```

```python
from contextlib import ExitStack

import concourse.bass as bass
import numpy as np
from concourse import mybir

ALU = mybir.AluOpType
ACT = mybir.ActivationFunctionType
AX = mybir.AxisListType
F32 = mybir.dt.float32
BF16 = mybir.dt.bfloat16
U32 = mybir.dt.uint32

P = 128
B = 32
L = 32
T = B * L
D = 256
DC = D // P
HALF = 512
NH = T // HALF
TT = T // P
SK = 257
XH = 16
DK = D // XH
HPC = P // DK
DI = 512
IC = DI // P
NS = 64
KW = 4
E = 8
FH = 512
BIG = 1e30


NORMS = [(0, "xn", 2), (1, "mn", 2), (1, "mr", 0), (2, "fn", 2), (2, "fr", 0), (2, "f2", 0), (3, "dn", 2),
         (4, "tn", 2), (5, "gn", 2)]
DENSE = [(0, "xq", 4, 0, 4), (0, "xw", 4, 0, 0), (1, "mi", 8, 0, 8), (1, "mc", 8, 8, 0),
         (1, "mx", 4, 4, 0), (1, "md", 8, 8, 0), (1, "mz", 8, 8, 0),
         (1, "mo", 4, 0, 0), (2, "fq", 6, 0, 6), (2, "fw", 4, 0, 0), (4, "tp", 16, 16, 0), (4, "to", 4, 0, 0)]


SHARED = ([(0, f"slot_ctx{j}", f"x_ctx{j}", 16 * (B // 2)) for j in range(2)]
         + [(0, f"slot_row{j}", f"x_v2{j}", 16 * (B // 2)) for j in range(2)]
         + [(0, "tile_qblk", "x_qblk", DC * B), (0, "tile_norm", "x_norm", B), (0, "tile_rec", "x_rec", B)]
         + [(2, f"slot_wt{j}", f"fe_wt{j}", 32 * (E // 2 + j)) for j in range(2)]
         + [(3, f"slot_ctx{j}", f"d_ctx{j}", 16 * (TT // 2)) for j in range(2)]
         + [(3, f"slot_row{j}", f"d_out{j}", 16 * (TT // 2)) for j in range(2)]
         + [(3, "tile_qblk", "d_ms", TT), (3, "tile_norm", "d_tm", TT), (3, "tile_rec", "d_add", TT)]
         + [(5, f"slot_wt{j}", f"ge_wt{j}", 48 * (E // 2)) for j in range(2)])


class Sems:

    def __init__(self, nc, ctx, first):
        self.nc, self.ctx, self.made, self.base = nc, ctx, {}, {}
        self.count = {}
        for stage, n, means in NORMS:
            if stage >= first:
                for kind, events in (("in", 1), ("mean", means), ("xc", means), ("sq", NH), ("var", NH), ("sd", NH), ("rec", NH), ("bc", NH),
                                     ("out", NH if means else NH * DC)):
                    self.add(f"{n}_{kind}", f"norm_{kind}", events)
        for stage, n, groups, a, d in DENSE:
            if stage >= first:
                for kind, events in (("mm", groups), ("ev_a", a), ("ev_d", d)):
                    self.add(f"{n}_{kind}", f"dense_{kind}", events)
        for stage, shared, n, events in SHARED:
            if stage >= first:
                self.add(n, shared, events)

    def add(self, name, shared, events):
        total = self.count.get(shared, 0)
        self.base[name] = (shared, total)
        self.count[shared] = total + events

    def __getitem__(self, name):
        name = self.base.get(name, (name, 0))[0]
        if name not in self.made:
            self.made[name] = self.ctx.enter_context(self.nc.semaphore(name))
        return self.made[name]

    def at(self, name, n):
        return self[name], self.base.get(name, (name, 0))[1] + n


class Chain:

    def __init__(self, eng, sem):
        self.eng, self.sem, self.n = eng, sem, 0

    def link(self, ins):
        self.n += 1
        ins.then_inc(self.sem, 1)
        self.eng.wait_ge(self.sem, self.n)

    def step(self, ins):
        self.n += 1
        ins.then_inc(self.sem, 1)

    def sync(self):
        self.eng.wait_ge(self.sem, self.n)


def build(nc, A, out, first=0, last=5):
    ctx = ExitStack()
    with ctx:
        S = Sems(nc, ctx, first)
        ar = ctx.enter_context(nc.sbuf_tensor("arena", [P, 51 * 1024], F32))
        ps = ctx.enter_context(nc.psum_tensor("ps", [P, 8, HALF], F32))

        vlast = nc.dram_tensor("vlast", (B, D), F32, kind="Internal").ap()
        dist = nc.dram_tensor("dist", (TT, P, SK), F32, kind="Internal").ap()

        def view(off, *shape):
            n = int(np.prod(shape))
            v = ar[:, off:off + n]
            if len(shape) == 1:
                return v
            names = "abcd"[:len(shape)]
            return v.rearrange(f"p ({' '.join(names)}) -> p {' '.join(names)}", **dict(zip(names, shape)))

        def bview(off, *shape):
            n = int(np.prod(shape))
            v = ar[:, off:off + (n + 1) // 2].bitcast(BF16)
            if len(shape) == 1:
                return v
            names = "abcd"[:len(shape)]
            return v.rearrange(f"p ({' '.join(names)}) -> p {' '.join(names)}", **dict(zip(names, shape)))

        K = 1024
        xT = view(0, DC, T)
        CONST = 44 * K
        EXTRA = 46 * K + 64
        ident = view(CONST, P)
        mean_w = view(CONST + 128, P)
        hmask = view(CONST + 256, HPC)
        ones = view(CONST + 264, 32)
        eps = view(CONST + 424, 4)
        identb = bview(CONST + 428, P)
        iota8 = view(CONST + 492, E)
        U = [view(2 * K * n, DC, T) for n in range(23)]

        dma_n = {}

        def signal(name):
            nc.vector.memset(view(CONST + 500, 1), 0.0).then_inc(S[name], 1)

        def load(sp, name, *pairs, shared=None):
            if shared:
                S.add(name, shared, 16 * len(pairs))
            for dst, src in pairs:
                sp.dma_start(dst, src).then_inc(S[name], 16)
            dma_n[name] = 16 * len(pairs)

        def half(v, c, h):
            return v[:, c, h * HALF:(h + 1) * HALF]

        def dense_pe(pe, name, groups, owners, banks):
            nb = len(banks)
            for g, (rows, pairs) in enumerate(groups):
                if g >= nb:
                    o = owners[g - nb]
                    pe.wait_ge(*S.at(f"{name}_ev_{o}", owners[:g - nb + 1].count(o)))
                for k, (lhsT, rhs) in enumerate(pairs):
                    dst = ps[0:rows, banks[g % nb], 0:rhs.shape[-1]]
                    last_mm = nc.tensor.matmul(dst, lhsT, rhs, start=(k == 0), stop=(k == len(pairs) - 1))
                last_mm.then_inc(S[f"{name}_mm"], 1)

        n_sd = view(CONST + 2040, TT)
        n_r = view(CONST + 2032, TT)

        def norm_pe(pe, name, src, sq, rms=False):
            if not rms:
                pe.wait_ge(*S.at(f"{name}_in", 1))
                for h in range(NH):
                    for c in range(DC):
                        mm = nc.tensor.matmul(ps[:, h, :], mean_w, half(src, c, h), start=(c == 0), stop=(c == 1))
                    mm.then_inc(S[f"{name}_mean"], 1)
                pe.wait_ge(*S.at(f"{name}_xc", NH))
            for h in range(NH):
                pe.wait_ge(*S.at(f"{name}_sq", h + 1))
                for t in range(4 * h, 4 * h + 4):
                    for c in range(DC):
                        mm = nc.tensor.matmul(ps[:, h, t:t + 1], sq[:, c, t * P:(t + 1) * P], mean_w[:, 0:1],
                                              start=(c == 0), stop=(c == 1))
                mm.then_inc(S[f"{name}_var"], 1)
            for h in range(NH):
                pe.wait_ge(*S.at(f"{name}_rec", h + 1))
                for t in range(4 * h, 4 * h + 4):
                    mm = nc.tensor.transpose(ps[:, 2 + h, (t % 4) * P:(t % 4 + 1) * P],
                                             n_r[:, t:t + 1].broadcast_to([P, P]), ident)
                mm.then_inc(S[f"{name}_bc"], 1)

        def norm_act(act, name, src, sq, eps_n, rms=False):
            for h in range(NH):
                if rms:
                    act.wait_ge(*S.at(f"{name}_in", 1))
                else:
                    act.wait_ge(*S.at(f"{name}_xc", h + 1))
                nc.scalar.activation(sq[:, :, h * HALF:(h + 1) * HALF], src[:, :, h * HALF:(h + 1) * HALF],
                                     ACT.Square).then_inc(S[f"{name}_sq"], 1)
            for h in range(NH):
                act.wait_ge(*S.at(f"{name}_var", h + 1))
                nc.scalar.activation(n_sd[:, 4 * h:4 * h + 4], ps[:, h, 4 * h:4 * h + 4], ACT.Sqrt,
                                     bias=eps[:, eps_n:eps_n + 1]).then_inc(S[f"{name}_sd"], 1)

        def norm_dve(ch, name, src, xc, dst, rms=False, gain=None):
            dve = ch.eng
            if not rms:
                for h in range(NH):
                    dve.wait_ge(*S.at(f"{name}_mean", h + 1))
                    sl = slice(h * HALF, (h + 1) * HALF)
                    nc.vector.tensor_tensor(xc[:, :, sl], src[:, :, sl],
                                            ps[:, h:h + 1, :].broadcast_to([P, DC, HALF]),
                                            ALU.subtract).then_inc(S[f"{name}_xc"], 1)
                dve.wait_ge(*S.at(f"{name}_xc", NH))
            for h in range(NH):
                dve.wait_ge(*S.at(f"{name}_sd", h + 1))
                nc.vector.reciprocal(n_r[:, 4 * h:4 * h + 4], n_sd[:, 4 * h:4 * h + 4]).then_inc(S[f"{name}_rec"], 1)
            for h in range(NH):
                dve.wait_ge(*S.at(f"{name}_bc", h + 1))
                sl = slice(h * HALF, (h + 1) * HALF)
                if gain is None:
                    nc.vector.tensor_tensor(dst[:, :, sl], xc[:, :, sl],
                                            ps[:, 2 + h:3 + h, :].broadcast_to([P, DC, HALF]),
                                            ALU.mult).then_inc(S[f"{name}_out"], 1)
                else:
                    for c in range(DC):
                        nc.vector.scalar_tensor_tensor(out=dst[:, c, sl], in0=xc[:, c, sl],
                                                       scalar=gain[:, c:c + 1], in1=ps[:, 2 + h, :],
                                                       op0=ALU.mult, op1=ALU.mult).then_inc(S[f"{name}_out"], 1)
            dve.wait_ge(*S.at(f"{name}_out", NH if gain is None else NH * DC))

        x0 = dict(
            wq=view(20 * K, DC, D), wk=view(20 * K + 512, DC, D), wv=view(21 * K, DC, D), wo=view(21 * K + 512, DC, D),
            bo=view(22 * K, DC),
            slope=bview(22 * K + 16, 4, P), pos=bview(22 * K + 16 + 256, SK + 1),
            cl=view(37 * K, DC, B), vl=view(37 * K + 64, D),
            slope32=view(36 * K, 4, P), pos32=view(36 * K + 512, SK),
            dmask=view(22 * K + 512, HALF),
            ctx=[view(23 * K + 520 * j, DC, SK) for j in range(2)],
            kT=[view(25 * K + 520 * j, DC, SK) for j in range(2)],
            v=[view(27 * K + 512 * j, 2, D) for j in range(2)],
            v2=[view(28 * K + 256 * j, D) for j in range(2)],
            qb=[view(28 * K + 512 + 512 * j, HALF) for j in range(2)],
            p=[view(30 * K + 1040 * j, 4, SK) for j in range(2)],
            pT=view(33 * K, 2, HALF), pT2=view(34 * K, HALF),
            om=view(34 * K + 512, HALF),
            st=[view(35 * K + 16 * j, 3, 4) for j in range(2)],
        )
        Xn, Xq, Xo = U[1], U[2], U[3]

        def x_load(sp):
            load(sp, "ld_const", (ident, A["c_ident"]), (mean_w, A["c_mean"]), (hmask, A["c_hmask"]),
                 (ones, A["c_ones"]), (eps, A["c_eps"]),
                 (iota8, A["c_iota8"]), (xT, A["x"]))

        def x_loads(sp):
            load(sp, "ld_x", (x0["wq"], A["L0_xattn_w_q"]), (x0["wk"], A["L0_xattn_w_k"]),
                 (x0["wv"], A["L0_xattn_w_v"]), (x0["wo"], A["L0_xattn_w_o"]), (x0["bo"], A["L0_xattn_b_o"]), (x0["cl"], A["ctx_lastT"]),
                 (x0["slope32"][0:6], A["c_slope"]), (x0["pos32"][0:6], A["c_pos"]), (x0["dmask"], A["c_dmask"]), shared="loads")

            def ctx_load(b, j):
                sp.dma_start(x0["ctx"][j], A["ctxT"][:, :, bass.ds(b * SK, SK)]).then_inc(S[f"x_ctx{j}"], 16)

            def v2_load(b, j):
                sp.dma_start(x0["v2"][j][0:1], vlast[bass.ds(b, 1), :]).then_inc(S[f"x_v2{j}"], 16)
            for j in range(2):
                ctx_load(j, j)
            sp.wait_ge(S["x_vlast"], 1)
            sp.dma_start(vlast, x0["vl"][0:B]).then_inc(S["x_vkept"], 16)
            sp.wait_ge(S["x_vkept"], 16)
            for j in range(2):
                v2_load(j, j)
            with sp.Fori(1, B // 2) as i:
                for j in range(2):
                    sp.wait_ge(S["x_v"], 2 * i + j - 1)
                    ctx_load(2 * i + j, j)
                    sp.wait_ge(S["x_o"], 2 * i + j - 1)
                    v2_load(2 * i + j, j)

        def x_pe(pe):
            pe.wait_ge(S["ld_const"], dma_n["ld_const"])
            norm_pe(pe, "xn", xT, Xo)
            pe.wait_ge(*S.at("ld_x", dma_n["ld_x"]))
            pe.wait_ge(*S.at("xn_out", 2))
            dense_pe(pe, "xq", [(P, [(x0["wq"][:, k, m * P:(m + 1) * P], half(Xn, k, h)) for k in range(DC)])
                                for m in range(DC) for h in range(NH)], "dddd", [4, 5, 6, 7])
            pe.wait_ge(*S.at("xq_ev_d", 4))
            for k in range(DC):
                mm = nc.tensor.matmul(ps[0:B, 0, 0:D], x0["cl"][:, k, :], x0["wv"][:, k, :], start=(k == 0), stop=(k == 1))
            mm.then_inc(S["x_vl"], 1)

            def proj(b, j, i):
                if not isinstance(b, int) or b >= 1:
                    pe.wait_ge(S["x_vev"], b)
                    pe.wait_ge(S["x_kev"], b)
                cx = x0["ctx"][j]
                pe.wait_ge(*S.at(f"x_ctx{j}", 16 * (i + 1)))
                for m in range(DC):
                    for k in range(DC):
                        mm = nc.tensor.matmul(ps[:, 4 + m, 0:SK], x0["wk"][:, k, m * P:(m + 1) * P], cx[:, k, :],
                                              start=(k == 0), stop=(k == 1))
                mm.then_inc(S["x_k"], 1)
                for t in range(2):
                    for k in range(DC):
                        mm = nc.tensor.matmul(ps[:, 6, t * D:(t + 1) * D], cx[:, k, t * P:(t + 1) * P],
                                              x0["wv"][:, k, :], start=(k == 0), stop=(k == 1))
                mm.then_inc(S["x_v"], 1)

            def scores(b, j):
                pe.wait_ge(S["x_kev"], b + 1)
                pe.wait_ge(S["x_qblk"], 2 * b + 2)
                if not isinstance(b, int) or b >= 1:
                    pe.wait_ge(S["x_exp"], 4 * b)
                for g in range(4):
                    nc.tensor.matmul(ps[:, g, 0:SK], x0["qb"][j][:, g * P:(g + 1) * P], x0["kT"][j][:, g // 2, :],
                                     start=True, stop=False)
                    mm = nc.tensor.matmul(ps[:, g, 0:SK], x0["slope"][0:6, g, :], x0["pos"][0:6, 0:SK],
                                          start=False, stop=True)
                mm.then_inc(S["x_s"], 1)

            def tail(b, j, i, vev):
                pe.wait_ge(S["x_norm"], b + 1)
                pe.wait_ge(S["x_vev"], vev)
                for t in range(3):
                    rows = min(P, SK - t * P)
                    for g in range(4):
                        mm = nc.tensor.transpose(ps[0:rows, 4 + t, g * P:(g + 1) * P],
                                                 x0["p"][j][:, g, t * P:t * P + rows], ident)
                    mm.then_inc(S["x_pt"], 1)
                pe.wait_ge(*S.at(f"x_v2{j}", 16 * (i + 1)))
                pe.wait_ge(S["x_or"], b + 1)
                for t in range(3):
                    pe.wait_ge(S[f"x_pt{t}ev"], b + 1)
                    for c in range(DC):
                        sl = slice(c * 256, (c + 1) * 256)
                        if t < 2:
                            lhsT, rhs = x0["v"][j][:, t, c * P:(c + 1) * P], x0["pT"][:, t, sl]
                        else:
                            lhsT, rhs = x0["v2"][j][0:1, c * P:(c + 1) * P], x0["pT2"][0:1, sl]
                        mm = nc.tensor.matmul(ps[:, 7, sl], lhsT, rhs, start=(t == 0 and c == 0), stop=(t == 2),
                                              skip_group_check=True)
                mm.then_inc(S["x_o"], 1)

            proj(0, 0, 0)
            pe.wait_ge(S["x_alibi"], 2)
            scores(0, 0)
            with pe.Fori(0, B // 2 - 1) as i:
                b = 2 * i
                proj(b + 1, 1, i)
                scores(b + 1, 1)
                tail(b, 0, i, b + 2)
                proj(b + 2, 0, i + 1)
                scores(b + 2, 0)
                tail(b + 1, 1, i, b + 3)
            proj(B - 1, 1, B // 2 - 1)
            scores(B - 1, 1)
            tail(B - 2, 0, B // 2 - 1, B)
            tail(B - 1, 1, B // 2 - 1, B)
            pe.wait_ge(S["x_or"], B + 1)
            dense_pe(pe, "xw", [(P, [(x0["wo"][:, k, m * P:(m + 1) * P], half(Xo, k, h)) for k in range(DC)])
                                for m in range(DC) for h in range(NH)], "dddd", [0, 1, 2, 3])

        def x_act(act):
            act.wait_ge(S["ld_const"], dma_n["ld_const"])
            norm_act(act, "xn", Xn, Xo, 0)

            def keys(b, j):
                act.wait_ge(S["x_k"], b + 1)
                nc.scalar.copy(x0["kT"][j], ps[:, 4:6, 0:SK]).then_inc(S["x_kev"], 1)

            def exps(b, j):
                act.wait_ge(S["x_max"], b + 1)
                for g in range(4):
                    nc.scalar.activation(x0["p"][j][:, g, :], ps[:, g, 0:SK], ACT.Exp,
                                         bias=x0["st"][j][:, 0, g:g + 1],
                                         accum_out=x0["st"][j][:, 1, g:g + 1]).then_inc(S["x_exp"], 1)

            def turned(b):
                act.wait_ge(S["x_pt"], 3 * b + 1)
                act.wait_ge(S["x_or"], b + 1)
                nc.scalar.copy(x0["pT"][:, 0, :], ps[:, 4, :]).then_inc(S["x_pt0ev"], 1)
                act.wait_ge(S["x_pt"], 3 * b + 3)
                nc.scalar.copy(x0["pT2"][0:1, :], ps[0:1, 6, :]).then_inc(S["x_pt2ev"], 1)

            keys(0, 0)
            exps(0, 0)
            with act.Fori(0, B // 2 - 1) as i:
                b = 2 * i
                keys(b + 1, 1)
                turned(b)
                exps(b + 1, 1)
                keys(b + 2, 0)
                turned(b + 1)
                exps(b + 2, 0)
            keys(B - 1, 1)
            turned(B - 2)
            exps(B - 1, 1)
            turned(B - 1)

        def x_dve(ch):
            dve = ch.eng
            dve.wait_ge(S["ld_const"], dma_n["ld_const"])
            norm_dve(ch, "xn", xT, Xn, Xn)
            for g in range(4):
                m, h = g // 2, g % 2
                dve.wait_ge(*S.at("xq_mm", g + 1))
                nc.vector.tensor_scalar(half(Xq, m, h), ps[:, 4 + g, :], 1.0 / DK ** 0.5, None,
                                        ALU.mult).then_inc(S["xq_ev_d"], 1)
            dve.wait_ge(*S.at("ld_x", dma_n["ld_x"]))
            dve.wait_ge(S["x_vl"], 1)
            nc.vector.tensor_copy(x0["vl"][0:B], ps[0:B, 0, 0:D]).then_inc(S["x_vlast"], 1)
            nc.vector.tensor_copy(x0["slope"][0:6], x0["slope32"][0:6]).then_inc(S["x_alibi"], 1)
            nc.vector.tensor_copy(x0["pos"][0:6, 0:SK], x0["pos32"][0:6]).then_inc(S["x_alibi"], 1)

            def values(b, j):
                dve.wait_ge(S["x_v"], b + 1)
                nc.vector.tensor_copy(x0["v"][j].rearrange("p a b -> p (a b)"), ps[:, 6, :]).then_inc(S["x_vev"], 1)

            def maxima(b, j):
                dve.wait_ge(S["x_s"], b + 1)
                nc.vector.tensor_reduce(x0["st"][j][:, 2, :], ps[:, 0:4, 0:SK], AX.X, ALU.max).then_inc(S["x_mx0"], 1)
                dve.wait_ge(S["x_mx0"], b + 1)
                nc.vector.tensor_scalar(x0["st"][j][:, 0, :], x0["st"][j][:, 2, :], -1.0, None,
                                        ALU.mult).then_inc(S["x_max"], 1)

            def sums(b, j):
                dve.wait_ge(S["x_exp"], 4 * b + 4)
                nc.vector.reciprocal(x0["st"][j][:, 2, :], x0["st"][j][:, 1, :]).then_inc(S["x_rec"], 1)

            def outs(b):
                dve.wait_ge(S["x_pt"], 3 * b + 2)
                nc.vector.tensor_copy(x0["pT"][:, 1, :], ps[:, 5, :]).then_inc(S["x_pt1ev"], 1)
                dve.wait_ge(S["x_o"], b + 1)
                nc.vector.tensor_tensor(x0["om"], ps[:, 7, :], x0["dmask"], ALU.mult).then_inc(S["x_om"], 1)
                dve.wait_ge(S["x_om"], b + 1)
                nc.vector.tensor_reduce(Xo[:, :, bass.ds(b * L, L)],
                                        x0["om"].rearrange("p (c h q) -> p c q h", c=DC, h=HPC),
                                        AX.X, ALU.add).then_inc(S["x_or"], 1)

            signal("x_or")
            values(0, 0)
            maxima(0, 0)
            sums(0, 0)
            with dve.Fori(0, B // 2 - 1) as i:
                b = 2 * i
                values(b + 1, 1)
                maxima(b + 1, 1)
                outs(b)
                sums(b + 1, 1)
                values(b + 2, 0)
                maxima(b + 2, 0)
                outs(b + 1)
                sums(b + 2, 0)
            values(B - 1, 1)
            maxima(B - 1, 1)
            outs(B - 2)
            sums(B - 1, 1)
            outs(B - 1)
            for g in range(4):
                m, h = g // 2, g % 2
                dve.wait_ge(*S.at("xw_mm", g + 1))
                ch.link(nc.vector.scalar_tensor_tensor(out=half(xT, m, h), in0=ps[:, g, :], scalar=x0["bo"][:, m:m + 1],
                                                       in1=half(xT, m, h), op0=ALU.add, op1=ALU.add))

        def x_pool(pool):
            pool.wait_ge(S["ld_const"], dma_n["ld_const"])
            pool.wait_ge(*S.at("xq_ev_d", 4))

            def qblk(b, j):
                if not isinstance(b, int) or b >= 2:
                    pool.wait_ge(S["x_s"], b - 1)
                for c in range(DC):
                    nc.gpsimd.tensor_tensor(
                        x0["qb"][j][:, c * 256:(c + 1) * 256].rearrange("p (h q) -> p h q", h=HPC),
                        Xq[:, c, bass.ds(b * L, L)].unsqueeze(1).broadcast_to([P, HPC, L]),
                        hmask.unsqueeze(2).broadcast_to([P, HPC, L]), ALU.mult).then_inc(S["x_qblk"], 1)

            def normed(b, j):
                pool.wait_ge(S["x_rec"], b + 1)
                nc.gpsimd.tensor_tensor(x0["p"][j], x0["p"][j],
                                        x0["st"][j][:, 2, :].unsqueeze(2).broadcast_to([P, 4, SK]),
                                        ALU.mult).then_inc(S["x_norm"], 1)

            qblk(0, 0)
            qblk(1, 1)
            normed(0, 0)
            with pool.Fori(0, B // 2 - 1) as i:
                b = 2 * i
                qblk(b + 2, 0)
                normed(b + 1, 1)
                qblk(b + 3, 1)
                normed(b + 2, 0)
            normed(B - 1, 1)

        m_xm = view(6 * K, IC, T)
        m_z = view(10 * K, IC, T)
        m_u = view(14 * K, IC, T)
        m_bc, m_dt = view(18 * K, T), view(19 * K, T)
        m_part = bview(20 * K, 3, T)
        m_delta = view(22 * K, IC, T)
        m_du = view(26 * K, IC, T)
        m_da = view(30 * K, 4, T)
        m_h = view(34 * K, 4, T)
        m_hc = view(38 * K, 4, T)
        m_cb = view(EXTRA + 2048, 2, HALF)
        m_win = view(42 * K, DC, 2 * DI)
        m_wx = view(38 * K, IC, 3 * 64)
        m_wdt = view(39 * K, DI)
        m_s = view(34 * K, IC, T)
        m_p = view(26 * K, IC, T)
        SM = CONST + 512
        m_wout = view(SM, IC, D)
        m_a = view(SM + 1024, IC, NS)
        m_cw = view(SM + 1280, IC, KW)
        m_cb1, m_dp, m_bdt, m_nw = (view(SM + 1296 + 4 * n, IC) for n in range(4))

        def m_load(sp):
            sp.wait_ge(*S.at("mn_in", 1))
            load(sp, "ld_m1", (m_nw[:, 0:DC], A["L0_attn_norm_w"]), (m_win, A["L0_attn_W_in"]))
            load(sp, "ld_m0", (m_cw, A["L0_attn_conv_w"]))
            load(sp, "ld_m", (m_cb1, A["L0_attn_conv_b"]), (m_dp, A["L0_attn_Dp"]), (m_bdt, A["L0_attn_b_dt"]),
                 (m_a, A["L0_attn_A_log"]), (m_wx, A["L0_attn_W_x"]),
                 (m_wdt[0:64], A["L0_attn_W_dt"]), (m_wout, A["L0_attn_W_out"]))

        MU = 2 * NS
        m_diag = view(EXTRA, IC, KW, P)

        def pair(v, cp, h):
            return v[:, 2 * cp:2 * cp + 2, h * HALF:(h + 1) * HALF]

        def two(v):
            return v.rearrange("p (c t) -> p c t", c=2)

        def m_pe(pe):
            norm_pe(pe, "mn", xT, U[2])
            norm_pe(pe, "mr", U[1], U[2], rms=True)
            pe.wait_ge(*S.at("mr_out", 4))
            pe.wait_ge(S["ld_m1"], dma_n["ld_m1"])
            dense_pe(pe, "mi", [(P, [(m_win[:, k, m * P:(m + 1) * P], half(U[2], k, h)) for k in range(DC)])
                                for m in range(IC) for h in range(NH)], "d" * 8, list(range(8)))
            pe.wait_ge(S["m_taps"], IC * KW)
            for g in range(8):
                c, h = g // 2, g % 2
                pe.wait_ge(*S.at("mi_ev_d", g + 1))
                x3 = half(m_xm, c, h).rearrange("p (b t) -> p b t", t=L)
                y3 = ps[:, g, :].rearrange("p (b t) -> p b t", t=L)
                for s in range(KW):
                    mm = nc.tensor.matmul(y3[:, :, s:], m_diag[:, c, KW - 1 - s, :], x3[:, :, :L - s],
                                          start=(s == 0), stop=(s == KW - 1), skip_group_check=True)
                mm.then_inc(S["mc_mm"], 1)
            pe.wait_ge(*S.at("ld_m", dma_n["ld_m"]))
            pe.wait_ge(*S.at("mc_ev_a", 8))
            dense_pe(pe, "mx", [(r, [(m_wx[:, k, o:o + r], half(m_u, k, h)) for k in range(IC)])
                                for o, r in ((0, 64), (64, P)) for h in range(NH)], "aaaa", [0, 1, 2, 3])
            pe.wait_ge(*S.at("mx_ev_a", 4))
            dense_pe(pe, "md", [(P, [(m_wdt[0:64, m * P:(m + 1) * P], m_dt[0:64, h * HALF:(h + 1) * HALF])])
                                for m in range(IC) for h in range(NH)], "a" * 8, [4, 5, 6, 7, 0, 1, 2, 3])
            for g in range(8):
                m, h = g // 2 + IC, g % 2
                pe.wait_ge(*S.at("md_ev_a", g + 1))
                for k in range(DC):
                    mm = nc.tensor.matmul(ps[:, (4 + g) % 8, :], m_win[:, k, m * P:(m + 1) * P], half(U[2], k, h),
                                          start=(k == 0), stop=(k == 1))
                mm.then_inc(S["mz_mm"], 1)
            pe.wait_ge(S["m_parts"], 3)
            pe.wait_ge(*S.at("mz_ev_a", 8))

            def spread(nn, n, par, h):
                for first_row, bank, done, used, per in ((0, 4, "m_b", "m_dbu", 2), (NS, 6, "m_c", "m_cc", 1)):
                    if not isinstance(nn, int) or nn >= 2:
                        pe.wait_ge(S[used], per * nn - per)
                    for k in range(3):
                        mm = nc.tensor.matmul(ps[:, bank + par, :],
                                              identb[:, bass.ds(n + first_row, 1)].broadcast_to([P, P]),
                                              m_part[:, k, h * HALF:(h + 1) * HALF], start=(k == 0), stop=(k == 2))
                    mm.then_inc(S[done], 1)

            def gather(w, n0, first_n, last_n):
                for cp in range(2):
                    pe.wait_ge(S["m_hc"], w + cp + 1)
                    for cc in range(2):
                        mm = nc.tensor.matmul(ps[:, 2 * cp + cc, :], ident,
                                              m_hc[:, 2 * n0 + cp, cc * HALF:(cc + 1) * HALF],
                                              start=first_n, stop=last_n, skip_group_check=True)
                    mm.then_inc(S["m_acc"], 1)

            for h in range(NH):
                o = NS * h
                if h:
                    pe.wait_ge(S["my_ev"], IC)
                spread(o, 0, 0, h)
                spread(o + 1, 1, 1, h)
                spread(o + 2, 2, 0, h)
                gather(2 * o, 0, True, False)
                with pe.Fori(1, NS // 2 - 1) as i:
                    spread(2 * i + (o + 1), 2 * i + 1, 1, h)
                    gather(4 * i + (2 * o - 2), 1, False, False)
                    spread(2 * i + (o + 2), 2 * i + 2, 0, h)
                    gather(4 * i + 2 * o, 0, False, False)
                spread(o + NS - 1, NS - 1, 1, h)
                for n in range(NS - 3, NS):
                    gather(2 * (o + n), n % 2, False, n == NS - 1)
            pe.wait_ge(S["m_gate"], 4)
            pe.wait_ge(S["my_ev"], 2 * IC)
            dense_pe(pe, "mo", [(P, [(m_wout[:, k, m * P:(m + 1) * P], half(m_xm, k, h)) for k in range(IC)])
                                for m in range(DC) for h in range(NH)], "dddd", [4, 5, 6, 7])

        def m_act(act):
            act.wait_ge(S["ld_m0"], dma_n["ld_m0"])
            for c in range(IC):
                for j in range(KW):
                    nc.scalar.activation(m_diag[:, c, j, :], ident, ACT.Copy,
                                         scale=m_cw[:, c, j:j + 1]).then_inc(S["m_taps"], 1)
            norm_act(act, "mn", U[1], U[2], 0)
            act.wait_ge(*S.at("mn_out", 2))
            norm_act(act, "mr", U[1], U[2], 1, rms=True)
            act.wait_ge(*S.at("ld_m", dma_n["ld_m"]))
            for g in range(8):
                c, h = g // 2, g % 2
                act.wait_ge(*S.at("mc_mm", g + 1))
                nc.scalar.activation(half(m_u, c, h), ps[:, g, :], ACT.Silu,
                                     bias=m_cb1[:, c:c + 1]).then_inc(S["mc_ev_a"], 1)
            for g in range(4):
                act.wait_ge(*S.at("mx_mm", g + 1))
                h = g % 2
                if g < 2:
                    ins = nc.scalar.copy(m_dt[0:64, h * HALF:(h + 1) * HALF], ps[0:64, g, :])
                else:
                    ins = nc.scalar.copy(m_bc[:, h * HALF:(h + 1) * HALF], ps[:, g, :])
                ins.then_inc(S["mx_ev_a"], 1)
            for g in range(8):
                m, h = g // 2, g % 2
                act.wait_ge(*S.at("md_mm", g + 1))
                nc.scalar.activation(half(m_delta, m, h), ps[:, (4 + g) % 8, :], ACT.Relu,
                                     bias=m_bdt[:, m:m + 1]).then_inc(S["m_relu"], 1)
                nc.scalar.activation(half(m_s, m, h), ps[:, (4 + g) % 8, :], ACT.Abs,
                                     bias=m_bdt[:, m:m + 1]).then_inc(S["md_ev_a"], 1)
            nc.scalar.activation(m_a, m_a, ACT.Exp).then_inc(S["m_ea"], 1)
            act.wait_ge(*S.at("md_ev_a", 8))
            for h in range(NH):
                sl = m_s[:, :, h * HALF:(h + 1) * HALF]
                nc.scalar.activation(sl, sl, ACT.Exp, scale=-1.0).then_inc(S["m_e"], 1)
            for g in range(8):
                act.wait_ge(*S.at("mz_mm", g + 1))
                nc.scalar.activation(half(m_z, g // 2, g % 2), ps[:, (4 + g) % 8, :], ACT.Silu)\
                    .then_inc(S["mz_ev_a"], 1)

            def c_copy(nn, par):
                act.wait_ge(S["m_c"], nn + 1)
                if not isinstance(nn, int) or nn >= 2:
                    act.wait_ge(S["m_hc"], 2 * nn - 2)
                nc.scalar.copy(m_cb[:, par, :], ps[:, 6 + par, :]).then_inc(S["m_cc"], 1)

            def decay(w, slot, cp, n, h):
                if not isinstance(w, int) or w >= 4:
                    act.wait_ge(S["m_hs"], w - 3)
                for cc in range(2):
                    c = 2 * cp + cc
                    nc.scalar.activation(
                        m_da[:, slot, cc * HALF:(cc + 1) * HALF].rearrange("p (b t) -> p b t", t=L)[:, :, 1:L],
                        half(m_delta, c, h).rearrange("p (b t) -> p b t", t=L)[:, :, 1:L], ACT.Exp,
                        scale=m_a[:, c, bass.ds(n, 1)]).then_inc(S["m_dec"], 1)

            act.wait_ge(S["m_ready"], 1)
            act.wait_ge(S["m_neg"], 1)
            act.wait_ge(S["m_delta"], 2)
            for h in range(NH):
                o = NS * h
                for n0 in range(2):
                    for cp in range(2):
                        decay(2 * (o + n0) + cp, 2 * n0 + cp, cp, n0, h)
                    c_copy(o + n0, n0)
                with act.Fori(1, NS // 2) as i:
                    for n0 in range(2):
                        for cp in range(2):
                            decay(4 * i + (2 * o + 2 * n0 + cp), 2 * n0 + cp, cp, 2 * i + n0, h)
                        c_copy(2 * i + (o + n0), n0)

        LOG1P = (1.0, -0.49999982118, 0.33332559466, -0.24987269938, 0.19890744985, -0.16105680168,
                 0.12418411672, -0.08244141191, 0.04147793353, -0.01340739243, 0.00203021383)

        def m_dve(ch):
            dve = ch.eng
            norm_dve(ch, "mn", xT, U[1], U[1])
            signal("mr_in")
            dve.wait_ge(S["ld_m1"], dma_n["ld_m1"])
            norm_dve(ch, "mr", None, U[1], U[2], rms=True, gain=m_nw)
            for g in range(8):
                dve.wait_ge(*S.at("mi_mm", g + 1))
                nc.vector.tensor_copy(half(m_xm, g // 2, g % 2), ps[:, g, :]).then_inc(S["mi_ev_d"], 1)
            dve.wait_ge(*S.at("mx_ev_a", 4))
            nc.vector.tensor_copy(m_part[:, 0, :], m_bc).then_inc(S["m_parts"], 1)
            dve.wait_ge(S["m_parts"], 1)
            ch.link(nc.vector.tensor_tensor(m_bc, m_bc, m_part[:, 0, :], ALU.subtract))
            nc.vector.tensor_copy(m_part[:, 1, :], m_bc).then_inc(S["m_parts"], 1)
            dve.wait_ge(S["m_parts"], 2)
            ch.link(nc.vector.tensor_tensor(m_bc, m_bc, m_part[:, 1, :], ALU.subtract))
            nc.vector.tensor_copy(m_part[:, 2, :], m_bc).then_inc(S["m_parts"], 1)
            dve.wait_ge(S["m_ea"], 1)
            nc.vector.tensor_scalar(m_a, m_a, -1.0, None, ALU.mult).then_inc(S["m_neg"], 1)
            for h in range(NH):
                e, p = (v[:, :, h * HALF:(h + 1) * HALF] for v in (m_s, m_p))
                dve.wait_ge(S["m_e"], h + 1)
                ch.link(nc.vector.tensor_scalar(p, e, LOG1P[-1], None, ALU.mult))
                for k in range(len(LOG1P) - 2, 0, -1):
                    ch.link(nc.vector.scalar_tensor_tensor(out=p, in0=p, scalar=LOG1P[k], in1=e,
                                                           op0=ALU.add, op1=ALU.mult))
                nc.vector.scalar_tensor_tensor(out=p, in0=p, scalar=LOG1P[0], in1=e,
                                               op0=ALU.add, op1=ALU.mult).then_inc(S["m_log"], 1)
            dve.wait_ge(S["m_delta"], 2)
            dve.wait_ge(S["m_ready"], 1)

            def inputs_of(nn, w, n0, h):
                dve.wait_ge(S["m_b"], nn + 1)
                for cp in range(2):
                    if not isinstance(w, int) or w >= 4:
                        dve.wait_ge(S["m_hc"], w + cp - 3)
                    nc.vector.tensor_tensor(two(m_h[:, 2 * n0 + cp, :]), pair(m_du, cp, h),
                                            ps[:, 4 + n0:5 + n0, :].broadcast_to([P, 2, HALF]),
                                            ALU.mult).then_inc(S["m_dbu"], 1)

            def scans(w, n0):
                for cp in range(2):
                    sl = 2 * n0 + cp
                    dve.wait_ge(S["m_dec"], 2 * w + 2 * cp + 2)
                    dve.wait_ge(S["m_dbu"], w + cp + 1)
                    nc.vector.tensor_tensor_scan(m_h[:, sl, :], m_da[:, sl, :], m_h[:, sl, :], 0.0,
                                                 ALU.mult, ALU.add).then_inc(S["m_hs"], 1)

            for h in range(NH):
                o = NS * h
                dve.wait_ge(S["m_dudone"], h + 1)
                for n0 in range(2):
                    inputs_of(o + n0, 2 * (o + n0), n0, h)
                    scans(2 * (o + n0), n0)
                with dve.Fori(1, NS // 2) as i:
                    for n0 in range(2):
                        inputs_of(2 * i + (o + n0), 4 * i + 2 * (o + n0), n0, h)
                        scans(4 * i + 2 * (o + n0), n0)
                dve.wait_ge(S["m_acc"], MU * (h + 1))
                for c in range(IC):
                    nc.vector.scalar_tensor_tensor(out=half(m_xm, c, h), in0=half(m_u, c, h),
                                                   scalar=m_dp[:, c:c + 1], in1=ps[:, c, :],
                                                   op0=ALU.mult, op1=ALU.add).then_inc(S["my_ev"], 1)
            dve.wait_ge(S["m_res"], 1)
            for g in range(4):
                m, h = g // 2, g % 2
                dve.wait_ge(*S.at("mo_mm", g + 1))
                ch.link(nc.vector.tensor_tensor(half(xT, m, h), half(xT, m, h), ps[:, 4 + g, :], ALU.add))

        def m_pool(pool):
            pool.wait_ge(*S.at("mn_out", 2))
            nc.gpsimd.tensor_tensor(xT, xT, U[1], ALU.add).then_inc(S["m_res"], 1)
            nc.gpsimd.memset(m_da.rearrange("p a t -> p (a t)"), 0.0).then_inc(S["m_ready"], 1)
            for h in range(NH):
                sl = slice(h * HALF, (h + 1) * HALF)
                pool.wait_ge(S["m_log"], h + 1)
                if h == 0:
                    pool.wait_ge(S["m_relu"], 8)
                nc.gpsimd.tensor_tensor(m_delta[:, :, sl], m_delta[:, :, sl], m_p[:, :, sl],
                                        ALU.add).then_inc(S["m_delta"], 1)
                pool.wait_ge(S["m_delta"], h + 1)
                nc.gpsimd.tensor_tensor(m_du[:, :, sl], m_delta[:, :, sl], m_u[:, :, sl],
                                        ALU.mult).then_inc(S["m_dudone"], 1)

            def used(nn, w, n0):
                pool.wait_ge(S["m_cc"], nn + 1)
                for cp in range(2):
                    pool.wait_ge(S["m_hs"], w + cp + 1)
                    if not isinstance(w, int) or w >= 4:
                        pool.wait_ge(S["m_acc"], w + cp - 3)
                    nc.gpsimd.tensor_tensor(two(m_hc[:, 2 * n0 + cp, :]), two(m_h[:, 2 * n0 + cp, :]),
                                            m_cb[:, n0, :].unsqueeze(1).broadcast_to([P, 2, HALF]),
                                            ALU.mult).then_inc(S["m_hc"], 1)

            for h in range(NH):
                o = NS * h
                for n0 in range(2):
                    used(o + n0, 2 * (o + n0), n0)
                with pool.Fori(1, NS // 2) as i:
                    for n0 in range(2):
                        used(2 * i + (o + n0), 4 * i + 2 * (o + n0), n0)
                pool.wait_ge(S["my_ev"], IC * (h + 1))
                for cp in range(2):
                    nc.gpsimd.tensor_tensor(pair(m_xm, cp, h), pair(m_xm, cp, h), pair(m_z, cp, h),
                                            ALU.mult).then_inc(S["m_gate"], 1)

        def router_areas(o):
            return dict(w=view(o, DC, E), b=view(o + 16, E), lg=view(o + 24, TT, E), pr=view(o + 88, TT, E),
                        m8=view(o + 152, TT, E), ix=view(o + 216, TT, E).bitcast(U32), ixf=view(o + 280, TT, E),
                        e1=view(o + 344, TT, E), e2=view(o + 408, TT, E), s=view(o + 472, 4, TT),
                        cT=view(o + 512, T), cS=view(o + 512 + T, T), part=bview(o + 512 + 2 * T, 3, T))

        def route_pe(pe, n, R, xf):
            for t in range(TT):
                for k in range(DC):
                    mm = nc.tensor.matmul(ps[:, 4, t * E:(t + 1) * E], xf[:, k, t * P:(t + 1) * P], R["w"][:, k, :],
                                          start=(k == 0), stop=(k == 1))
            mm.then_inc(S[n + "_lg"], 1)
            pe.wait_ge(S[n + "_cm"], 1)
            for t in range(TT):
                mm = nc.tensor.transpose(ps[0:E, 5 + t // 4, (t % 4) * P:(t % 4 + 1) * P], R["e1"][:, t, :], ident)
            mm.then_inc(S[n + "_cT"], 1)

        def route_act(act, n, R, renorm):
            act.wait_ge(S[n + "_sub"], 1)
            nc.scalar.activation(R["pr"], R["lg"], ACT.Exp).then_inc(S[n + "_exp"], 1)
            if renorm:
                act.wait_ge(S[n + "_d"], 1)
                nc.scalar.activation(R["s"][:, 2, :], R["s"][:, 1, :], ACT.Exp).then_inc(S[n + "_e2"], 1)

        def route_dve(ch, n, R, renorm):
            dve, ln = ch.eng, ch.link
            v = nc.vector

            def over_e(x):
                return x.unsqueeze(2).broadcast_to([P, TT, E])
            dve.wait_ge(S[n + "_lg"], 1)
            ln(v.tensor_tensor(R["lg"], ps[:, 4, 0:TT * E].rearrange("p (t e) -> p t e", e=E),
                               R["b"].unsqueeze(1).broadcast_to([P, TT, E]), ALU.add))
            ln(v.tensor_reduce(R["s"][:, 0, :], R["lg"], AX.X, ALU.max))
            v.tensor_tensor(R["lg"], R["lg"], over_e(R["s"][:, 0, :]), ALU.subtract).then_inc(S[n + "_sub"], 1)
            dve.wait_ge(S[n + "_exp"], 1)
            ln(v.tensor_reduce(R["s"][:, 0, :], R["pr"], AX.X, ALU.add))
            ln(v.reciprocal(R["s"][:, 0, :], R["s"][:, 0, :]))
            ln(v.tensor_tensor(R["pr"], R["pr"], over_e(R["s"][:, 0, :]), ALU.mult))
            for t in range(TT):
                ch.step(v.max(R["m8"][:, t, :], R["pr"][:, t, :]))
            ch.sync()
            for t in range(TT):
                ch.step(v.max_index(R["ix"][:, t, :], R["m8"][:, t, :], R["pr"][:, t, :]))
            ch.sync()
            ln(v.tensor_copy(R["ixf"], R["ix"]))
            w1, w2 = R["m8"][:, :, 0], R["m8"][:, :, 1]
            if renorm:
                v.tensor_tensor(R["s"][:, 1, :], w2, w1, ALU.subtract).then_inc(S[n + "_d"], 1)
                dve.wait_ge(S[n + "_e2"], 1)
                ln(v.tensor_scalar(R["s"][:, 1, :], R["s"][:, 2, :], 1.0, None, ALU.add))
                ln(v.reciprocal(R["s"][:, 0, :], R["s"][:, 1, :]))
                ln(v.tensor_tensor(R["s"][:, 3, :], R["s"][:, 2, :], R["s"][:, 0, :], ALU.mult))
                w1, w2 = R["s"][:, 0, :], R["s"][:, 3, :]
            for k, (w, e) in enumerate(((w1, "e1"), (w2, "e2"))):
                ln(v.tensor_tensor(R[e], iota8.unsqueeze(1).broadcast_to([P, TT, E]), over_e(R["ixf"][:, :, k]),
                                   ALU.is_equal))
                ln(v.tensor_tensor(R[e], R[e], over_e(w), ALU.mult))
            v.tensor_tensor(R["e1"], R["e1"], R["e2"], ALU.add).then_inc(S[n + "_cm"], 1)
            dve.wait_ge(S[n + "_cT"], 1)
            ln(v.tensor_copy(R["cT"][0:E, :], ps[0:E, 5:7, :].rearrange("p a b -> p (a b)")))

        def route_parts(ch, n, R):
            rest, part = R["cT"], R["part"]
            ch.eng.wait_ge(S[n + "_zero"], 1)
            for k in range(3):
                ins = nc.vector.tensor_copy(part[0:E, k, :], rest[0:E, :])
                if k == 2:
                    ins.then_inc(S[n + "_part"], 1)
                    break
                ch.link(ins)
                ch.link(nc.vector.tensor_tensor(R["cS"][0:E, :], rest[0:E, :], part[0:E, k, :], ALU.subtract))
                rest = R["cS"]

        def route_pool(pool, n, R, stage_in):
            pool.wait_ge(*S.at(stage_in, 1))
            nc.gpsimd.memset(R["part"].rearrange("p k t -> p (k t)"), 0.0).then_inc(S[n + "_zero"], 1)

        def weight_pe(R, e, h):
            for k in range(3):
                mm = nc.tensor.matmul(ps[:, 6 + h, :], identb[:, bass.ds(e, 1)].broadcast_to([P, P]),
                                      R["part"][:, k, h * HALF:(h + 1) * HALF], start=(k == 0), stop=(k == 2))
            return mm

        f_q = U[3]
        f_k = view(8 * K, T)
        f_v = view(9 * K, TT, P)
        f_o = U[5]
        f_S = [view(12 * K + 512 * j, 4, P) for j in range(2)]
        f_pT = [view(13 * K + 512 * j, HALF) for j in range(2)]
        f_st = [view(14 * K + 16 * j, 3, 4) for j in range(2)]
        f_neg = view(14 * K + 64, P)
        f_g = view(14 * K + 256, 2, DC)
        f_wq, f_wkv, f_wo = view(15 * K, DC, D), view(15 * K + 512, DC, 2 * P), view(16 * K, DC, D)
        f_R = router_areas(17 * K)
        f_w13 = [view(21 * K + 1024 * j, DC, 2 * D) for j in range(2)]
        f_w2 = [view(23 * K + 512 * j, DC, D) for j in range(2)]
        f_sa = view(24 * K, 2, HALF)
        f_sb = view(25 * K, HALF)
        f_h = [view(26 * K + 1024 * j, 2, HALF) for j in range(2)]

        def f_load(sp):
            sp.wait_ge(*S.at("fn_in", 1))
            load(sp, "ld_f", (f_wq, A["L0_ffn_Wq"]), (f_wkv, A["L0_ffn_Wkv"]), (f_wo, A["L0_ffn_Wo"]),
                 (f_g[:, 0, :], A["L0_ffn_g1"]), (f_g[:, 1, :], A["L0_ffn_g2"]), (f_neg, A["c_neg"]),
                 (f_R["w"], A["L0_ffn_Wr"]), (f_R["b"], A["L0_ffn_expert_bias"]), shared="loads")
            sp.dma_start(f_w13[1], A["L0_ffn_sW13"]).then_inc(S["fe_wt1"], 16)
            sp.dma_start(f_w2[1], A["L0_ffn_sW2"]).then_inc(S["fe_wt1"], 16)

            def expert(e, j):
                sp.dma_start(f_w13[j], A["L0_ffn_eW13"][:, bass.ds(e, 1)].rearrange("p a k f -> p (a k) f"))\
                    .then_inc(S[f"fe_wt{j}"], 16)
                sp.dma_start(f_w2[j], A["L0_ffn_eW2"][:, bass.ds(e, 1)].rearrange("p a k f -> p (a k) f"))\
                    .then_inc(S[f"fe_wt{j}"], 16)
            expert(0, 0)
            sp.wait_ge(S["fe_w2"], 2)
            expert(1, 1)
            with sp.Fori(1, E // 2) as i:
                for j in range(2):
                    sp.wait_ge(S["fe_w2"], 4 * i + 2 * j)
                    expert(2 * i + j, j)

        def f_pe(pe):
            norm_pe(pe, "fn", xT, U[2])
            norm_pe(pe, "fr", U[1], U[2], rms=True)
            pe.wait_ge(*S.at("fr_out", 4))
            pe.wait_ge(*S.at("ld_f", dma_n["ld_f"]))
            dense_pe(pe, "fq", [(P, [(w[:, k, m * P:(m + 1) * P], half(U[2], k, h)) for k in range(DC)])
                                for w, m in ((f_wq, 0), (f_wq, 1), (f_wkv, 0)) for h in range(NH)],
                     "d" * 6, list(range(6)))
            for t in range(TT):
                for k in range(DC):
                    mm = nc.tensor.matmul(ps[:, 6 + t // 4, (t % 4) * P:(t % 4 + 1) * P],
                                          U[2][:, k, t * P:(t + 1) * P], f_wkv[:, k, P:2 * P],
                                          start=(k == 0), stop=(k == 1))
                if t % 4 == 3:
                    mm.then_inc(S["f_v"], 1)
            pe.wait_ge(*S.at("fq_ev_d", 6))

            def sc(t):
                if t >= 2:
                    pe.wait_ge(S["f_sm"], t - 1)
                if t == 0:
                    pe.wait_ge(*S.at("fq_ev_d", 6))
                for hd in range(4):
                    r = slice(64 * (hd % 2), 64 * (hd % 2) + 64)
                    mm = nc.tensor.matmul(ps[:, 2 * (t % 2) + hd % 2, (hd // 2) * P:(hd // 2 + 1) * P],
                                          f_q[r, hd // 2, t * P:(t + 1) * P],
                                          f_k[r, t * P:(t + 1) * P], start=True, stop=True)
                mm.then_inc(S["f_s"], 1)

            def turn(t):
                pe.wait_ge(S["f_norm"], t + 1)
                for hd in range(4):
                    mm = nc.tensor.transpose(ps[:, 4 + t % 2, hd * P:(hd + 1) * P], f_S[t % 2][:, hd, :], ident)
                mm.then_inc(S["f_pt"], 1)
                pe.wait_ge(S["f_ptev"], t + 1)
                if t >= 2:
                    pe.wait_ge(S["f_oev"], 2 * t - 2)
                nc.tensor.matmul(ps[:, 6 + t % 2, :], f_v[:, t, :], f_pT[t % 2], start=True,
                                 stop=True).then_inc(S["f_pv"], 1)

            pe.wait_ge(S["f_vev"], 2)
            sc(0)
            for t in range(TT):
                if t + 1 < TT:
                    sc(t + 1)
                turn(t)
            pe.wait_ge(S["f_oev"], 2 * TT)
            dense_pe(pe, "fw", [(P, [(f_wo[:, k, m * P:(m + 1) * P], half(f_o, k, h)) for k in range(DC)])
                                for m in range(DC) for h in range(NH)], "dddd", [0, 1, 6, 7])
            norm_pe(pe, "f2", U[1], U[2], rms=True)
            pe.wait_ge(*S.at("f2_out", 4))
            route_pe(pe, "fr", f_R, U[2])

            def up(v, h, j, e):
                for f in range(2):
                    for part in range(2):
                        if not isinstance(v, int) or v or f:
                            pe.wait_ge(S[("fe_sa", "fe_sb")[part]], 2 * v + f)
                        for k in range(DC):
                            mm = nc.tensor.matmul(ps[:, 4 + part, :],
                                                  f_w13[j][:, k, part * D + f * P:part * D + (f + 1) * P],
                                                  half(U[2], k, h), start=(k == 0), stop=(k == 1))
                        mm.then_inc(S["fe_ab"], 1)
                    if f == 0 and e is not None:
                        if not isinstance(v, int) or v >= 2:
                            pe.wait_ge(S["fe_h"], 2 * v - 2)
                        weight_pe(f_R, e, h).then_inc(S["fe_c"], 1)

            def down(v, h, j, start, stop):
                pe.wait_ge(S["fe_h"], 2 * v + 2)
                for m in range(DC):
                    for f in range(2):
                        mm = nc.tensor.matmul(ps[:, 2 * m + h, :], f_w2[j][:, f, m * P:(m + 1) * P], f_h[h][:, f, :],
                                              start=start and f == 0, stop=stop and f == 1, skip_group_check=True)
                mm.then_inc(S["fe_w2"], 1)

            pe.wait_ge(S["fr_part"], 1)
            pe.wait_ge(*S.at("fe_wt1", 32))
            up(0, 0, 1, None)
            up(1, 1, 1, None)
            down(0, 0, 1, True, False)

            def expert_pair(i, first_pair):
                for j in range(2):
                    v = 4 * i + 2 + 2 * j
                    pe.wait_ge(*S.at(f"fe_wt{j}", 32 * i + 32 + 32 * j))
                    up(v, 0, j, 2 * i + j)
                    down(v - 1, 1, 1 - j, first_pair and j == 0, False)
                    up(v + 1, 1, j, 2 * i + j)
                    down(v, 0, j, False, False)
            expert_pair(0, True)
            with pe.Fori(1, E // 2) as i:
                expert_pair(i, False)
            down(2 * E + 1, 1, 1, False, True)

        def f_act(act):
            norm_act(act, "fn", U[1], U[2], 0)
            act.wait_ge(*S.at("fn_out", 2))
            norm_act(act, "fr", U[1], U[2], 2, rms=True)
            for n in range(2):
                act.wait_ge(S["f_v"], n + 1)
                nc.scalar.copy(f_v[:, 4 * n:4 * n + 4, :].rearrange("p a b -> p (a b)"), ps[:, 6 + n, :])\
                    .then_inc(S["f_vev"], 1)
            for t in range(TT + 1):
                if t < TT:
                    act.wait_ge(S["f_max"], t + 1)
                    for hd in range(4):
                        nc.scalar.activation(f_S[t % 2][:, hd, :], f_S[t % 2][:, hd, :], ACT.Exp,
                                             bias=f_st[t % 2][:, 0, hd:hd + 1],
                                             accum_out=f_st[t % 2][:, 1, hd:hd + 1]).then_inc(S["f_exp"], 1)
                if t >= 1:
                    act.wait_ge(S["f_pt"], t)
                    if t >= 3:
                        act.wait_ge(S["f_pv"], t - 2)
                    nc.scalar.copy(f_pT[(t - 1) % 2], ps[:, 4 + (t - 1) % 2, :]).then_inc(S["f_ptev"], 1)
            act.wait_ge(*S.at("f2_in", 1))
            norm_act(act, "f2", U[1], U[2], 2, rms=True)
            route_act(act, "fr", f_R, True)

            def gate(r, f):
                act.wait_ge(S["fe_ab"], 2 * r + 1)
                if not isinstance(r, int) or r >= 2:
                    act.wait_ge(S["fe_sb"], r - 1)
                nc.scalar.activation(f_sa[:, f, :], ps[:, 4, :], ACT.Silu).then_inc(S["fe_sa"], 1)
            for r in range(4):
                gate(r, r % 2)
            with act.Fori(1, E + 1) as i:
                for r in range(4):
                    gate(4 * i + r, r % 2)

        def f_dve(ch):
            dve = ch.eng
            norm_dve(ch, "fn", xT, U[1], U[1])
            signal("fr_in")
            dve.wait_ge(*S.at("ld_f", dma_n["ld_f"]))
            norm_dve(ch, "fr", None, U[1], U[2], rms=True, gain=f_g[:, 0, :])
            for g in range(6):
                dve.wait_ge(*S.at("fq_mm", g + 1))
                dst = half(f_q, g // 2, g % 2) if g < 4 else f_k[:, (g - 4) * HALF:(g - 3) * HALF]
                nc.vector.tensor_scalar(dst, ps[:, g, :], 0.125 if g < 4 else 1.0, None,
                                        ALU.mult).then_inc(S["fq_ev_d"], 1)

            def soft(t):
                st = f_st[t % 2]
                dve.wait_ge(S["f_s"], t + 1)
                if t >= 2:
                    dve.wait_ge(S["f_pt"], t - 1)
                nc.vector.tensor_tensor(f_S[t % 2].rearrange("p (o c) k -> p o c k", o=2),
                                        ps[:, 2 * (t % 2):2 * (t % 2) + 2, 0:2 * P].rearrange("p o (c k) -> p o c k", c=2),
                                        f_neg.unsqueeze(1).unsqueeze(1).broadcast_to([P, 2, 2, P]), ALU.add).then_inc(S["f_sm"], 1)
                dve.wait_ge(S["f_sm"], t + 1)
                ch.link(nc.vector.tensor_reduce(st[:, 2, :], f_S[t % 2], AX.X, ALU.max))
                nc.vector.tensor_scalar(st[:, 0, :], st[:, 2, :], -1.0, None, ALU.mult).then_inc(S["f_max"], 1)

            soft(0)
            for t in range(TT):
                if t + 1 < TT:
                    soft(t + 1)
                dve.wait_ge(S["f_exp"], 4 * t + 4)
                nc.vector.reciprocal(f_st[t % 2][:, 2, :], f_st[t % 2][:, 1, :]).then_inc(S["f_rec"], 1)
                if t >= 1:
                    heads_out(dve, t - 1)
            heads_out(dve, TT - 1)
            for g in range(4):
                m, h = g // 2, g % 2
                dve.wait_ge(*S.at("fw_mm", g + 1))
                ch.link(nc.vector.tensor_tensor(half(U[1], m, h), half(U[1], m, h),
                                                ps[:, (0, 1, 6, 7)[g], :], ALU.add))
            signal("f2_in")
            norm_dve(ch, "f2", None, U[1], U[2], rms=True, gain=f_g[:, 1, :])
            route_dve(ch, "fr", f_R, True)
            route_parts(ch, "fr", f_R)

            def product(v, r, h, f, e):
                dve.wait_ge(S["fe_sa"], r + 1)
                dve.wait_ge(S["fe_ab"], 2 * r + 2)
                nc.vector.tensor_tensor(f_sb, f_sa[:, f, :], ps[:, 5, :], ALU.mult).then_inc(S["fe_sb"], 1)
                dve.wait_ge(S["fe_sb"], r + 1)
                if not isinstance(v, int) or v >= 2:
                    dve.wait_ge(S["fe_w2"], v - 1)
                if e:
                    dve.wait_ge(S["fe_c"], v - 1)
                    ins = nc.vector.tensor_tensor(f_h[h][:, f, :], f_sb, ps[:, 6 + h, :], ALU.mult)
                else:
                    ins = nc.vector.tensor_copy(f_h[h][:, f, :], f_sb)
                ins.then_inc(S["fe_h"], 1)
                dve.wait_ge(S["fe_h"], r + 1)
            for h in range(NH):
                for f in range(2):
                    product(h, 2 * h + f, h, f, False)
            with dve.Fori(1, E + 1) as i:
                for h in range(NH):
                    for f in range(2):
                        product(2 * i + h, 4 * i + 2 * h + f, h, f, True)
            dve.wait_ge(S["f_res"], 1)
            dve.wait_ge(S["fe_w2"], 2 * E + 2)
            for g in range(4):
                ch.link(nc.vector.tensor_tensor(half(xT, g // 2, g % 2), half(xT, g // 2, g % 2),
                                                ps[:, g, :], ALU.add))

        def heads_out(dve, t):
            dve.wait_ge(S["f_pv"], t + 1)
            for o in range(2):
                r = slice(64 * o, 64 * o + 64)
                nc.vector.tensor_copy(f_o[r, :, t * P:(t + 1) * P],
                                      ps[r, 6 + t % 2, :].rearrange("p (o c q) -> p o c q", c=2, o=2)[:, o, :, :])\
                    .then_inc(S["f_oev"], 1)

        def f_pool(pool):
            route_pool(pool, "fr", f_R, "fn_in")
            for t in range(TT):
                pool.wait_ge(S["f_rec"], t + 1)
                nc.gpsimd.tensor_tensor(f_S[t % 2], f_S[t % 2],
                                        f_st[t % 2][:, 2, :].unsqueeze(2).broadcast_to([P, 4, P]),
                                        ALU.mult).then_inc(S["f_norm"], 1)
            pool.wait_ge(*S.at("f2_in", 1))
            nc.gpsimd.tensor_tensor(xT, xT, U[1], ALU.add).then_inc(S["f_res"], 1)

        IP = SK + 1
        d_m2 = U[3]
        d_xs = [view(34 * K + 256 * j, DC, P) for j in range(2)]
        SL = 4
        d_ctx = [view(26 * K + 2080 * j, DC, SL * SK) for j in range(2)]
        d_sq = [view(EXTRA + 2080 * j, DC, SL * SK) for j in range(2)]
        d_ss = [view(31 * K + 1040 * j, SL * SK) for j in range(2)]
        d_dt = [view(39 * K + 260 * j, SK) for j in range(2)]
        d_bb = view(40 * K, TT)
        d_R = view(8 * K, L + 1, IP)
        d_D = view(17 * K, L, SK)
        d_t = view(25 * K + 256, L, SK)
        d_from = bview(34 * K, L, 2, IP)
        d_up = bview(EXTRA, L, IP)
        d_V = bview(21 * K + 256, L, IP)
        d_E, d_VD = view(42 * K + 640, IP), view(33 * K + 300, 2, IP)
        d_M = view(8 * K, 3, B, L)
        RT = -(-SK // 3)
        ROWS = (RT, RT, SK - 2 * RT)
        d_ct = [view(26 * K + 3072 * j, SL, 3, D) for j in range(2)]
        d_ms = [view(12 * K + 384 * j, 3, P) for j in range(2)]
        d_tm = [view(13 * K + 256 * j, D) for j in range(2)]

        def d_load(sp):
            sp.wait_ge(*S.at("dn_in", 1))

            def ctx_load(g, j):
                sp.dma_start(d_ctx[j], A["ctxT"][:, :, bass.ds(g * (SL * SK), SL * SK)]).then_inc(S[f"d_ctx{j}"], 16)

            def keep(g, j):
                sp.wait_ge(S["d_sqrt"], g + 1)
                sp.dma_start(dist[bass.ds(g, 1)].rearrange("a p i -> (a p) i"), d_dt[j]).then_inc(S[f"d_out{j}"], 16)
            ctx_load(0, 0)
            ctx_load(1, 1)
            with sp.Fori(1, TT // 2) as i:
                for j in range(2):
                    sp.wait_ge(S["d_ab"], 2 * i + j - 1)
                    ctx_load(2 * i + j, j)
                    keep(2 * i + (j - 2), j)
            keep(TT - 2, 0)
            keep(TT - 1, 1)
            for j in range(2):
                sp.wait_ge(*S.at(f"d_out{j}", 16 * TT // 2))
            sp.dma_start(d_D[0:B].rearrange("p j i -> p (j i)"),
                         dist.rearrange("g (s j) i -> (g s) (j i)", j=L)).then_inc(S["d_back"], 16)

            def rows(g, j):
                sp.dma_start(d_ct[j][0:RT], A["ctx_rows"][:, bass.ds(g * SL, SL)]).then_inc(S[f"d_rows{j}"], 16)
            sp.wait_ge(S["d_choice"], 2 * L)
            rows(0, 0)
            rows(1, 1)
            with sp.Fori(1, TT // 2) as i:
                for j in range(2):
                    sp.wait_ge(S["d_exp"], 2 * i + j - 1)
                    rows(2 * i + j, j)

        def d_pe(pe):
            norm_pe(pe, "dn", xT, U[2])
            pe.wait_ge(S["d_tsq"], 1)
            for g in range(TT):
                for k in range(DC):
                    mm = nc.tensor.matmul(ps[:, 4, g:g + 1], U[2][:, k, g * P:(g + 1) * P], ones[:, 0:1],
                                          start=(k == 0), stop=(k == 1))
            mm.then_inc(S["d_bb"], 1)

            def tile(g, j, i):
                pe.wait_ge(S["d_xs"], g + 1)
                pe.wait_ge(*S.at(f"d_ctx{j}", 16 * i + 16))
                if not isinstance(g, int) or g >= 2:
                    pe.wait_ge(S["d_clip"], g - 1)
                for bi in range(SL):
                    own = slice(bi * SK, (bi + 1) * SK)
                    dst = ps[32 * bi:32 * bi + 32, j, 0:SK]
                    for k in range(DC):
                        nc.tensor.matmul(dst, d_xs[j][:, k, 32 * bi:32 * bi + 32], d_ctx[j][:, k, own],
                                         start=(k == 0), stop=False)
                    if bi == 0:
                        pe.wait_ge(S["d_ss"], g + 1)
                    mm = nc.tensor.matmul(dst, ones, d_ss[j][:, own], start=False, stop=True)
                mm.then_inc(S["d_ab"], 1)
            tile(0, 0, 0)
            tile(1, 1, 0)
            with pe.Fori(1, TT // 2) as i:
                for j in range(2):
                    tile(2 * i + j, j, i)
            for n in range(L):
                pe.wait_ge(S["d_v"], n + 1)
                j = L - 1 - n
                for t, rows in enumerate(ROWS):
                    mm = nc.tensor.transpose(
                        ps[0:rows, t, :].bitcast(BF16)[:, j * B:(j + 1) * B],
                        d_V[0:B, j, t * RT:t * RT + rows],
                        identb[0:B, 0:B])
                mm.then_inc(S["d_vT"], 1)
            
            def turn(g, j):
                pe.wait_ge(*S.at("d_tm", g + 1))
                if not isinstance(g, int) or g >= 2:
                    pe.wait_ge(*S.at("d_add", g - 1))
                for c in range(DC):
                    mm = nc.tensor.transpose(ps[:, 6 + j, c * P:(c + 1) * P], d_tm[j][:, c * P:(c + 1) * P], ident)
                mm.then_inc(S["d_tr"], 1)

            def expand(g, j, i):
                pe.wait_ge(*S.at("d_ms", g + 1))
                pe.wait_ge(S[f"d_rows{j}"], 16 * i + 16)
                if not isinstance(g, int) or g >= 2:
                    pe.wait_ge(*S.at("d_tm", g - 1))
                for bi in range(SL):
                    for t, rows in enumerate(ROWS):
                        mm = nc.tensor.matmul(ps[32 * bi:32 * bi + 32, 4 + j, 0:D],
                                              d_ms[j][0:rows, t, 32 * bi:32 * bi + 32], d_ct[j][0:rows, bi, t, :],
                                              start=(t == 0), stop=(t == 2))
                mm.then_inc(S["d_exp"], 1)
            expand(0, 0, 0)
            expand(1, 1, 0)
            turn(0, 0)
            with pe.Fori(1, TT // 2) as i:
                for j in range(2):
                    expand(2 * i + j, j, i)
                    turn(2 * i + (j - 1), 1 - j)
            turn(TT - 1, 1)

        def d_act(act):
            norm_act(act, "dn", U[1], U[2], 0)
            act.wait_ge(*S.at("dn_out", 2))
            nc.scalar.activation(U[2], U[1], ACT.Square).then_inc(S["d_tsq"], 1)

            def squares(g, j, i):
                act.wait_ge(*S.at(f"d_ctx{j}", 16 * i + 16))
                if not isinstance(g, int) or g >= 2:
                    act.wait_ge(S["d_ss"], g - 1)
                nc.scalar.activation(d_sq[j], d_ctx[j], ACT.Square).then_inc(S["d_sq"], 1)

            def root(g, j):
                act.wait_ge(S["d_clip"], g + 1)
                nc.scalar.activation(d_dt[j], d_dt[j], ACT.Sqrt).then_inc(S["d_sqrt"], 1)

            squares(0, 0, 0)
            squares(1, 1, 0)
            root(0, 0)
            with act.Fori(1, TT // 2) as i:
                for j in range(2):
                    squares(2 * i + j, j, i)
                    root(2 * i + (j - 1), 1 - j)
            root(TT - 1, 1)
            act.wait_ge(S["d_vT"], L)
            for t, rows in enumerate(ROWS):
                nc.scalar.copy(d_M[0:rows, t].rearrange("p b j -> p j b"),
                               ps[0:rows, t, :].bitcast(BF16).rearrange("p (j b) -> p j b", j=L)).then_inc(S["d_mev"], 1)
            act.wait_ge(S["d_mev"], 3)

            def path(g, j):
                nc.scalar.copy(d_ms[j][0:RT].rearrange("p t (b q) -> p t b q", q=L),
                               d_M[0:RT, :, bass.ds(g * SL, SL), :]).then_inc(S["d_ms"], 1)

            def evict(g, j):
                act.wait_ge(S["d_exp"], g + 1)
                if not isinstance(g, int) or g >= 2:
                    act.wait_ge(S["d_tr"], g - 1)
                nc.scalar.copy(d_tm[j], ps[:, 4 + j, 0:D]).then_inc(S["d_tm"], 1)
            path(0, 0)
            path(1, 1)
            evict(0, 0)
            path(2, 0)
            evict(1, 1)
            path(3, 1)
            with act.Fori(1, TT // 2 - 1) as i:
                for j in range(2):
                    evict(2 * i + j, j)
                    path(2 * i + j + 2, j)
            evict(TT - 2, 0)
            evict(TT - 1, 1)

        def d_dve(ch):
            dve = ch.eng
            norm_dve(ch, "dn", xT, U[1], U[1])
            nc.vector.tensor_scalar(d_m2, U[1], -2.0, None, ALU.mult).then_inc(S["d_m2"], 1)
            dve.wait_ge(S["d_bb"], 1)
            ch.link(nc.vector.tensor_copy(d_bb, ps[:, 4, 0:TT]))

            def clip(g, j):
                dve.wait_ge(S["d_ab"], g + 1)
                if not isinstance(g, int) or g >= 2:
                    dve.wait_ge(*S.at(f"d_out{j}", 8 * (g - j)))
                nc.vector.tensor_scalar(d_dt[j], ps[:, j, 0:SK], d_bb[:, bass.ds(g, 1)], 0.0, ALU.add,
                                        ALU.max).then_inc(S["d_clip"], 1)
            clip(0, 0)
            clip(1, 1)
            with dve.Fori(1, TT // 2) as i:
                for j in range(2):
                    clip(2 * i + j, j)
            R, least = d_R[0:B], d_t[0:B]
            lf, dg, up = d_from[0:B, :, 0], d_from[0:B, :, 1], d_up[0:B]
            E_, VD = d_E[0:B], d_VD[0:B]
            ch.link(nc.vector.memset(R[:, 0, :], BIG))
            ch.link(nc.vector.memset(R[:, 0, 0:1], 0.0))
            ch.link(nc.vector.memset(R[:, 1:L + 1, 0:1], BIG))
            ch.link(nc.vector.memset(up[:, :, 0:1], 0.0))
            ch.link(nc.vector.memset(E_, 0.0))
            ch.link(nc.vector.memset(VD[:, 1, 0:1], 0.0))
            ch.link(nc.vector.memset(E_[:, 0:1], 1.0))
            dve.wait_ge(S["d_back"], 16)

            def choice(j, part):
                if j < 0:
                    return
                dve.wait_ge(S["d_least"], j + 1)
                dst, src = ((up, R[:, j + 1, 0:SK]), (dg, R[:, j, 0:SK]))[part]
                nc.vector.tensor_tensor(dst[:, j, IP - 1:0:-1], src, least[:, j, :], ALU.is_le).then_inc(S["d_choice"], 1)

            def least_of(j):
                nc.vector.tensor_tensor(least[:, j, :], least[:, j, :], R[:, j + 1, 0:SK], ALU.min).then_inc(S["d_least"], 1)
            for j in range(L):
                prev, cur = R[:, j, :], R[:, j + 1, :]
                nc.vector.tensor_tensor(least[:, j, :], prev[:, 1:IP], prev[:, 0:SK], ALU.min).then_inc(S["d_fwd"], 1)
                if j:
                    least_of(j - 1)
                choice(j - 2, 0)
                dve.wait_ge(S["d_fwd"], 2 * j + 1)
                nc.vector.tensor_tensor_scan(cur[:, 1:IP], least[:, j, :], d_D[0:B, j, :], BIG,
                                             ALU.min, ALU.add).then_inc(S["d_fwd"], 1)
                choice(j - 2, 1)
                dve.wait_ge(S["d_fwd"], 2 * j + 2)
            least_of(L - 1)
            for j in range(L - 2, L):
                for part in range(2):
                    choice(j, part)
            dve.wait_ge(S["d_choice"], 2 * L)
            ch.link(nc.vector.memset(d_M[64:96, 2].rearrange("p b j -> p (b j)"), 0.0))

            def sort_left(j):
                nc.vector.scalar_tensor_tensor(out=lf[:, j, 1:IP], in0=dg[:, j, 1:IP], scalar=0.0, in1=up[:, j, 1:IP],
                                               op0=ALU.is_equal, op1=ALU.is_gt).then_inc(S["d_sort"], 1)

            def sort_up(j):
                dve.wait_ge(S["d_sort"], 2 * (L - 1 - j) + 1)
                nc.vector.tensor_tensor(up[:, j, 1:IP], up[:, j, 1:IP], dg[:, j, 1:IP],
                                        ALU.is_gt).then_inc(S["d_sort"], 1)
            sort_left(L - 1)
            sort_up(L - 1)
            for n in range(L):
                j = L - 1 - n
                dve.wait_ge(S["d_sort"], 2 * n + 2)
                v = d_V[0:B, j, :]
                nc.vector.tensor_tensor_scan(v[:, 0:SK], up[:, j, 0:SK], E_[:, 0:SK], 0.0,
                                             ALU.mult, ALU.add).then_inc(S["d_v"], 1)
                if j:
                    sort_left(j - 1)
                dve.wait_ge(S["d_v"], n + 1)
                nc.vector.tensor_tensor(VD[:, :, 1:IP], v[:, 0:SK].unsqueeze(1).broadcast_to([B, 2, SK]),
                                        d_from[0:B, j, :, 1:IP],
                                        ALU.mult).then_inc(S["d_bw"], 1)
                if j:
                    sort_up(j - 1)
                dve.wait_ge(S["d_bw"], 2 * n + 1)
                nc.vector.tensor_tensor(E_[:, 0:SK], VD[:, 0, 1:IP], VD[:, 1, 0:SK], ALU.add).then_inc(S["d_bw"], 1)
                dve.wait_ge(S["d_bw"], 2 * n + 2)

            def add(g, j):
                dve.wait_ge(S["d_tr"], g + 1)
                dst = xT[:, :, bass.ds(g * P, P)]
                nc.vector.tensor_tensor(dst, dst, ps[:, 6 + j, 0:D].rearrange("p (c j) -> p c j", c=DC),
                                        ALU.add).then_inc(S["d_add"], 1)
            with dve.Fori(0, TT // 2) as i:
                for j in range(2):
                    add(2 * i + j, j)
            dve.wait_ge(*S.at("d_add", TT))

        def d_pool(pool):
            def slot(g, j):
                if not isinstance(g, int) or g >= 2:
                    pool.wait_ge(S["d_ab"], g - 1)
                nc.gpsimd.tensor_copy(d_xs[j], d_m2[:, :, bass.ds(g * P, P)]).then_inc(S["d_xs"], 1)
                pool.wait_ge(S["d_sq"], g + 1)
                nc.gpsimd.tensor_tensor(d_ss[j], d_sq[j][:, 0, :], d_sq[j][:, 1, :], ALU.add).then_inc(S["d_ss"], 1)
            pool.wait_ge(S["d_m2"], 1)
            slot(0, 0)
            slot(1, 1)
            with pool.Fori(1, TT // 2) as i:
                for j in range(2):
                    slot(2 * i + j, j)

        t_raw = [U[2], U[3], U[4]]
        t_g = U[5]
        t_x = [U[6], U[7], U[8]]
        t_sq = [U[9], U[10]]
        t_v = view(22 * K, TT, D)
        t_o = view(24 * K, TT, D)
        t_osq = view(18 * K, TT, D)
        t_qm = [view(26 * K + 2048 * j, DC, HPC, P) for j in range(2)]
        t_S = [view(30 * K + 2048 * j, XH, P) for j in range(2)]
        t_w = [view(34 * K + 512 * n, DC, D) for n in range(5)]
        t_W0 = view(37 * K, DC, P)
        t_tril = view(37 * K + 256, P)
        t_cw = view(37 * K + 384, 3, DC, KW)
        t_gam, t_bet = view(37 * K + 512, DK), view(37 * K + 528, DK)
        t_ns = view(38 * K, 2, 2 * P)
        t_rep = view(39 * K, 2, TT, D)
        t_st = view(37 * K + 544, 2, TT * XH)

        def t_load(sp):
            sp.wait_ge(*S.at("tn_in", 1))
            load(sp, "ld_t", *((t_w[n], A["L1_attn_W" + x]) for n, x in enumerate("qkvgo")), (t_cw, A["L1_attn_conv"]),
                 (t_W0, A["L1_attn_W_init"]), (t_tril, A["c_tril"]),
                 (t_gam, A["L1_attn_ln_gamma"]), (t_bet, A["L1_attn_ln_beta"]), shared="loads")

        def t_pe(pe):
            norm_pe(pe, "tn", xT, U[2])
            pe.wait_ge(*S.at("tn_out", 2))
            pe.wait_ge(*S.at("ld_t", dma_n["ld_t"]))
            dense_pe(pe, "tp", [(P, [(t_w[n][:, k, m * P:(m + 1) * P], half(U[1], k, h)) for k in range(DC)])
                                for n in range(4) for m in range(DC) for h in range(NH)], "a" * 16, list(range(8)))
            pe.wait_ge(*S.at("tp_ev_a", 16))
            for n in range(4):
                pe.wait_ge(S["t_sq"], n + 1)
                for t in range(TT):
                    o = (n // 2) * P + t * XH + (n % 2) * HPC
                    mm = nc.tensor.matmul(ps[:, 4, o:o + HPC], t_sq[n // 2][:, n % 2, t * P:(t + 1) * P], hmask,
                                          start=True, stop=True)
            mm.then_inc(S["t_ss"], 1)
            pe.wait_ge(S["t_rn"], 1)
            for g in range(8):
                n, c, h = g // 4, (g // 2) % 2, g % 2
                if g >= 4:
                    pe.wait_ge(S["t_qk"], g - 3)
                for t in range(4 * h, 4 * h + 4):
                    mm = nc.tensor.transpose(ps[:, g % 4, (t % 4) * P:(t % 4 + 1) * P],
                                             t_rep[:, n, t, c * P:(c + 1) * P], ident)
                mm.then_inc(S["t_nrm"], 1)
            pe.wait_ge(S["t_silu"], 6)
            for t in range(TT):
                for c in range(DC):
                    o = (t % 2) * D + c * P
                    mm = nc.tensor.transpose(ps[:, 4 + (t // 2 + 1) % 4, o:o + P], t_x[2][:, c, t * P:(t + 1) * P], ident)
                if t % 2:
                    mm.then_inc(S["t_vT"], 1)
            pe.wait_ge(S["t_vev"], 4)
            pe.wait_ge(S["t_qk"], 8)

            def sc(t):
                for b in range(4):
                    if t:
                        pe.wait_ge(S["t_mask"], 4 * (t - 1) + b + 1)
                    pe.wait_ge(S["t_qm"], 2 * t + b // 2 + 1)
                    nc.tensor.matmul(ps[:, b, :], t_x[1][:, b // 2, t * P:(t + 1) * P],
                                     t_qm[t % 2][:, b // 2, 4 * (b % 2):4 * (b % 2) + 4, :].rearrange("p h q -> p (h q)"),
                                     start=True, stop=True).then_inc(S["t_s"], 1)

            sc(0)
            for t in range(TT):
                if t + 1 < TT:
                    sc(t + 1)
                if t >= 2:
                    pe.wait_ge(S["t_oev"], t - 1)
                for c in range(DC):
                    nc.tensor.matmul(ps[:, 4 + t % 2, c * P:(c + 1) * P], t_x[0][:, c, t * P:(t + 1) * P],
                                     t_W0[:, c, :], start=True, stop=False, skip_group_check=True)
                    for hd in range(HPC * c, HPC * (c + 1)):
                        if hd % 4 == 0:
                            pe.wait_ge(S["t_mask"], 4 * t + hd // 4 + 1)
                        mm = nc.tensor.matmul(ps[:, 4 + t % 2, hd * DK:(hd + 1) * DK], t_S[t % 2][:, hd, :],
                                              t_v[:, t, hd * DK:(hd + 1) * DK], start=False,
                                              stop=True, skip_group_check=True)
                mm.then_inc(S["t_om"], 1)
            pe.wait_ge(S["t_ln"], 1)
            for t in range(TT):
                for c in range(DC):
                    mm = nc.tensor.transpose(ps[:, 2 * c + t // 4, (t % 4) * P:(t % 4 + 1) * P],
                                             t_o[:, t, c * P:(c + 1) * P], ident)
            mm.then_inc(S["t_oT"], 1)
            pe.wait_ge(S["t_gate"], 4)
            dense_pe(pe, "to", [(P, [(t_w[4][:, k, m * P:(m + 1) * P], half(t_x[0], k, h)) for k in range(DC)])
                                for m in range(DC) for h in range(NH)], "dddd", [4, 5, 6, 7])

        def t_act(act):
            norm_act(act, "tn", U[1], U[2], 0)
            for g in range(16):
                n, m, h = g // 4, (g // 2) % 2, g % 2
                act.wait_ge(*S.at("tp_mm", g + 1))
                dst = (t_raw + [t_g])[n]
                nc.scalar.copy(half(dst, m, h), ps[:, g % 8, :]).then_inc(S["tp_ev_a"], 1)
            for n in range(6):
                act.wait_ge(S["t_conv"], n + 1)
                x = t_x[n // 2][:, n % 2, :]
                nc.scalar.activation(x, x, ACT.Silu).then_inc(S["t_silu"], 1)
            for n in range(4):
                act.wait_ge(S["t_silu"], n + 1)
                nc.scalar.activation(t_sq[n // 2][:, n % 2, :], t_x[n // 2][:, n % 2, :],
                                     ACT.Square).then_inc(S["t_sq"], 1)
            act.wait_ge(S["t_ss"], 1)
            nc.scalar.activation(t_ns[:, 0, :], ps[:, 4, 0:2 * P], ACT.Sqrt, bias=eps[:, 3:4]).then_inc(S["t_root"], 1)
            for n in range(4):
                act.wait_ge(S["t_vT"], n + 1)
                nc.scalar.copy(t_v[:, 2 * n:2 * n + 2, :].rearrange("p a b -> p (a b)"), ps[:, 4 + (n + 1) % 4, :])\
                    .then_inc(S["t_vev"], 1)
            for t in range(TT):
                act.wait_ge(S["t_om"], t + 1)
                nc.scalar.copy(t_o[:, t, :], ps[:, 4 + t % 2, 0:D]).then_inc(S["t_oev"], 1)
            act.wait_ge(S["t_cen"], 1)
            nc.scalar.activation(t_osq, t_o, ACT.Square).then_inc(S["t_osq"], 1)
            act.wait_ge(S["t_var"], 1)
            nc.scalar.activation(t_st[:, 1, :], t_st[:, 0, :], ACT.Sqrt, bias=eps[:, 0:1],
                                 scale=1.0 / DK).then_inc(S["t_sd"], 1)

        def t_dve(ch):
            dve, ln = ch.eng, ch.link
            v = nc.vector
            norm_dve(ch, "tn", xT, U[1], U[1])
            dve.wait_ge(*S.at("ld_t", dma_n["ld_t"]))
            for n in range(6):
                w, c = n // 2, n % 2
                dve.wait_ge(*S.at("tp_ev_a", 2 * n + 2))
                x, y = t_raw[w][:, c, :], t_x[w][:, c, :]
                x3, y3 = (z.rearrange("p (b t) -> p b t", t=L) for z in (x, y))
                ln(v.scalar_tensor_tensor(out=y, in0=x, scalar=t_cw[:, w, c, KW - 1:KW], in1=x,
                                          op0=ALU.mult, op1=ALU.add))
                for s in range(1, KW):
                    ins = v.scalar_tensor_tensor(out=y3[:, :, s:], in0=x3[:, :, :L - s],
                                                 scalar=t_cw[:, w, c, KW - 1 - s:KW - s], in1=y3[:, :, s:],
                                                 op0=ALU.mult, op1=ALU.add)
                    if s < KW - 1:
                        ln(ins)
                ins.then_inc(S["t_conv"], 1)
            dve.wait_ge(S["t_root"], 1)
            ln(v.reciprocal(t_ns[:, 1, :], t_ns[:, 0, :]))
            v.tensor_copy(t_rep.rearrange("p n t (h d) -> p (n t h) d", d=DK),
                          t_ns[:, 1, :].unsqueeze(2).broadcast_to([P, 2 * P, DK])).then_inc(S["t_rn"], 1)
            for g in range(8):
                x = half(t_x[g // 4], (g // 2) % 2, g % 2)
                dve.wait_ge(S["t_nrm"], g + 1)
                v.tensor_tensor(x, x, ps[:, g % 4, :], ALU.mult).then_inc(S["t_qk"], 1)
            for t in range(TT):
                if t >= 2:
                    dve.wait_ge(S["t_om"], t - 1)
                for b in range(4):
                    dve.wait_ge(S["t_s"], 4 * t + b + 1)
                    v.tensor_tensor(t_S[t % 2][:, 4 * b:4 * b + 4, :],
                                    ps[:, b, :].rearrange("p (h q) -> p h q", h=4),
                                    t_tril.unsqueeze(1).broadcast_to([P, 4, P]), ALU.mult).then_inc(S["t_mask"], 1)
            dve.wait_ge(S["t_oev"], TT)
            o4 = t_o.rearrange("p t (h d) -> p (t h) d", d=DK)
            q4 = t_osq.rearrange("p t (h d) -> p (t h) d", d=DK)
            G = TT * XH

            def wide(s):
                return s.unsqueeze(2).broadcast_to([P, G, DK])
            ln(v.tensor_reduce(t_st[:, 0, :], o4, AX.X, ALU.add))
            ln(v.tensor_scalar(t_st[:, 1, :], t_st[:, 0, :], 1.0 / DK, None, ALU.mult))
            v.tensor_tensor(o4, o4, wide(t_st[:, 1, :]), ALU.subtract).then_inc(S["t_cen"], 1)
            dve.wait_ge(S["t_osq"], 1)
            v.tensor_reduce(t_st[:, 0, :], q4, AX.X, ALU.add).then_inc(S["t_var"], 1)
            dve.wait_ge(S["t_sd"], 1)
            ln(v.reciprocal(t_st[:, 0, :], t_st[:, 1, :]))
            ln(v.tensor_tensor(o4, o4, wide(t_st[:, 0, :]), ALU.mult))
            ln(v.tensor_tensor(o4, o4, t_gam.unsqueeze(1).broadcast_to([P, G, DK]), ALU.mult))
            v.tensor_tensor(o4, o4, t_bet.unsqueeze(1).broadcast_to([P, G, DK]), ALU.add).then_inc(S["t_ln"], 1)
            dve.wait_ge(S["t_oT"], 1)
            for g in range(4):
                v.tensor_tensor(half(t_x[0], g // 2, g % 2), ps[:, g, :], half(t_g, g // 2, g % 2),
                                ALU.mult).then_inc(S["t_gate"], 1)
            for g in range(4):
                dve.wait_ge(*S.at("to_mm", g + 1))
                ln(v.tensor_tensor(half(xT, g // 2, g % 2), half(xT, g // 2, g % 2), ps[:, 4 + g, :], ALU.add))

        def t_pool(pool):
            pool.wait_ge(S["t_qk"], 4)
            for t in range(TT):
                for c in range(DC):
                    if t >= 2:
                        pool.wait_ge(S["t_s"], 4 * (t - 2) + 2 * c + 2)
                    nc.gpsimd.tensor_tensor(t_qm[t % 2][:, c],
                                            t_x[0][:, c, t * P:(t + 1) * P].unsqueeze(1).broadcast_to([P, HPC, P]),
                                            hmask.unsqueeze(2).broadcast_to([P, HPC, P]),
                                            ALU.mult).then_inc(S["t_qm"], 1)

        FC = FH // P
        g_w1 = [view(21 * K + 1024 * j, DC, FH) for j in range(2)]
        g_w2 = [view(23 * K + 1024 * j, FC, D) for j in range(2)]
        g_b1 = [view(25 * K + 16 * j, FC) for j in range(2)]
        g_b2 = view(25 * K + 64, D)
        g_sa = view(26 * K, 2, HALF)
        g_h = [view(27 * K + 2048 * j, FC, HALF) for j in range(2)]

        def g_load(sp):
            sp.wait_ge(*S.at("gn_in", 1))
            load(sp, "ld_g", (f_R["w"], A["L1_ffn_gate_w"]), (f_R["b"], A["L1_ffn_gate_b"]), (g_b2[0:E], A["L1_ffn_b2"]), shared="loads")

            def expert(e, j):
                for dst, src in ((g_w1[j], "w1"), (g_w2[j], "w2"), (g_b1[j].unsqueeze(1), "b1")):
                    sp.dma_start(dst, A["L1_ffn_" + src][:, bass.ds(e, 1)].rearrange("p a k f -> p (a k) f"))\
                        .then_inc(S[f"ge_wt{j}"], 16)
            expert(0, 0)
            expert(1, 1)
            with sp.Fori(1, E // 2) as i:
                for j in range(2):
                    sp.wait_ge(S["ge_w2"], 4 * i + 2 * j - 2)
                    expert(2 * i + j, j)

        def g_pe(pe):
            norm_pe(pe, "gn", xT, U[2])
            pe.wait_ge(*S.at("gn_out", 2))
            pe.wait_ge(*S.at("ld_g", dma_n["ld_g"]))
            route_pe(pe, "gr", f_R, U[1])

            def up(v, h, j, e):
                for f in range(FC):
                    r = 4 * v + f
                    if not isinstance(v, int) or r >= 2:
                        pe.wait_ge(S["ge_sa"], r - 1)
                    for k in range(DC):
                        mm = nc.tensor.matmul(ps[:, 4 + f % 2, :], g_w1[j][:, k, f * P:(f + 1) * P],
                                              half(U[1], k, h), start=(k == 0), stop=(k == 1))
                    mm.then_inc(S["ge_a"], 1)
                    if f == 0:
                        if not isinstance(v, int) or v >= 2:
                            pe.wait_ge(S["ge_h"], 4 * v - 4)
                        weight_pe(f_R, e, h).then_inc(S["ge_c"], 1)

            def down(v, h, j, stop):
                pe.wait_ge(S["ge_h"], 4 * v + 4)
                for m in range(DC):
                    for f in range(FC):
                        mm = nc.tensor.matmul(ps[:, 2 * m + h, :], g_w2[j][:, f, m * P:(m + 1) * P], g_h[h][:, f, :],
                                              start=False, stop=stop and f == FC - 1, skip_group_check=True)
                mm.then_inc(S["ge_w2"], 1)

            pe.wait_ge(S["gr_part"], 1)
            for m in range(DC):
                for h in range(NH):
                    nc.tensor.matmul(ps[:, 2 * m + h, :], g_b2[0:E, m * P:(m + 1) * P],
                                     f_R["cT"][0:E, h * HALF:(h + 1) * HALF], start=True, stop=False,
                                     skip_group_check=True)

            def expert_pair(i, first_pair):
                for j in range(2):
                    v = 4 * i + 2 * j
                    pe.wait_ge(*S.at(f"ge_wt{j}", 48 * i + 48))
                    up(v, 0, j, 2 * i + j)
                    if not (first_pair and j == 0):
                        down(v - 1, 1, 1 - j, False)
                    up(v + 1, 1, j, 2 * i + j)
                    down(v, 0, j, False)
            expert_pair(0, True)
            with pe.Fori(1, E // 2) as i:
                expert_pair(i, False)
            down(2 * E - 1, 1, 1, True)

        def g_act(act):
            norm_act(act, "gn", U[1], U[2], 0)
            route_act(act, "gr", f_R, False)

            def relu(r, f, j):
                act.wait_ge(S["ge_a"], r + 1)
                if not isinstance(r, int) or r >= 2:
                    act.wait_ge(S["ge_h"], r - 1)
                nc.scalar.activation(g_sa[:, f % 2, :], ps[:, 4 + f % 2, :], ACT.Relu,
                                     bias=g_b1[j][:, f:f + 1]).then_inc(S["ge_sa"], 1)

            def pair(i):
                for j in range(2):
                    act.wait_ge(*S.at(f"ge_wt{j}", 48 * i + 48))
                    for n in range(2 * FC):
                        relu(16 * i + 8 * j + n, n % FC, j)
            pair(0)
            with act.Fori(1, E // 2) as i:
                pair(i)

        def g_dve(ch):
            dve = ch.eng
            norm_dve(ch, "gn", xT, U[1], U[1])
            dve.wait_ge(*S.at("ld_g", dma_n["ld_g"]))
            route_dve(ch, "gr", f_R, False)
            route_parts(ch, "gr", f_R)

            def product(v, h):
                dve.wait_ge(S["ge_c"], v + 1)
                if not isinstance(v, int) or v >= 2:
                    dve.wait_ge(S["ge_w2"], v - 1)
                for f in range(FC):
                    dve.wait_ge(S["ge_sa"], 4 * v + f + 1)
                    nc.vector.tensor_tensor(g_h[h][:, f, :], g_sa[:, f % 2, :], ps[:, 6 + h, :],
                                            ALU.mult).then_inc(S["ge_h"], 1)
            product(0, 0)
            product(1, 1)
            with dve.Fori(1, E) as i:
                for h in range(NH):
                    product(2 * i + h, h)
            dve.wait_ge(S["ge_w2"], 2 * E)
            for g in range(4):
                ch.link(nc.vector.tensor_tensor(half(xT, g // 2, g % 2), half(xT, g // 2, g % 2),
                                                ps[:, g, :], ALU.add))

        def g_pool(pool):
            route_pool(pool, "gr", f_R, "gn_in")


        stages = {0: (x_loads, x_pe, x_act, x_dve, x_pool)}
        stages[1] = (m_load, m_pe, m_act, m_dve, m_pool)
        stages[2] = (f_load, f_pe, f_act, f_dve, f_pool)
        stages[3] = (d_load, d_pe, d_act, d_dve, d_pool)
        stages[4] = (t_load, t_pe, t_act, t_dve, t_pool)
        stages[5] = (g_load, g_pe, g_act, g_dve, g_pool)
        block = ctx.enter_context(nc.Block())

        @block.sync
        def _(sp):
            x_load(sp)
            for s in range(first, last + 1):
                stages[s][0](sp)
            sp.wait_ge(S["all_done"], 1)
            sp.dma_start(out, xT).then_inc(S["stored"], 16)
            sp.wait_ge(S["stored"], 16)

        @block.vector
        def _(dve):
            ch = Chain(dve, S["dve_own"])
            dve.wait_ge(S["ld_const"], dma_n["ld_const"])
            ch.link(nc.vector.tensor_copy(identb, ident))
            for s in range(first, last + 1):
                signal(("xn", "mn", "fn", "dn", "tn", "gn")[s] + "_in")
                stages[s][3](ch)
            signal("all_done")

        @block.scalar
        def _(act):
            for s in range(first, last + 1):
                stages[s][2](act)

        @block.gpsimd
        def _(pool):
            for s in range(first, last + 1):
                stages[s][4](pool)

        @block.tensor
        def _(pe):
            for s in range(first, last + 1):
                stages[s][1](pe)


def feat(w):
    w = np.asarray(w)
    return np.ascontiguousarray(w.T.reshape(w.shape[1] // P, P, w.shape[0]).transpose(1, 0, 2))


def cols(v):
    v = np.asarray(v)
    return np.ascontiguousarray(v.reshape(-1, P).T)


def constants():
    def split(v):
        parts = []
        for _ in range(3):
            parts.append((v.view(np.uint32) & np.uint32(0xFFFF0000)).view(np.float32))
            v = v - parts[-1]
        return parts

    p = np.arange(P)
    c = {
        "c_ident": np.eye(P, dtype=np.float32),
        "c_mean": np.full((P, P), 1.0 / D, np.float32),
        "c_hmask": (p[:, None] // DK == np.arange(HPC)[None]).astype(np.float32),
        "c_ones": np.ones((P, 32), np.float32),
        "c_eps": np.tile(np.array([1e-5, np.finfo(np.float32).eps, 1e-6, 1e-12], np.float32), (P, 1)),
        "c_iota8": np.tile(np.arange(E, dtype=np.float32), (P, 1)),
    }
    slopes = np.array([2.0 ** (-8.0 * (i + 1) / XH) for i in range(XH)], np.float32)
    sl = np.repeat(slopes.reshape(4, 4), L, axis=1)
    qs = -(sl * np.tile(np.arange(L, dtype=np.float32), 4)[None])
    c["c_slope"] = np.ascontiguousarray(np.stack(split(sl) + split(qs)))
    pos = np.arange(SK, dtype=np.float32)
    c["c_pos"] = np.stack([pos] * 3 + [np.ones_like(pos)] * 3)
    hq = np.repeat(np.arange(HPC), L)
    c["c_dmask"] = np.tile((p[:, None] // DK == hq[None]).astype(np.float32), (1, DC))
    tok = p // L
    c["c_neg"] = np.where(tok[:, None] == tok[None], 0.0, -BIG).astype(np.float32)
    c["c_tril"] = ((tok[:, None] == tok[None]) & (p[:, None] <= p[None])).astype(np.float32)
    return c


def layout(inputs):
    a = {}
    a["x"] = feat(np.asarray(inputs["x"]).reshape(T, D))
    ctx = np.asarray(inputs["ctx_1024"])
    a["ctxT"] = feat(ctx.reshape(B * SK, D))
    a["ctx_lastT"] = feat(ctx[:, SK - 1])
    for n in ("w_q", "w_k", "w_v", "w_o"):
        a["L0_xattn_" + n] = feat(inputs["L0_xattn_" + n])
    a["L0_xattn_b_o"] = cols(inputs["L0_xattn_b_o"])
    pre = "L0_attn_"
    a[pre + "norm_w"] = cols(inputs[pre + "norm_w"])
    for n in ("W_in", "W_x", "W_out"):
        a[pre + n] = feat(inputs[pre + n])
    a[pre + "W_dt"] = np.ascontiguousarray(np.asarray(inputs[pre + "W_dt"]).T)
    for n in ("conv_b", "Dp", "b_dt"):
        a[pre + n] = cols(inputs[pre + n])
    a[pre + "conv_w"] = np.ascontiguousarray(np.asarray(inputs[pre + "conv_w"]).reshape(IC, P, KW).transpose(1, 0, 2))
    a[pre + "A_log"] = np.ascontiguousarray(np.asarray(inputs[pre + "A_log"]).reshape(IC, P, NS).transpose(1, 0, 2))
    pre = "L0_ffn_"
    a[pre + "Wq"], a[pre + "Wo"] = feat(inputs[pre + "Wq"]), feat(inputs[pre + "Wo"])
    k, v = feat(inputs[pre + "Wkc"]), feat(inputs[pre + "Wvc"])
    a[pre + "Wkv"] = np.concatenate([k, k, v, v], axis=2)
    a[pre + "g1"], a[pre + "g2"] = cols(inputs[pre + "g1"]), cols(inputs[pre + "g2"])
    a[pre + "Wr"] = feat(inputs[pre + "Wr"])
    a[pre + "expert_bias"] = np.ascontiguousarray(np.broadcast_to(np.asarray(inputs[pre + "expert_bias"]), (P, E)))
    a[pre + "sW13"] = np.concatenate([feat(inputs[pre + "sW1"]), feat(inputs[pre + "sW3"])], axis=2)
    a[pre + "sW2"] = feat(inputs[pre + "sW2"])
    a[pre + "eW13"] = np.stack([np.concatenate([feat(w1), feat(w3)], axis=2) for w1, w3 in
                                zip(np.asarray(inputs[pre + "eW1"]), np.asarray(inputs[pre + "eW3"]))], axis=1)
    a[pre + "eW2"] = np.stack([feat(w) for w in np.asarray(inputs[pre + "eW2"])], axis=1)
    rt = -(-SK // 3)
    back = np.concatenate([ctx[:, ::-1], np.zeros((B, 3 * rt - SK, D), np.float32)], axis=1)
    a["ctx_rows"] = np.ascontiguousarray(back.reshape(B, 3, rt, D).transpose(2, 0, 1, 3))
    pre = "L1_attn_"
    for x in "qkvgo":
        a[pre + "W" + x] = feat(inputs[pre + "W" + x])
    a[pre + "conv"] = np.stack([np.asarray(inputs[pre + "conv_" + x]).reshape(DC, P, KW).transpose(1, 0, 2)
                                for x in "qkv"], axis=1)
    w0 = np.zeros((P, DC, P), np.float32)
    for h in range(XH):
        r = DK * (h % HPC)
        w0[r:r + DK, h // HPC, r:r + DK] = np.asarray(inputs[pre + "W_init"])[0, h]
    a[pre + "W_init"] = w0
    for n in ("ln_gamma", "ln_beta"):
        a[pre + n] = np.ascontiguousarray(np.broadcast_to(np.asarray(inputs[pre + n]), (P, DK)))
    pre = "L1_ffn_"
    a[pre + "gate_w"] = feat(np.asarray(inputs[pre + "gate_w"]).T)
    a[pre + "gate_b"] = np.ascontiguousarray(np.broadcast_to(np.asarray(inputs[pre + "gate_b"]), (P, E)))
    a[pre + "w1"] = np.stack([feat(w.T) for w in np.asarray(inputs[pre + "w1"])], axis=1)
    a[pre + "w2"] = np.stack([feat(w.T) for w in np.asarray(inputs[pre + "w2"])], axis=1)
    a[pre + "b1"] = np.ascontiguousarray(np.asarray(inputs[pre + "b1"]).reshape(E, 1, FH // P, P).transpose(3, 0, 1, 2))
    a[pre + "b2"] = np.ascontiguousarray(np.asarray(inputs[pre + "b2"]))
    return a


def kernel(**inputs):
    import concourse.bacc as _bacc
    from concourse.bass_utils import run_bass_kernel_spmd as _run

    nc = _bacc.Bacc("TRN2", target_bir_lowering=False, num_devices=1)
    arrays = {**layout(inputs), **constants()}
    aps = {n: nc.dram_tensor(n, a.shape, mybir.dt.from_np(a.dtype), kind="ExternalInput").ap()
           for n, a in arrays.items()}
    out = nc.dram_tensor("out", (P, DC, T), F32, kind="ExternalOutput").ap()
    build(nc, aps, out)
    r = _run(nc, [arrays], core_ids=[0])
    got = np.asarray(r.results[0]["out"])
    return np.ascontiguousarray(got.transpose(2, 1, 0).reshape(B, L, D))
```

```python
from contextlib import ExitStack

import concourse.bass as bass
import numpy as np
from concourse import mybir

ALU = mybir.AluOpType
ACT = mybir.ActivationFunctionType
AX = mybir.AxisListType
F32 = mybir.dt.float32
BF16 = mybir.dt.bfloat16
U32 = mybir.dt.uint32

P = 128
B = 32
L = 32
T = B * L
D = 256
DC = D // P
HALF = 512
NH = T // HALF
TT = T // P
SK = 257
XH = 16
DK = D // XH
HPC = P // DK
DI = 512
IC = DI // P
NS = 64
KW = 4
E = 8
FH = 512
BIG = 1e30


NORMS = [(0, "xn", 2), (1, "mn", 2), (1, "mr", 0), (2, "fn", 2), (2, "fr", 0), (2, "f2", 0), (3, "dn", 2),
         (4, "tn", 2), (5, "gn", 2)]
DENSE = [(0, "xq", 4, 0, 4), (0, "xw", 4, 0, 0), (1, "mi", 8, 0, 8), (1, "mo", 4, 0, 0),
         (2, "fq", 6, 0, 6), (2, "fw", 4, 0, 0), (4, "tp", 16, 16, 0), (4, "to", 4, 0, 0)]


SHARED = ([(0, f"slot_ctx{j}", f"x_ctx{j}", 16 * (B // 2)) for j in range(2)]
         + [(0, "tile_qblk", "x_qblk", DC * B), (0, "tile_norm", "x_norm", B), (0, "tile_rec", "x_rec", B)]
         + [(0, "once_1", "x_vl", 1), (0, "once_2", "x_vlast", 1)]
         + [(1, "once_3", "m_neg", 1), (1, "once_4", "m_ea", 1), (1, "once_5", "m_ready", 1)]
         + [(2, f"slot_wt{j}", f"fe_wt{j}", 32 * (E // 2 + j)) for j in range(2)]
         + [(3, f"slot_ctx{j}", f"d_ctx{j}", 16 * (TT // 2)) for j in range(2)]
         + [(3, "tile_qblk", "d_ms", TT), (3, "tile_norm", "d_tm", TT), (3, "tile_rec", "d_add", TT)]
         + [(3, "once_3", "d_m2", 1), (3, "once_4", "d_bb", 1), (3, "once_5", "d_tsq", 1)]
         + [(4, "once_1", "t_ss", 1), (4, "once_2", "t_root", 1), (4, "once_3", "t_oT", NH), (4, "once_4", "t_ln", NH)]
         + [(5, f"slot_wt{j}", f"ge_wt{j}", 48 * (E // 2)) for j in range(2)])


class Sems:

    def __init__(self, nc, ctx, first):
        self.nc, self.ctx, self.made, self.base = nc, ctx, {}, {}
        self.count = {}
        for stage, n, means in NORMS:
            if stage >= first:
                for kind, events in (("in", 1), ("mean", means), ("xc", means), ("sq", NH), ("var", NH), ("sd", NH), ("rec", NH), ("bc", NH),
                                     ("out", NH if means else NH * DC)):
                    self.add(f"{n}_{kind}", f"norm_{kind}", events)
        for stage, n, groups, a, d in DENSE:
            if stage >= first:
                for kind, events in (("mm", groups), ("ev_a", a), ("ev_d", d)):
                    self.add(f"{n}_{kind}", f"dense_{kind}", events)
        for stage, shared, n, events in SHARED:
            if stage >= first:
                self.add(n, shared, events)

    def add(self, name, shared, events):
        total = self.count.get(shared, 0)
        self.base[name] = (shared, total)
        self.count[shared] = total + events

    def __getitem__(self, name):
        name = self.base.get(name, (name, 0))[0]
        if name not in self.made:
            self.made[name] = self.ctx.enter_context(self.nc.semaphore(name))
        return self.made[name]

    def at(self, name, n):
        return self[name], self.base.get(name, (name, 0))[1] + n


class Chain:

    def __init__(self, eng, sem):
        self.eng, self.sem, self.n = eng, sem, 0

    def link(self, ins):
        self.n += 1
        ins.then_inc(self.sem, 1)
        self.eng.wait_ge(self.sem, self.n)

    def step(self, ins):
        self.n += 1
        ins.then_inc(self.sem, 1)

    def sync(self):
        self.eng.wait_ge(self.sem, self.n)


def build(nc, A, out, first=0, last=5):
    ctx = ExitStack()
    with ctx:
        S = Sems(nc, ctx, first)
        ar = ctx.enter_context(nc.sbuf_tensor("arena", [P, 51 * 1024], F32))
        ps = ctx.enter_context(nc.psum_tensor("ps", [P, 8, HALF], F32))

        dist = nc.dram_tensor("dist", (TT, P, SK), F32, kind="Internal").ap()

        def view(off, *shape):
            n = int(np.prod(shape))
            v = ar[:, off:off + n]
            if len(shape) == 1:
                return v
            names = "abcd"[:len(shape)]
            return v.rearrange(f"p ({' '.join(names)}) -> p {' '.join(names)}", **dict(zip(names, shape)))

        def bview(off, *shape):
            n = int(np.prod(shape))
            v = ar[:, off:off + (n + 1) // 2].bitcast(BF16)
            if len(shape) == 1:
                return v
            names = "abcd"[:len(shape)]
            return v.rearrange(f"p ({' '.join(names)}) -> p {' '.join(names)}", **dict(zip(names, shape)))

        K = 1024
        xT = view(0, DC, T)
        CONST = 44 * K
        EXTRA = 46 * K + 64
        ident = view(CONST, P)
        mean_w = view(CONST + 128, P)
        hmask = view(CONST + 256, HPC)
        ones = view(CONST + 264, 32)
        eps = view(CONST + 424, 4)
        identb = bview(CONST + 428, P)
        iota8 = view(CONST + 492, E)
        U = [view(2 * K * n, DC, T) for n in range(23)]

        dma_n = {}

        def signal(name):
            nc.vector.memset(view(CONST + 500, 1), 0.0).then_inc(S[name], 1)

        def load(sp, name, *pairs, shared=None):
            if shared:
                S.add(name, shared, 16 * len(pairs))
            for dst, src in pairs:
                sp.dma_start(dst, src).then_inc(S[name], 16)
            dma_n[name] = 16 * len(pairs)

        def half(v, c, h):
            return v[:, c, h * HALF:(h + 1) * HALF]

        def dense_pe(pe, name, groups, owners, banks):
            nb = len(banks)
            for g, (rows, pairs) in enumerate(groups):
                if g >= nb:
                    o = owners[g - nb]
                    pe.wait_ge(*S.at(f"{name}_ev_{o}", owners[:g - nb + 1].count(o)))
                for k, (lhsT, rhs) in enumerate(pairs):
                    dst = ps[0:rows, banks[g % nb], 0:rhs.shape[-1]]
                    last_mm = nc.tensor.matmul(dst, lhsT, rhs, start=(k == 0), stop=(k == len(pairs) - 1))
                last_mm.then_inc(S[f"{name}_mm"], 1)

        n_sd = view(CONST + 2040, TT)
        n_r = view(CONST + 2032, TT)

        def norm_pe(pe, name, src, sq, rms=False):
            if not rms:
                pe.wait_ge(*S.at(f"{name}_in", 1))
                for h in range(NH):
                    for c in range(DC):
                        mm = nc.tensor.matmul(ps[:, h, :], mean_w, half(src, c, h), start=(c == 0), stop=(c == 1))
                    mm.then_inc(S[f"{name}_mean"], 1)
                pe.wait_ge(*S.at(f"{name}_xc", NH))
            for h in range(NH):
                pe.wait_ge(*S.at(f"{name}_sq", h + 1))
                for t in range(4 * h, 4 * h + 4):
                    for c in range(DC):
                        mm = nc.tensor.matmul(ps[:, h, t:t + 1], sq[:, c, t * P:(t + 1) * P], mean_w[:, 0:1],
                                              start=(c == 0), stop=(c == 1))
                mm.then_inc(S[f"{name}_var"], 1)
            for h in range(NH):
                pe.wait_ge(*S.at(f"{name}_rec", h + 1))
                for t in range(4 * h, 4 * h + 4):
                    mm = nc.tensor.transpose(ps[:, 2 + h, (t % 4) * P:(t % 4 + 1) * P],
                                             n_r[:, t:t + 1].broadcast_to([P, P]), ident)
                mm.then_inc(S[f"{name}_bc"], 1)

        def norm_act(act, name, src, sq, eps_n, rms=False):
            for h in range(NH):
                if rms:
                    act.wait_ge(*S.at(f"{name}_in", 1))
                else:
                    act.wait_ge(*S.at(f"{name}_xc", h + 1))
                nc.scalar.activation(sq[:, :, h * HALF:(h + 1) * HALF], src[:, :, h * HALF:(h + 1) * HALF],
                                     ACT.Square).then_inc(S[f"{name}_sq"], 1)
            for h in range(NH):
                act.wait_ge(*S.at(f"{name}_var", h + 1))
                nc.scalar.activation(n_sd[:, 4 * h:4 * h + 4], ps[:, h, 4 * h:4 * h + 4], ACT.Sqrt,
                                     bias=eps[:, eps_n:eps_n + 1]).then_inc(S[f"{name}_sd"], 1)

        def norm_dve(ch, name, src, xc, dst, rms=False, gain=None):
            dve = ch.eng
            if not rms:
                for h in range(NH):
                    dve.wait_ge(*S.at(f"{name}_mean", h + 1))
                    sl = slice(h * HALF, (h + 1) * HALF)
                    nc.vector.tensor_tensor(xc[:, :, sl], src[:, :, sl],
                                            ps[:, h:h + 1, :].broadcast_to([P, DC, HALF]),
                                            ALU.subtract).then_inc(S[f"{name}_xc"], 1)
                dve.wait_ge(*S.at(f"{name}_xc", NH))
            for h in range(NH):
                dve.wait_ge(*S.at(f"{name}_sd", h + 1))
                nc.vector.reciprocal(n_r[:, 4 * h:4 * h + 4], n_sd[:, 4 * h:4 * h + 4]).then_inc(S[f"{name}_rec"], 1)
            for h in range(NH):
                dve.wait_ge(*S.at(f"{name}_bc", h + 1))
                sl = slice(h * HALF, (h + 1) * HALF)
                if gain is None:
                    nc.vector.tensor_tensor(dst[:, :, sl], xc[:, :, sl],
                                            ps[:, 2 + h:3 + h, :].broadcast_to([P, DC, HALF]),
                                            ALU.mult).then_inc(S[f"{name}_out"], 1)
                else:
                    for c in range(DC):
                        nc.vector.scalar_tensor_tensor(out=dst[:, c, sl], in0=xc[:, c, sl],
                                                       scalar=gain[:, c:c + 1], in1=ps[:, 2 + h, :],
                                                       op0=ALU.mult, op1=ALU.mult).then_inc(S[f"{name}_out"], 1)
            dve.wait_ge(*S.at(f"{name}_out", NH if gain is None else NH * DC))

        x0 = dict(
            wq=view(20 * K, DC, D), wk=view(20 * K + 512, DC, D), wv=view(21 * K, DC, D), wo=view(21 * K + 512, DC, D),
            bo=view(22 * K, DC),
            slope=bview(22 * K + 16, 4, P), pos=bview(22 * K + 16 + 256, SK + 1),
            cl=view(37 * K, DC, B), vl=view(37 * K + 64, DC, B),
            slope32=view(36 * K, 4, P), pos32=view(36 * K + 512, SK),
            dmask=view(22 * K + 512, HALF),
            ctx=[view(23 * K + 520 * j, DC, SK) for j in range(2)],
            kT=[view(25 * K + 520 * j, DC, SK) for j in range(2)],
            v=[view(27 * K + 512 * j, 2, D) for j in range(2)],
            plast=view(12 * K, 4, B), pick=view(12 * K + 128, 2, P), own=view(12 * K + 384, L),
            spread=view(8 * K, 4, B, L), last=view(14 * K, DC, T),
            qb=[view(28 * K + 512 + 512 * j, HALF) for j in range(2)],
            p=[view(30 * K + 1040 * j, 4, SK) for j in range(2)],
            pT=view(33 * K, 2, HALF),
            om=view(34 * K + 512, HALF),
            st=[view(35 * K + 16 * j, 3, 4) for j in range(2)],
        )
        Xn, Xq, Xo = U[1], U[2], U[3]

        def x_load(sp):
            load(sp, "ld_const", (ident, A["c_ident"]), (mean_w, A["c_mean"]), (hmask, A["c_hmask"]),
                 (ones, A["c_ones"]), (eps, A["c_eps"]),
                 (iota8, A["c_iota8"]), (xT, A["x"]))

        def x_loads(sp):
            load(sp, "ld_x", (x0["wq"], A["L0_xattn_w_q"]), (x0["wk"], A["L0_xattn_w_k"]),
                 (x0["wv"], A["L0_xattn_w_v"]), (x0["wo"], A["L0_xattn_w_o"]), (x0["bo"], A["L0_xattn_b_o"]), (x0["cl"], A["ctx_lastT"]),
                 (x0["slope32"][0:6], A["c_slope"]), (x0["pos32"][0:6], A["c_pos"]), (x0["dmask"], A["c_dmask"]),
                 (x0["pick"], A["c_pick"]), (x0["own"], A["c_own"]), shared="loads")

            def ctx_load(b, j):
                sp.dma_start(x0["ctx"][j], A["ctxT"][:, :, bass.ds(b * SK, SK)]).then_inc(S[f"x_ctx{j}"], 16)

            for j in range(2):
                ctx_load(j, j)
            with sp.Fori(1, B // 2) as i:
                for j in range(2):
                    sp.wait_ge(S["x_v"], 2 * i + j - 1)
                    ctx_load(2 * i + j, j)

        def x_pe(pe):
            pe.wait_ge(S["ld_const"], dma_n["ld_const"])
            norm_pe(pe, "xn", xT, Xo)
            pe.wait_ge(*S.at("ld_x", dma_n["ld_x"]))
            pe.wait_ge(*S.at("xn_out", 2))
            dense_pe(pe, "xq", [(P, [(x0["wq"][:, k, m * P:(m + 1) * P], half(Xn, k, h)) for k in range(DC)])
                                for m in range(DC) for h in range(NH)], "dddd", [4, 5, 6, 7])
            pe.wait_ge(*S.at("xq_ev_d", 4))
            for m in range(DC):
                for k in range(DC):
                    mm = nc.tensor.matmul(ps[:, 0, m * B:(m + 1) * B], x0["wv"][:, k, m * P:(m + 1) * P],
                                          x0["cl"][:, k, :], start=(k == 0), stop=(k == 1))
            mm.then_inc(S["x_vl"], 1)

            def proj(b, j, i):
                if not isinstance(b, int) or b >= 1:
                    pe.wait_ge(S["x_vev"], b)
                    pe.wait_ge(S["x_kev"], b)
                cx = x0["ctx"][j]
                pe.wait_ge(*S.at(f"x_ctx{j}", 16 * (i + 1)))
                for m in range(DC):
                    for k in range(DC):
                        mm = nc.tensor.matmul(ps[:, 4 + m, 0:SK], x0["wk"][:, k, m * P:(m + 1) * P], cx[:, k, :],
                                              start=(k == 0), stop=(k == 1))
                mm.then_inc(S["x_k"], 1)
                for t in range(2):
                    for k in range(DC):
                        mm = nc.tensor.matmul(ps[:, 6, t * D:(t + 1) * D], cx[:, k, t * P:(t + 1) * P],
                                              x0["wv"][:, k, :], start=(k == 0), stop=(k == 1))
                mm.then_inc(S["x_v"], 1)

            def scores(b, j):
                pe.wait_ge(S["x_kev"], b + 1)
                pe.wait_ge(S["x_qblk"], 2 * b + 2)
                if not isinstance(b, int) or b >= 1:
                    pe.wait_ge(S["x_exp"], 4 * b)
                for g in range(4):
                    nc.tensor.matmul(ps[:, g, 0:SK], x0["qb"][j][:, g * P:(g + 1) * P], x0["kT"][j][:, g // 2, :],
                                     start=True, stop=False)
                    mm = nc.tensor.matmul(ps[:, g, 0:SK], x0["slope"][0:6, g, :], x0["pos"][0:6, 0:SK],
                                          start=False, stop=True)
                mm.then_inc(S["x_s"], 1)

            def tail(b, j):
                pe.wait_ge(S["x_norm"], b + 1)
                for t in range(2):
                    for g in range(4):
                        mm = nc.tensor.transpose(ps[:, 4 + t, g * P:(g + 1) * P],
                                                 x0["p"][j][:, g, t * P:(t + 1) * P], ident)
                    mm.then_inc(S["x_pt"], 1)
                pe.wait_ge(S["x_or"], b + 1)
                for t in range(2):
                    pe.wait_ge(S[f"x_pt{t}ev"], b + 1)
                    for c in range(DC):
                        sl = slice(c * 256, (c + 1) * 256)
                        mm = nc.tensor.matmul(ps[:, 7, sl], x0["v"][j][:, t, c * P:(c + 1) * P], x0["pT"][:, t, sl],
                                              start=(t == 0 and c == 0), stop=(t == 1), skip_group_check=True)
                mm.then_inc(S["x_o"], 1)

            proj(0, 0, 0)
            pe.wait_ge(S["x_alibi"], 2)
            scores(0, 0)
            with pe.Fori(0, B // 2 - 1) as i:
                b = 2 * i
                proj(b + 1, 1, i)
                scores(b + 1, 1)
                tail(b, 0)
                proj(b + 2, 0, i + 1)
                scores(b + 2, 0)
                tail(b + 1, 1)
            proj(B - 1, 1, B // 2 - 1)
            scores(B - 1, 1)
            tail(B - 2, 0)
            tail(B - 1, 1)
            pe.wait_ge(S["x_or"], B + 1)
            for c in range(DC):
                for h in range(NH):
                    for k in range(2):
                        g = 2 * c + k
                        pe.wait_ge(S["x_spread"], g + 1)
                        mm = nc.tensor.matmul(ps[:, 4 + 2 * c + h, :], x0["pick"][:, k, :],
                                              x0["spread"][:, g, h * (B // NH):(h + 1) * (B // NH), :].rearrange("p b q -> p (b q)"),
                                              start=(k == 0), stop=(k == 1))
                    mm.then_inc(S["x_last"], 1)
            pe.wait_ge(S["x_whole"], 4)
            dense_pe(pe, "xw", [(P, [(x0["wo"][:, k, m * P:(m + 1) * P], half(Xo, k, h)) for k in range(DC)])
                                for m in range(DC) for h in range(NH)], "dddd", [0, 1, 2, 3])

        def x_act(act):
            act.wait_ge(S["ld_const"], dma_n["ld_const"])
            norm_act(act, "xn", Xn, Xo, 0)

            def keys(b, j):
                act.wait_ge(S["x_k"], b + 1)
                nc.scalar.copy(x0["kT"][j], ps[:, 4:6, 0:SK]).then_inc(S["x_kev"], 1)

            def exps(b, j):
                act.wait_ge(S["x_max"], b + 1)
                for g in range(4):
                    nc.scalar.activation(x0["p"][j][:, g, :], ps[:, g, 0:SK], ACT.Exp,
                                         bias=x0["st"][j][:, 0, g:g + 1],
                                         accum_out=x0["st"][j][:, 1, g:g + 1]).then_inc(S["x_exp"], 1)

            def turned(b):
                act.wait_ge(S["x_pt"], 2 * b + 1)
                act.wait_ge(S["x_or"], b + 1)
                nc.scalar.copy(x0["pT"][:, 0, :], ps[:, 4, :]).then_inc(S["x_pt0ev"], 1)

            keys(0, 0)
            exps(0, 0)
            with act.Fori(0, B // 2 - 1) as i:
                b = 2 * i
                keys(b + 1, 1)
                turned(b)
                exps(b + 1, 1)
                keys(b + 2, 0)
                turned(b + 1)
                exps(b + 2, 0)
            keys(B - 1, 1)
            turned(B - 2)
            exps(B - 1, 1)
            turned(B - 1)

        def x_dve(ch):
            dve = ch.eng
            dve.wait_ge(S["ld_const"], dma_n["ld_const"])
            norm_dve(ch, "xn", xT, Xn, Xn)
            for g in range(4):
                m, h = g // 2, g % 2
                dve.wait_ge(*S.at("xq_mm", g + 1))
                nc.vector.tensor_scalar(half(Xq, m, h), ps[:, 4 + g, :], 1.0 / DK ** 0.5, None,
                                        ALU.mult).then_inc(S["xq_ev_d"], 1)
            dve.wait_ge(*S.at("ld_x", dma_n["ld_x"]))
            dve.wait_ge(S["x_vl"], 1)
            nc.vector.tensor_copy(x0["vl"].rearrange("p c b -> p (c b)"), ps[:, 0, 0:DC * B]).then_inc(S["x_vlast"], 1)
            nc.vector.tensor_copy(x0["slope"][0:6], x0["slope32"][0:6]).then_inc(S["x_alibi"], 1)
            nc.vector.tensor_copy(x0["pos"][0:6, 0:SK], x0["pos32"][0:6]).then_inc(S["x_alibi"], 1)

            def values(b, j):
                dve.wait_ge(S["x_v"], b + 1)
                nc.vector.tensor_copy(x0["v"][j].rearrange("p a b -> p (a b)"), ps[:, 6, :]).then_inc(S["x_vev"], 1)

            def maxima(b, j):
                dve.wait_ge(S["x_s"], b + 1)
                nc.vector.tensor_reduce(x0["st"][j][:, 2, :], ps[:, 0:4, 0:SK], AX.X, ALU.max).then_inc(S["x_mx0"], 1)
                dve.wait_ge(S["x_mx0"], b + 1)
                nc.vector.tensor_scalar(x0["st"][j][:, 0, :], x0["st"][j][:, 2, :], -1.0, None,
                                        ALU.mult).then_inc(S["x_max"], 1)

            def sums(b, j):
                dve.wait_ge(S["x_exp"], 4 * b + 4)
                nc.vector.reciprocal(x0["st"][j][:, 2, :], x0["st"][j][:, 1, :]).then_inc(S["x_rec"], 1)

            def outs(b):
                dve.wait_ge(S["x_pt"], 2 * b + 2)
                nc.vector.tensor_copy(x0["pT"][:, 1, :], ps[:, 5, :]).then_inc(S["x_pt1ev"], 1)
                dve.wait_ge(S["x_o"], b + 1)
                nc.vector.tensor_tensor(x0["om"], ps[:, 7, :], x0["dmask"], ALU.mult).then_inc(S["x_om"], 1)
                dve.wait_ge(S["x_om"], b + 1)
                nc.vector.tensor_reduce(Xo[:, :, bass.ds(b * L, L)],
                                        x0["om"].rearrange("p (c h q) -> p c q h", c=DC, h=HPC),
                                        AX.X, ALU.add).then_inc(S["x_or"], 1)

            signal("x_or")
            values(0, 0)
            maxima(0, 0)
            sums(0, 0)
            with dve.Fori(0, B // 2 - 1) as i:
                b = 2 * i
                values(b + 1, 1)
                maxima(b + 1, 1)
                outs(b)
                sums(b + 1, 1)
                values(b + 2, 0)
                maxima(b + 2, 0)
                outs(b + 1)
                sums(b + 2, 0)
            values(B - 1, 1)
            maxima(B - 1, 1)
            outs(B - 2)
            sums(B - 1, 1)
            dve.wait_ge(S["x_norm"], B)
            for g in range(4):
                nc.vector.tensor_tensor(x0["spread"][:, g], x0["plast"][:, g, :].unsqueeze(2).broadcast_to([P, B, L]),
                                        x0["own"].unsqueeze(1).broadcast_to([P, B, L]), ALU.mult).then_inc(S["x_spread"], 1)
            outs(B - 1)
            dve.wait_ge(S["x_vlast"], 1)
            for g in range(4):
                c, h = g // 2, g % 2
                dve.wait_ge(S["x_last"], g + 1)
                ch.link(nc.vector.tensor_tensor(
                    half(x0["last"], c, h).rearrange("p (b q) -> p b q", q=L),
                    ps[:, 4 + g, :].rearrange("p (b q) -> p b q", q=L),
                    x0["vl"][:, c, h * (B // NH):(h + 1) * (B // NH)].unsqueeze(2).broadcast_to([P, B // NH, L]), ALU.mult))
                nc.vector.tensor_tensor(half(Xo, c, h), half(Xo, c, h), half(x0["last"], c, h),
                                        ALU.add).then_inc(S["x_whole"], 1)
            for g in range(4):
                m, h = g // 2, g % 2
                dve.wait_ge(*S.at("xw_mm", g + 1))
                ch.link(nc.vector.scalar_tensor_tensor(out=half(xT, m, h), in0=ps[:, g, :], scalar=x0["bo"][:, m:m + 1],
                                                       in1=half(xT, m, h), op0=ALU.add, op1=ALU.add))

        def x_pool(pool):
            pool.wait_ge(S["ld_const"], dma_n["ld_const"])
            pool.wait_ge(*S.at("xq_ev_d", 4))

            def qblk(b, j):
                if not isinstance(b, int) or b >= 2:
                    pool.wait_ge(S["x_s"], b - 1)
                for c in range(DC):
                    nc.gpsimd.tensor_tensor(
                        x0["qb"][j][:, c * 256:(c + 1) * 256].rearrange("p (h q) -> p h q", h=HPC),
                        Xq[:, c, bass.ds(b * L, L)].unsqueeze(1).broadcast_to([P, HPC, L]),
                        hmask.unsqueeze(2).broadcast_to([P, HPC, L]), ALU.mult).then_inc(S["x_qblk"], 1)

            def normed(b, j):
                pool.wait_ge(S["x_rec"], b + 1)
                nc.gpsimd.tensor_tensor(x0["plast"][:, :, bass.ds(b, 1)], x0["p"][j][:, :, SK - 1:SK],
                                        x0["st"][j][:, 2, :].unsqueeze(2), ALU.mult)
                nc.gpsimd.tensor_tensor(x0["p"][j][:, :, 0:SK - 1], x0["p"][j][:, :, 0:SK - 1],
                                        x0["st"][j][:, 2, :].unsqueeze(2).broadcast_to([P, 4, SK - 1]),
                                        ALU.mult).then_inc(S["x_norm"], 1)

            qblk(0, 0)
            qblk(1, 1)
            normed(0, 0)
            with pool.Fori(0, B // 2 - 1) as i:
                b = 2 * i
                qblk(b + 2, 0)
                normed(b + 1, 1)
                qblk(b + 3, 1)
                normed(b + 2, 0)
            normed(B - 1, 1)

        m_xm = view(6 * K, IC, T)
        m_z = view(10 * K, IC, T)
        m_u = view(14 * K, IC, T)
        m_bb, m_cc, m_dt = view(18 * K, T), view(19 * K, T), view(40 * K + 512, T)
        m_part = bview(20 * K, 3, T)
        m_pick = bview(CONST + 1856, NS)
        m_delta = view(22 * K, IC, T)
        m_du = view(26 * K, IC, T)
        m_da = view(30 * K, 4, T)
        m_h = view(34 * K, 4, T)
        m_hc = view(38 * K, 4, T)
        m_cb = view(EXTRA + 2048, 2, HALF)
        m_win = view(42 * K, DC, 2 * DI)
        m_wx = view(38 * K, IC, 5 * 64)
        m_wdt = view(40 * K, DI)
        m_s = view(34 * K, IC, T)
        m_p = view(26 * K, IC, T)
        SM = CONST + 512
        m_wout = view(SM, IC, D)
        m_a = view(SM + 1024, IC, NS)
        m_cw = view(SM + 1280, IC, KW)
        m_cb1, m_dp, m_bdt, m_nw = (view(SM + 1296 + 4 * n, IC) for n in range(4))

        def m_load(sp):
            sp.wait_ge(*S.at("mn_in", 1))
            load(sp, "ld_m1", (m_nw[:, 0:DC], A["L0_attn_norm_w"]), (m_win, A["L0_attn_W_in"]))
            load(sp, "ld_m0", (m_cw, A["L0_attn_conv_w"]))
            load(sp, "ld_m", (m_cb1, A["L0_attn_conv_b"]), (m_dp, A["L0_attn_Dp"]), (m_bdt, A["L0_attn_b_dt"]),
                 (m_a, A["L0_attn_A_log"]), (m_wx, A["L0_attn_W_x"]),
                 (m_wdt[0:64], A["L0_attn_W_dt"]), (m_wout, A["L0_attn_W_out"]))

        MU = 2 * NS
        m_diag = view(EXTRA, IC, KW, P)

        def pair(v, cp, h):
            return v[:, 2 * cp:2 * cp + 2, h * HALF:(h + 1) * HALF]

        def two(v):
            return v.rearrange("p (c t) -> p c t", c=2)

        def z_bank(g):
            return IC * (g // IC) + (g + 3) % IC

        def m_pe(pe):
            norm_pe(pe, "mn", xT, U[2])
            norm_pe(pe, "mr", U[1], U[2], rms=True)
            pe.wait_ge(*S.at("mr_out", 4))
            pe.wait_ge(S["ld_m1"], dma_n["ld_m1"])
            dense_pe(pe, "mi", [(P, [(m_win[:, k, m * P:(m + 1) * P], half(U[2], k, h)) for k in range(DC)])
                                for h in range(NH) for m in range(IC)], "d" * 8, list(range(8)))

            def product(bank, rows, pairs, done):
                for k, (lhsT, rhs) in enumerate(pairs):
                    mm = nc.tensor.matmul(ps[0:rows, bank, :], lhsT, rhs, start=(k == 0), stop=(k == len(pairs) - 1))
                mm.then_inc(S[done], 1)
            pe.wait_ge(S["m_taps"], IC * KW)
            for h in range(NH):
                for c in range(IC):
                    g = IC * h + c
                    pe.wait_ge(*S.at("mi_ev_d", g + 1))
                    x3 = half(m_xm, c, h).rearrange("p (b t) -> p b t", t=L)
                    y3 = ps[:, g, :].rearrange("p (b t) -> p b t", t=L)
                    for s in range(KW):
                        mm = nc.tensor.matmul(y3[:, :, s:], m_diag[:, c, KW - 1 - s, :], x3[:, :, :L - s],
                                              start=(s == 0), stop=(s == KW - 1), skip_group_check=True)
                    mm.then_inc(S["mc_mm"], 1)
                pe.wait_ge(*S.at("ld_m", dma_n["ld_m"]))
                pe.wait_ge(*S.at("mc_ev_a", IC * h + IC))
                for n, (o, r) in enumerate(((0, 64), (64, P), (64 + P, P))):
                    product(IC * h + n, r, [(m_wx[:, k, o:o + r], half(m_u, k, h)) for k in range(IC)], "mx_mm")
                pe.wait_ge(*S.at("mx_ev_a", 3 * h + 1))
                for m in range(IC):
                    if m == 1:
                        pe.wait_ge(*S.at("mx_ev_a", 3 * h + 3))
                    product(IC * h + (m + 3) % IC, P, [(m_wdt[0:64, m * P:(m + 1) * P],
                                                        m_dt[0:64, h * HALF:(h + 1) * HALF])], "md_mm")
            for g in range(8):
                m, h = g // 2 + IC, g % 2
                pe.wait_ge(*S.at("md_ev_a", g + 1))
                product(z_bank(g), P, [(m_win[:, k, m * P:(m + 1) * P], half(U[2], k, h)) for k in range(DC)], "mz_mm")
            pe.wait_ge(S["m_parts"], 2 * NH)
            pe.wait_ge(*S.at("mz_ev_a", 8))

            def spread(nn, n, par, h):
                for k, (bank, done, used, per) in enumerate(((4, "m_b", "m_dbu", 2), (6, "m_c", "m_cc", 1))):
                    if not isinstance(nn, int) or nn >= 2:
                        pe.wait_ge(S[used], per * nn - per)
                    for part, lhsT in ((k, m_pick[:, bass.ds(n, 1)]), (2, identb[:, bass.ds(n + NS * k, 1)])):
                        mm = nc.tensor.matmul(ps[:, bank + par, :], lhsT.broadcast_to([P, P]),
                                              m_part[:, part, h * HALF:(h + 1) * HALF], start=(part == k), stop=(part == 2))
                    mm.then_inc(S[done], 1)

            def gather(w, n0, first_n, last_n):
                for cp in range(2):
                    pe.wait_ge(S["m_hc"], w + cp + 1)
                    for cc in range(2):
                        mm = nc.tensor.matmul(ps[:, 2 * cp + cc, :], ident,
                                              m_hc[:, 2 * n0 + cp, cc * HALF:(cc + 1) * HALF],
                                              start=first_n, stop=last_n, skip_group_check=True)
                    mm.then_inc(S["m_acc"], 1)

            for h in range(NH):
                o = NS * h
                if h:
                    pe.wait_ge(S["my_ev"], IC)
                spread(o, 0, 0, h)
                spread(o + 1, 1, 1, h)
                spread(o + 2, 2, 0, h)
                gather(2 * o, 0, True, False)
                with pe.Fori(1, NS // 2 - 1) as i:
                    spread(2 * i + (o + 1), 2 * i + 1, 1, h)
                    gather(4 * i + (2 * o - 2), 1, False, False)
                    spread(2 * i + (o + 2), 2 * i + 2, 0, h)
                    gather(4 * i + 2 * o, 0, False, False)
                spread(o + NS - 1, NS - 1, 1, h)
                for n in range(NS - 3, NS):
                    gather(2 * (o + n), n % 2, False, n == NS - 1)
            for h in range(NH):
                pe.wait_ge(S["m_gate"], 2 * h + 2)
                pe.wait_ge(S["m_dbu"], 2 * MU)
                pe.wait_ge(S["m_cc"], MU)
                for m in range(DC):
                    product(4 + 2 * h + m, P, [(m_wout[:, k, m * P:(m + 1) * P], half(m_xm, k, h)) for k in range(IC)],
                            "mo_mm")

        def m_act(act):
            act.wait_ge(S["ld_m0"], dma_n["ld_m0"])
            for c in range(IC):
                for j in range(KW):
                    nc.scalar.activation(m_diag[:, c, j, :], ident, ACT.Copy,
                                         scale=m_cw[:, c, j:j + 1]).then_inc(S["m_taps"], 1)
            norm_act(act, "mn", U[1], U[2], 0)
            act.wait_ge(*S.at("mn_out", 2))
            norm_act(act, "mr", U[1], U[2], 1, rms=True)
            act.wait_ge(*S.at("ld_m", dma_n["ld_m"]))
            nc.scalar.activation(m_a, m_a, ACT.Exp).then_inc(S["m_ea"], 1)
            for h in range(NH):
                sl = slice(h * HALF, (h + 1) * HALF)
                for c in range(IC):
                    g = IC * h + c
                    act.wait_ge(*S.at("mc_mm", g + 1))
                    nc.scalar.activation(half(m_u, c, h), ps[:, g, :], ACT.Silu,
                                         bias=m_cb1[:, c:c + 1]).then_inc(S["mc_ev_a"], 1)
                for n, dst in enumerate((m_dt[0:64, sl], m_bb[:, sl], m_cc[:, sl])):
                    act.wait_ge(*S.at("mx_mm", 3 * h + n + 1))
                    nc.scalar.copy(dst, ps[0:dst.shape[0], IC * h + n, :]).then_inc(S["mx_ev_a"], 1)
                for m in range(IC):
                    act.wait_ge(*S.at("md_mm", IC * h + m + 1))
                    bank = ps[:, IC * h + (m + 3) % IC, :]
                    nc.scalar.activation(half(m_delta, m, h), bank, ACT.Relu,
                                         bias=m_bdt[:, m:m + 1]).then_inc(S["m_relu"], 1)
                    nc.scalar.activation(half(m_s, m, h), bank, ACT.Abs,
                                         bias=m_bdt[:, m:m + 1]).then_inc(S["md_ev_a"], 1)
                act.wait_ge(*S.at("md_ev_a", IC * h + IC))
                nc.scalar.activation(m_s[:, :, sl], m_s[:, :, sl], ACT.Exp, scale=-1.0).then_inc(S["m_e"], 1)
            for g in range(8):
                act.wait_ge(*S.at("mz_mm", g + 1))
                nc.scalar.activation(half(m_z, g // 2, g % 2), ps[:, z_bank(g), :], ACT.Silu)\
                    .then_inc(S["mz_ev_a"], 1)

            def c_copy(nn, par):
                act.wait_ge(S["m_c"], nn + 1)
                if not isinstance(nn, int) or nn >= 2:
                    act.wait_ge(S["m_hc"], 2 * nn - 2)
                nc.scalar.copy(m_cb[:, par, :], ps[:, 6 + par, :]).then_inc(S["m_cc"], 1)

            def decay(w, slot, cp, n, h):
                if not isinstance(w, int) or w >= 4:
                    act.wait_ge(S["m_hs"], w - 3)
                for cc in range(2):
                    c = 2 * cp + cc
                    nc.scalar.activation(
                        m_da[:, slot, cc * HALF:(cc + 1) * HALF].rearrange("p (b t) -> p b t", t=L)[:, :, 1:L],
                        half(m_delta, c, h).rearrange("p (b t) -> p b t", t=L)[:, :, 1:L], ACT.Exp,
                        scale=m_a[:, c, bass.ds(n, 1)]).then_inc(S["m_dec"], 1)

            act.wait_ge(S["m_ready"], 1)
            act.wait_ge(S["m_neg"], 1)
            for h in range(NH):
                o = NS * h
                act.wait_ge(S["m_delta"], h + 1)
                for n0 in range(2):
                    for cp in range(2):
                        decay(2 * (o + n0) + cp, 2 * n0 + cp, cp, n0, h)
                    c_copy(o + n0, n0)
                with act.Fori(1, NS // 2) as i:
                    for n0 in range(2):
                        for cp in range(2):
                            decay(4 * i + (2 * o + 2 * n0 + cp), 2 * n0 + cp, cp, 2 * i + n0, h)
                        c_copy(2 * i + (o + n0), n0)

        LOG1P = (1.0, -0.49999982118, 0.33332559466, -0.24987269938, 0.19890744985, -0.16105680168,
                 0.12418411672, -0.08244141191, 0.04147793353, -0.01340739243, 0.00203021383)

        def m_dve(ch):
            dve = ch.eng
            norm_dve(ch, "mn", xT, U[1], U[1])
            signal("mr_in")
            dve.wait_ge(S["ld_m1"], dma_n["ld_m1"])
            norm_dve(ch, "mr", None, U[1], U[2], rms=True, gain=m_nw)
            for g in range(8):
                dve.wait_ge(*S.at("mi_mm", g + 1))
                nc.vector.tensor_copy(half(m_xm, g % IC, g // IC), ps[:, g, :]).then_inc(S["mi_ev_d"], 1)
            ch.link(nc.vector.tensor_tensor(m_pick, identb[:, 0:NS], identb[:, NS:P], ALU.add))
            dve.wait_ge(S["m_ea"], 1)
            nc.vector.tensor_scalar(m_a, m_a, -1.0, None, ALU.mult).then_inc(S["m_neg"], 1)
            lower, upper = slice(0, NS), slice(NS, P)
            for h in range(NH):
                e, p = (v[:, :, h * HALF:(h + 1) * HALF] for v in (m_s, m_p))
                dve.wait_ge(S["m_e"], h + 1)
                ch.link(nc.vector.tensor_scalar(p, e, LOG1P[-1], None, ALU.mult))
                for k in range(len(LOG1P) - 2, 0, -1):
                    ch.link(nc.vector.scalar_tensor_tensor(out=p, in0=p, scalar=LOG1P[k], in1=e,
                                                           op0=ALU.add, op1=ALU.mult))
                nc.vector.scalar_tensor_tensor(out=p, in0=p, scalar=LOG1P[0], in1=e,
                                               op0=ALU.add, op1=ALU.mult).then_inc(S["m_log"], 1)
                dve.wait_ge(*S.at("mx_ev_a", 3 * h + 3))
                sl = slice(h * HALF, (h + 1) * HALF)
                for k, (v, rows) in enumerate(((m_bb, lower), (m_cc, upper))):
                    ch.link(nc.vector.tensor_copy(m_part[:, k, sl], v[:, sl]))
                    ch.link(nc.vector.tensor_tensor(v[rows, sl], v[rows, sl], m_part[rows, k, sl], ALU.subtract))
                    ch.link(nc.vector.tensor_copy(m_part[rows, k, sl], v[rows, sl]))
                    ch.link(nc.vector.tensor_tensor(v[rows, sl], v[rows, sl], m_part[rows, k, sl], ALU.subtract))
                    nc.vector.tensor_copy(m_part[rows, 2, sl], v[rows, sl]).then_inc(S["m_parts"], 1)
            dve.wait_ge(S["m_delta"], 2)
            dve.wait_ge(S["m_ready"], 1)

            def inputs_of(nn, w, n0, h):
                dve.wait_ge(S["m_b"], nn + 1)
                for cp in range(2):
                    if not isinstance(w, int) or w >= 4:
                        dve.wait_ge(S["m_hc"], w + cp - 3)
                    nc.vector.tensor_tensor(two(m_h[:, 2 * n0 + cp, :]), pair(m_du, cp, h),
                                            ps[:, 4 + n0:5 + n0, :].broadcast_to([P, 2, HALF]),
                                            ALU.mult).then_inc(S["m_dbu"], 1)

            def scans(w, n0):
                for cp in range(2):
                    sl = 2 * n0 + cp
                    dve.wait_ge(S["m_dec"], 2 * w + 2 * cp + 2)
                    dve.wait_ge(S["m_dbu"], w + cp + 1)
                    nc.vector.tensor_tensor_scan(m_h[:, sl, :], m_da[:, sl, :], m_h[:, sl, :], 0.0,
                                                 ALU.mult, ALU.add).then_inc(S["m_hs"], 1)

            for h in range(NH):
                o = NS * h
                dve.wait_ge(S["m_dudone"], h + 1)
                for n0 in range(2):
                    inputs_of(o + n0, 2 * (o + n0), n0, h)
                    scans(2 * (o + n0), n0)
                with dve.Fori(1, NS // 2) as i:
                    for n0 in range(2):
                        inputs_of(2 * i + (o + n0), 4 * i + 2 * (o + n0), n0, h)
                        scans(4 * i + 2 * (o + n0), n0)
                dve.wait_ge(S["m_acc"], MU * (h + 1))
                for c in range(IC):
                    nc.vector.scalar_tensor_tensor(out=half(m_xm, c, h), in0=half(m_u, c, h),
                                                   scalar=m_dp[:, c:c + 1], in1=ps[:, c, :],
                                                   op0=ALU.mult, op1=ALU.add).then_inc(S["my_ev"], 1)
            dve.wait_ge(S["m_res"], 1)
            for g in range(4):
                m, h = g % 2, g // 2
                dve.wait_ge(*S.at("mo_mm", g + 1))
                ch.link(nc.vector.tensor_tensor(half(xT, m, h), half(xT, m, h), ps[:, 4 + g, :], ALU.add))

        def m_pool(pool):
            pool.wait_ge(*S.at("mn_out", 2))
            nc.gpsimd.tensor_tensor(xT, xT, U[1], ALU.add).then_inc(S["m_res"], 1)
            nc.gpsimd.memset(m_da.rearrange("p a t -> p (a t)"), 0.0).then_inc(S["m_ready"], 1)
            for h in range(NH):
                sl = slice(h * HALF, (h + 1) * HALF)
                pool.wait_ge(S["m_log"], h + 1)
                pool.wait_ge(S["m_relu"], IC * h + IC)
                nc.gpsimd.tensor_tensor(m_delta[:, :, sl], m_delta[:, :, sl], m_p[:, :, sl],
                                        ALU.add).then_inc(S["m_delta"], 1)
                pool.wait_ge(S["m_delta"], h + 1)
                nc.gpsimd.tensor_tensor(m_du[:, :, sl], m_delta[:, :, sl], m_u[:, :, sl],
                                        ALU.mult).then_inc(S["m_dudone"], 1)

            def used(nn, w, n0):
                pool.wait_ge(S["m_cc"], nn + 1)
                for cp in range(2):
                    pool.wait_ge(S["m_hs"], w + cp + 1)
                    if not isinstance(w, int) or w >= 4:
                        pool.wait_ge(S["m_acc"], w + cp - 3)
                    nc.gpsimd.tensor_tensor(two(m_hc[:, 2 * n0 + cp, :]), two(m_h[:, 2 * n0 + cp, :]),
                                            m_cb[:, n0, :].unsqueeze(1).broadcast_to([P, 2, HALF]),
                                            ALU.mult).then_inc(S["m_hc"], 1)

            for h in range(NH):
                o = NS * h
                for n0 in range(2):
                    used(o + n0, 2 * (o + n0), n0)
                with pool.Fori(1, NS // 2) as i:
                    for n0 in range(2):
                        used(2 * i + (o + n0), 4 * i + 2 * (o + n0), n0)
                pool.wait_ge(S["my_ev"], IC * (h + 1))
                for cp in range(2):
                    nc.gpsimd.tensor_tensor(pair(m_xm, cp, h), pair(m_xm, cp, h), pair(m_z, cp, h),
                                            ALU.mult).then_inc(S["m_gate"], 1)

        def router_areas(o):
            return dict(w=view(o, DC, E), b=view(o + 16, E), lg=view(o + 24, TT, E), pr=view(o + 88, TT, E),
                        m8=view(o + 152, TT, E), ix=view(o + 216, TT, E).bitcast(U32), ixf=view(o + 280, TT, E),
                        e1=view(o + 344, TT, E), e2=view(o + 408, TT, E), s=view(o + 472, 4, TT),
                        cT=view(o + 512, T), cS=view(o + 512 + T, T), part=bview(o + 512 + 2 * T, 3, T))

        def route_pe(pe, n, R, xf):
            for t in range(TT):
                for k in range(DC):
                    mm = nc.tensor.matmul(ps[:, 4, t * E:(t + 1) * E], xf[:, k, t * P:(t + 1) * P], R["w"][:, k, :],
                                          start=(k == 0), stop=(k == 1))
            mm.then_inc(S[n + "_lg"], 1)
            pe.wait_ge(S[n + "_cm"], 1)
            for t in range(TT):
                mm = nc.tensor.transpose(ps[0:E, 5 + t // 4, (t % 4) * P:(t % 4 + 1) * P], R["e1"][:, t, :], ident)
            mm.then_inc(S[n + "_cT"], 1)

        def route_act(act, n, R, renorm):
            act.wait_ge(S[n + "_sub"], 1)
            nc.scalar.activation(R["pr"], R["lg"], ACT.Exp).then_inc(S[n + "_exp"], 1)
            if renorm:
                act.wait_ge(S[n + "_d"], 1)
                nc.scalar.activation(R["s"][:, 2, :], R["s"][:, 1, :], ACT.Exp).then_inc(S[n + "_e2"], 1)

        def route_dve(ch, n, R, renorm):
            dve, ln = ch.eng, ch.link
            v = nc.vector

            def over_e(x):
                return x.unsqueeze(2).broadcast_to([P, TT, E])
            dve.wait_ge(S[n + "_lg"], 1)
            ln(v.tensor_tensor(R["lg"], ps[:, 4, 0:TT * E].rearrange("p (t e) -> p t e", e=E),
                               R["b"].unsqueeze(1).broadcast_to([P, TT, E]), ALU.add))
            ln(v.tensor_reduce(R["s"][:, 0, :], R["lg"], AX.X, ALU.max))
            v.tensor_tensor(R["lg"], R["lg"], over_e(R["s"][:, 0, :]), ALU.subtract).then_inc(S[n + "_sub"], 1)
            dve.wait_ge(S[n + "_exp"], 1)
            ln(v.tensor_reduce(R["s"][:, 0, :], R["pr"], AX.X, ALU.add))
            ln(v.reciprocal(R["s"][:, 0, :], R["s"][:, 0, :]))
            ln(v.tensor_tensor(R["pr"], R["pr"], over_e(R["s"][:, 0, :]), ALU.mult))
            for t in range(TT):
                ch.step(v.max(R["m8"][:, t, :], R["pr"][:, t, :]))
            ch.sync()
            for t in range(TT):
                ch.step(v.max_index(R["ix"][:, t, :], R["m8"][:, t, :], R["pr"][:, t, :]))
            ch.sync()
            ln(v.tensor_copy(R["ixf"], R["ix"]))
            w1, w2 = R["m8"][:, :, 0], R["m8"][:, :, 1]
            if renorm:
                v.tensor_tensor(R["s"][:, 1, :], w2, w1, ALU.subtract).then_inc(S[n + "_d"], 1)
                dve.wait_ge(S[n + "_e2"], 1)
                ln(v.tensor_scalar(R["s"][:, 1, :], R["s"][:, 2, :], 1.0, None, ALU.add))
                ln(v.reciprocal(R["s"][:, 0, :], R["s"][:, 1, :]))
                ln(v.tensor_tensor(R["s"][:, 3, :], R["s"][:, 2, :], R["s"][:, 0, :], ALU.mult))
                w1, w2 = R["s"][:, 0, :], R["s"][:, 3, :]
            for k, (w, e) in enumerate(((w1, "e1"), (w2, "e2"))):
                ln(v.tensor_tensor(R[e], iota8.unsqueeze(1).broadcast_to([P, TT, E]), over_e(R["ixf"][:, :, k]),
                                   ALU.is_equal))
                ln(v.tensor_tensor(R[e], R[e], over_e(w), ALU.mult))
            v.tensor_tensor(R["e1"], R["e1"], R["e2"], ALU.add).then_inc(S[n + "_cm"], 1)
            dve.wait_ge(S[n + "_cT"], 1)
            ln(v.tensor_copy(R["cT"][0:E, :], ps[0:E, 5:7, :].rearrange("p a b -> p (a b)")))

        def route_parts(ch, n, R):
            rest, part = R["cT"], R["part"]
            ch.eng.wait_ge(S[n + "_zero"], 1)
            for k in range(3):
                ins = nc.vector.tensor_copy(part[0:E, k, :], rest[0:E, :])
                if k == 2:
                    ins.then_inc(S[n + "_part"], 1)
                    break
                ch.link(ins)
                ch.link(nc.vector.tensor_tensor(R["cS"][0:E, :], rest[0:E, :], part[0:E, k, :], ALU.subtract))
                rest = R["cS"]

        def route_pool(pool, n, R, stage_in):
            pool.wait_ge(*S.at(stage_in, 1))
            nc.gpsimd.memset(R["part"].rearrange("p k t -> p (k t)"), 0.0).then_inc(S[n + "_zero"], 1)

        def weight_pe(R, e, h):
            for k in range(3):
                mm = nc.tensor.matmul(ps[:, 6 + h, :], identb[:, bass.ds(e, 1)].broadcast_to([P, P]),
                                      R["part"][:, k, h * HALF:(h + 1) * HALF], start=(k == 0), stop=(k == 2))
            return mm

        f_q = U[3]
        f_k = view(8 * K, T)
        f_v = view(9 * K, TT, P)
        f_o = U[5]
        f_S = [view(12 * K + 512 * j, 4, P) for j in range(2)]
        f_pT = [view(13 * K + 512 * j, HALF) for j in range(2)]
        f_st = [view(14 * K + 16 * j, 3, 4) for j in range(2)]
        f_neg = view(14 * K + 64, P)
        f_g = view(14 * K + 256, 2, DC)
        f_wq, f_wkv, f_wo = view(15 * K, DC, D), view(15 * K + 512, DC, 2 * P), view(16 * K, DC, D)
        f_R = router_areas(17 * K)
        f_w13 = [view(21 * K + 1024 * j, DC, 2 * D) for j in range(2)]
        f_w2 = [view(23 * K + 512 * j, DC, D) for j in range(2)]
        f_sa = view(24 * K, 2, HALF)
        f_sb = view(25 * K, HALF)
        f_h = [view(26 * K + 1024 * j, 2, HALF) for j in range(2)]

        def f_load(sp):
            sp.wait_ge(*S.at("fn_in", 1))
            load(sp, "ld_f", (f_wq, A["L0_ffn_Wq"]), (f_wkv, A["L0_ffn_Wkv"]), (f_wo, A["L0_ffn_Wo"]),
                 (f_g[:, 0, :], A["L0_ffn_g1"]), (f_g[:, 1, :], A["L0_ffn_g2"]), (f_neg, A["c_neg"]),
                 (f_R["w"], A["L0_ffn_Wr"]), (f_R["b"], A["L0_ffn_expert_bias"]), shared="loads")
            sp.dma_start(f_w13[1], A["L0_ffn_sW13"]).then_inc(S["fe_wt1"], 16)
            sp.dma_start(f_w2[1], A["L0_ffn_sW2"]).then_inc(S["fe_wt1"], 16)

            def expert(e, j):
                sp.dma_start(f_w13[j], A["L0_ffn_eW13"][:, bass.ds(e, 1)].rearrange("p a k f -> p (a k) f"))\
                    .then_inc(S[f"fe_wt{j}"], 16)
                sp.dma_start(f_w2[j], A["L0_ffn_eW2"][:, bass.ds(e, 1)].rearrange("p a k f -> p (a k) f"))\
                    .then_inc(S[f"fe_wt{j}"], 16)
            expert(0, 0)
            sp.wait_ge(S["fe_w2"], 2)
            expert(1, 1)
            with sp.Fori(1, E // 2) as i:
                for j in range(2):
                    sp.wait_ge(S["fe_w2"], 4 * i + 2 * j)
                    expert(2 * i + j, j)

        def f_pe(pe):
            norm_pe(pe, "fn", xT, U[2])
            norm_pe(pe, "fr", U[1], U[2], rms=True)
            pe.wait_ge(*S.at("fr_out", 4))
            pe.wait_ge(*S.at("ld_f", dma_n["ld_f"]))
            dense_pe(pe, "fq", [(P, [(w[:, k, m * P:(m + 1) * P], half(U[2], k, h)) for k in range(DC)])
                                for w, m in ((f_wq, 0), (f_wq, 1), (f_wkv, 0)) for h in range(NH)],
                     "d" * 6, list(range(6)))
            for t in range(TT):
                for k in range(DC):
                    mm = nc.tensor.matmul(ps[:, 6 + t // 4, (t % 4) * P:(t % 4 + 1) * P],
                                          U[2][:, k, t * P:(t + 1) * P], f_wkv[:, k, P:2 * P],
                                          start=(k == 0), stop=(k == 1))
                if t % 4 == 3:
                    mm.then_inc(S["f_v"], 1)
            pe.wait_ge(*S.at("fq_ev_d", 6))

            def sc(t):
                if t >= 2:
                    pe.wait_ge(S["f_sm"], t - 1)
                if t == 0:
                    pe.wait_ge(*S.at("fq_ev_d", 6))
                for hd in range(4):
                    r = slice(64 * (hd % 2), 64 * (hd % 2) + 64)
                    mm = nc.tensor.matmul(ps[:, 2 * (t % 2) + hd % 2, (hd // 2) * P:(hd // 2 + 1) * P],
                                          f_q[r, hd // 2, t * P:(t + 1) * P],
                                          f_k[r, t * P:(t + 1) * P], start=True, stop=True)
                mm.then_inc(S["f_s"], 1)

            def turn(t):
                pe.wait_ge(S["f_norm"], t + 1)
                for hd in range(4):
                    mm = nc.tensor.transpose(ps[:, 4 + t % 2, hd * P:(hd + 1) * P], f_S[t % 2][:, hd, :], ident)
                mm.then_inc(S["f_pt"], 1)

            def values(t):
                pe.wait_ge(S["f_ptev"], t + 1)
                if t >= 2:
                    pe.wait_ge(S["f_oev"], 2 * t - 2)
                nc.tensor.matmul(ps[:, 6 + t % 2, :], f_v[:, t, :], f_pT[t % 2], start=True,
                                 stop=True).then_inc(S["f_pv"], 1)

            pe.wait_ge(S["f_vev"], 2)
            sc(0)
            for t in range(TT):
                if t + 1 < TT:
                    sc(t + 1)
                turn(t)
                if t:
                    values(t - 1)
            values(TT - 1)
            pe.wait_ge(S["f_oev"], 2 * TT)
            dense_pe(pe, "fw", [(P, [(f_wo[:, k, m * P:(m + 1) * P], half(f_o, k, h)) for k in range(DC)])
                                for m in range(DC) for h in range(NH)], "dddd", [0, 1, 6, 7])
            norm_pe(pe, "f2", U[1], U[2], rms=True)
            pe.wait_ge(*S.at("f2_out", 4))
            route_pe(pe, "fr", f_R, U[2])

            def up(v, h, j, e):
                for f in range(2):
                    for part in range(2):
                        if not isinstance(v, int) or v or f:
                            pe.wait_ge(S[("fe_sa", "fe_sb")[part]], 2 * v + f)
                        for k in range(DC):
                            mm = nc.tensor.matmul(ps[:, 4 + part, :],
                                                  f_w13[j][:, k, part * D + f * P:part * D + (f + 1) * P],
                                                  half(U[2], k, h), start=(k == 0), stop=(k == 1))
                        mm.then_inc(S["fe_ab"], 1)
                    if f == 0 and e is not None:
                        if not isinstance(v, int) or v >= 2:
                            pe.wait_ge(S["fe_h"], 2 * v - 2)
                        weight_pe(f_R, e, h).then_inc(S["fe_c"], 1)

            def down(v, h, j, start, stop):
                pe.wait_ge(S["fe_h"], 2 * v + 2)
                for m in range(DC):
                    for f in range(2):
                        mm = nc.tensor.matmul(ps[:, 2 * m + h, :], f_w2[j][:, f, m * P:(m + 1) * P], f_h[h][:, f, :],
                                              start=start and f == 0, stop=stop and f == 1, skip_group_check=True)
                mm.then_inc(S["fe_w2"], 1)

            pe.wait_ge(S["fr_part"], 1)
            pe.wait_ge(*S.at("fe_wt1", 32))
            up(0, 0, 1, None)
            up(1, 1, 1, None)
            down(0, 0, 1, True, False)

            def expert_pair(i, first_pair):
                for j in range(2):
                    v = 4 * i + 2 + 2 * j
                    pe.wait_ge(*S.at(f"fe_wt{j}", 32 * i + 32 + 32 * j))
                    up(v, 0, j, 2 * i + j)
                    down(v - 1, 1, 1 - j, first_pair and j == 0, False)
                    up(v + 1, 1, j, 2 * i + j)
                    down(v, 0, j, False, False)
            expert_pair(0, True)
            with pe.Fori(1, E // 2) as i:
                expert_pair(i, False)
            down(2 * E + 1, 1, 1, False, True)

        def f_act(act):
            norm_act(act, "fn", U[1], U[2], 0)
            act.wait_ge(*S.at("fn_out", 2))
            norm_act(act, "fr", U[1], U[2], 2, rms=True)
            for n in range(2):
                act.wait_ge(S["f_v"], n + 1)
                nc.scalar.copy(f_v[:, 4 * n:4 * n + 4, :].rearrange("p a b -> p (a b)"), ps[:, 6 + n, :])\
                    .then_inc(S["f_vev"], 1)
            for t in range(TT + 1):
                if t < TT:
                    act.wait_ge(S["f_max"], t + 1)
                    for hd in range(4):
                        nc.scalar.activation(f_S[t % 2][:, hd, :], f_S[t % 2][:, hd, :], ACT.Exp,
                                             bias=f_st[t % 2][:, 0, hd:hd + 1],
                                             accum_out=f_st[t % 2][:, 1, hd:hd + 1]).then_inc(S["f_exp"], 1)
                if t >= 1:
                    act.wait_ge(S["f_pt"], t)
                    if t >= 3:
                        act.wait_ge(S["f_pv"], t - 2)
                    nc.scalar.copy(f_pT[(t - 1) % 2], ps[:, 4 + (t - 1) % 2, :]).then_inc(S["f_ptev"], 1)
            act.wait_ge(*S.at("f2_in", 1))
            norm_act(act, "f2", U[1], U[2], 2, rms=True)
            route_act(act, "fr", f_R, True)

            def gate(r, f):
                act.wait_ge(S["fe_ab"], 2 * r + 1)
                if not isinstance(r, int) or r >= 2:
                    act.wait_ge(S["fe_sb"], r - 1)
                nc.scalar.activation(f_sa[:, f, :], ps[:, 4, :], ACT.Silu).then_inc(S["fe_sa"], 1)
            for r in range(4):
                gate(r, r % 2)
            with act.Fori(1, E + 1) as i:
                for r in range(4):
                    gate(4 * i + r, r % 2)

        def f_dve(ch):
            dve = ch.eng
            norm_dve(ch, "fn", xT, U[1], U[1])
            signal("fr_in")
            dve.wait_ge(*S.at("ld_f", dma_n["ld_f"]))
            norm_dve(ch, "fr", None, U[1], U[2], rms=True, gain=f_g[:, 0, :])
            for g in range(6):
                dve.wait_ge(*S.at("fq_mm", g + 1))
                dst = half(f_q, g // 2, g % 2) if g < 4 else f_k[:, (g - 4) * HALF:(g - 3) * HALF]
                nc.vector.tensor_scalar(dst, ps[:, g, :], 0.125 if g < 4 else 1.0, None,
                                        ALU.mult).then_inc(S["fq_ev_d"], 1)

            def soft(t):
                st = f_st[t % 2]
                dve.wait_ge(S["f_s"], t + 1)
                if t >= 2:
                    dve.wait_ge(S["f_pt"], t - 1)
                nc.vector.tensor_tensor(f_S[t % 2].rearrange("p (o c) k -> p o c k", o=2),
                                        ps[:, 2 * (t % 2):2 * (t % 2) + 2, 0:2 * P].rearrange("p o (c k) -> p o c k", c=2),
                                        f_neg.unsqueeze(1).unsqueeze(1).broadcast_to([P, 2, 2, P]), ALU.add).then_inc(S["f_sm"], 1)
                dve.wait_ge(S["f_sm"], t + 1)
                ch.link(nc.vector.tensor_reduce(st[:, 2, :], f_S[t % 2], AX.X, ALU.max))
                nc.vector.tensor_scalar(st[:, 0, :], st[:, 2, :], -1.0, None, ALU.mult).then_inc(S["f_max"], 1)

            soft(0)
            for t in range(TT):
                if t + 1 < TT:
                    soft(t + 1)
                dve.wait_ge(S["f_exp"], 4 * t + 4)
                nc.vector.reciprocal(f_st[t % 2][:, 2, :], f_st[t % 2][:, 1, :]).then_inc(S["f_rec"], 1)
                if t >= 1:
                    heads_out(dve, t - 1)
            heads_out(dve, TT - 1)
            for g in range(4):
                m, h = g // 2, g % 2
                dve.wait_ge(*S.at("fw_mm", g + 1))
                ch.link(nc.vector.tensor_tensor(half(U[1], m, h), half(U[1], m, h),
                                                ps[:, (0, 1, 6, 7)[g], :], ALU.add))
            signal("f2_in")
            norm_dve(ch, "f2", None, U[1], U[2], rms=True, gain=f_g[:, 1, :])
            route_dve(ch, "fr", f_R, True)
            route_parts(ch, "fr", f_R)

            def product(v, r, h, f, e):
                dve.wait_ge(S["fe_sa"], r + 1)
                dve.wait_ge(S["fe_ab"], 2 * r + 2)
                nc.vector.tensor_tensor(f_sb, f_sa[:, f, :], ps[:, 5, :], ALU.mult).then_inc(S["fe_sb"], 1)
                dve.wait_ge(S["fe_sb"], r + 1)
                if not isinstance(v, int) or v >= 2:
                    dve.wait_ge(S["fe_w2"], v - 1)
                if e:
                    dve.wait_ge(S["fe_c"], v - 1)
                    ins = nc.vector.tensor_tensor(f_h[h][:, f, :], f_sb, ps[:, 6 + h, :], ALU.mult)
                else:
                    ins = nc.vector.tensor_copy(f_h[h][:, f, :], f_sb)
                ins.then_inc(S["fe_h"], 1)
                dve.wait_ge(S["fe_h"], r + 1)
            for h in range(NH):
                for f in range(2):
                    product(h, 2 * h + f, h, f, False)
            with dve.Fori(1, E + 1) as i:
                for h in range(NH):
                    for f in range(2):
                        product(2 * i + h, 4 * i + 2 * h + f, h, f, True)
            dve.wait_ge(S["f_res"], 1)
            dve.wait_ge(S["fe_w2"], 2 * E + 2)
            for g in range(4):
                ch.link(nc.vector.tensor_tensor(half(xT, g // 2, g % 2), half(xT, g // 2, g % 2),
                                                ps[:, g, :], ALU.add))

        def heads_out(dve, t):
            dve.wait_ge(S["f_pv"], t + 1)
            for o in range(2):
                r = slice(64 * o, 64 * o + 64)
                nc.vector.tensor_copy(f_o[r, :, t * P:(t + 1) * P],
                                      ps[r, 6 + t % 2, :].rearrange("p (o c q) -> p o c q", c=2, o=2)[:, o, :, :])\
                    .then_inc(S["f_oev"], 1)

        def f_pool(pool):
            route_pool(pool, "fr", f_R, "fn_in")
            for t in range(TT):
                pool.wait_ge(S["f_rec"], t + 1)
                nc.gpsimd.tensor_tensor(f_S[t % 2], f_S[t % 2],
                                        f_st[t % 2][:, 2, :].unsqueeze(2).broadcast_to([P, 4, P]),
                                        ALU.mult).then_inc(S["f_norm"], 1)
            pool.wait_ge(*S.at("f2_in", 1))
            nc.gpsimd.tensor_tensor(xT, xT, U[1], ALU.add).then_inc(S["f_res"], 1)

        IP = SK + 1
        d_m2 = U[3]
        d_xs = [view(34 * K + 256 * j, DC, P) for j in range(2)]
        SL = 4
        d_ctx = [view(26 * K + 2080 * j, DC, SL * SK) for j in range(2)]
        d_sq = [view(EXTRA + 2080 * j, DC, SL * SK) for j in range(2)]
        d_ss = [view(31 * K + 1040 * j, SL * SK) for j in range(2)]
        d_dt = [view(39 * K + 260 * j, SK) for j in range(2)]
        d_bb = view(40 * K, TT)
        d_R = view(8 * K, L + 1, IP)
        d_D = view(17 * K, L, SK)
        d_t = view(25 * K + 256, L, SK)
        d_from = bview(34 * K, L, 2, IP)
        d_up = bview(EXTRA, L, IP)
        d_V = bview(21 * K + 256, L, IP)
        d_E, d_VD = view(42 * K + 640, IP), view(33 * K + 300, 2, IP)
        d_M = view(8 * K, 3, B, L)
        RT = -(-SK // 3)
        ROWS = (RT, RT, SK - 2 * RT)
        d_ct = [view(26 * K + 3072 * j, SL, 3, D) for j in range(2)]
        d_ms = [view(12 * K + 384 * j, 3, P) for j in range(2)]
        d_tm = [view(13 * K + 256 * j, D) for j in range(2)]

        def d_load(sp):
            sp.wait_ge(*S.at("dn_in", 1))

            def ctx_load(g, j):
                sp.dma_start(d_ctx[j], A["ctxT"][:, :, bass.ds(g * (SL * SK), SL * SK)]).then_inc(S[f"d_ctx{j}"], 16)

            def keep(g, j):
                sp.wait_ge(S["d_sqrt"], g + 1)
                sp.dma_start(dist[bass.ds(g, 1)].rearrange("a p i -> (a p) i"), d_dt[j]).then_inc(S[f"d_out{j}"], 16)
            ctx_load(0, 0)
            ctx_load(1, 1)
            with sp.Fori(1, TT // 2) as i:
                for j in range(2):
                    sp.wait_ge(S["d_ab"], 2 * i + j - 1)
                    ctx_load(2 * i + j, j)
                    keep(2 * i + (j - 2), j)
            keep(TT - 2, 0)
            keep(TT - 1, 1)
            for j in range(2):
                sp.wait_ge(S[f"d_out{j}"], 16 * TT // 2)
            sp.dma_start(d_D[0:B].rearrange("p j i -> p (j i)"),
                         dist.rearrange("g (s j) i -> (g s) (j i)", j=L)).then_inc(S["d_back"], 16)

            def rows(g, j):
                sp.dma_start(d_ct[j][0:RT], A["ctx_rows"][:, bass.ds(g * SL, SL)]).then_inc(S[f"d_rows{j}"], 16)
            sp.wait_ge(S["d_choice"], 2 * L)
            rows(0, 0)
            rows(1, 1)
            with sp.Fori(1, TT // 2) as i:
                for j in range(2):
                    sp.wait_ge(S["d_exp"], 2 * i + j - 1)
                    rows(2 * i + j, j)

        def d_pe(pe):
            norm_pe(pe, "dn", xT, U[2])
            pe.wait_ge(*S.at("d_tsq", 1))
            for g in range(TT):
                for k in range(DC):
                    mm = nc.tensor.matmul(ps[:, 4, g:g + 1], U[2][:, k, g * P:(g + 1) * P], ones[:, 0:1],
                                          start=(k == 0), stop=(k == 1))
            mm.then_inc(S["d_bb"], 1)

            def tile(g, j, i):
                pe.wait_ge(S["d_xs"], g + 1)
                pe.wait_ge(*S.at(f"d_ctx{j}", 16 * i + 16))
                if not isinstance(g, int) or g >= 2:
                    pe.wait_ge(S["d_clip"], g - 1)
                for bi in range(SL):
                    own = slice(bi * SK, (bi + 1) * SK)
                    dst = ps[32 * bi:32 * bi + 32, j, 0:SK]
                    for k in range(DC):
                        nc.tensor.matmul(dst, d_xs[j][:, k, 32 * bi:32 * bi + 32], d_ctx[j][:, k, own],
                                         start=(k == 0), stop=False)
                    if bi == 0:
                        pe.wait_ge(S["d_ss"], g + 1)
                    mm = nc.tensor.matmul(dst, ones, d_ss[j][:, own], start=False, stop=True)
                mm.then_inc(S["d_ab"], 1)
            tile(0, 0, 0)
            tile(1, 1, 0)
            with pe.Fori(1, TT // 2) as i:
                for j in range(2):
                    tile(2 * i + j, j, i)
            for n in range(L):
                pe.wait_ge(S["d_v"], n + 1)
                j = L - 1 - n
                for t, rows in enumerate(ROWS):
                    mm = nc.tensor.transpose(
                        ps[0:rows, t, :].bitcast(BF16)[:, j * B:(j + 1) * B],
                        d_V[0:B, j, t * RT:t * RT + rows],
                        identb[0:B, 0:B])
                mm.then_inc(S["d_vT"], 1)
            
            def turn(g, j):
                pe.wait_ge(*S.at("d_tm", g + 1))
                if not isinstance(g, int) or g >= 2:
                    pe.wait_ge(*S.at("d_add", g - 1))
                for c in range(DC):
                    mm = nc.tensor.transpose(ps[:, 6 + j, c * P:(c + 1) * P], d_tm[j][:, c * P:(c + 1) * P], ident)
                mm.then_inc(S["d_tr"], 1)

            def expand(g, j, i):
                pe.wait_ge(*S.at("d_ms", g + 1))
                pe.wait_ge(S[f"d_rows{j}"], 16 * i + 16)
                if not isinstance(g, int) or g >= 2:
                    pe.wait_ge(*S.at("d_tm", g - 1))
                for bi in range(SL):
                    for t, rows in enumerate(ROWS):
                        mm = nc.tensor.matmul(ps[32 * bi:32 * bi + 32, 4 + j, 0:D],
                                              d_ms[j][0:rows, t, 32 * bi:32 * bi + 32], d_ct[j][0:rows, bi, t, :],
                                              start=(t == 0), stop=(t == 2))
                mm.then_inc(S["d_exp"], 1)
            expand(0, 0, 0)
            expand(1, 1, 0)
            turn(0, 0)
            with pe.Fori(1, TT // 2) as i:
                for j in range(2):
                    expand(2 * i + j, j, i)
                    turn(2 * i + (j - 1), 1 - j)
            turn(TT - 1, 1)

        def d_act(act):
            norm_act(act, "dn", U[1], U[2], 0)
            act.wait_ge(*S.at("dn_out", 2))
            nc.scalar.activation(U[2], U[1], ACT.Square).then_inc(S["d_tsq"], 1)

            def squares(g, j, i):
                act.wait_ge(*S.at(f"d_ctx{j}", 16 * i + 16))
                if not isinstance(g, int) or g >= 2:
                    act.wait_ge(S["d_ss"], g - 1)
                nc.scalar.activation(d_sq[j], d_ctx[j], ACT.Square).then_inc(S["d_sq"], 1)

            def root(g, j):
                act.wait_ge(S["d_clip"], g + 1)
                nc.scalar.activation(d_dt[j], d_dt[j], ACT.Sqrt).then_inc(S["d_sqrt"], 1)

            squares(0, 0, 0)
            squares(1, 1, 0)
            root(0, 0)
            with act.Fori(1, TT // 2) as i:
                for j in range(2):
                    squares(2 * i + j, j, i)
                    root(2 * i + (j - 1), 1 - j)
            root(TT - 1, 1)
            act.wait_ge(S["d_vT"], L)
            for t, rows in enumerate(ROWS):
                nc.scalar.copy(d_M[0:rows, t].rearrange("p b j -> p j b"),
                               ps[0:rows, t, :].bitcast(BF16).rearrange("p (j b) -> p j b", j=L)).then_inc(S["d_mev"], 1)
            act.wait_ge(S["d_mev"], 3)

            def path(g, j):
                nc.scalar.copy(d_ms[j][0:RT].rearrange("p t (b q) -> p t b q", q=L),
                               d_M[0:RT, :, bass.ds(g * SL, SL), :]).then_inc(S["d_ms"], 1)

            def evict(g, j):
                act.wait_ge(S["d_exp"], g + 1)
                if not isinstance(g, int) or g >= 2:
                    act.wait_ge(S["d_tr"], g - 1)
                nc.scalar.copy(d_tm[j], ps[:, 4 + j, 0:D]).then_inc(S["d_tm"], 1)
            path(0, 0)
            path(1, 1)
            evict(0, 0)
            path(2, 0)
            evict(1, 1)
            path(3, 1)
            with act.Fori(1, TT // 2 - 1) as i:
                for j in range(2):
                    evict(2 * i + j, j)
                    path(2 * i + j + 2, j)
            evict(TT - 2, 0)
            evict(TT - 1, 1)

        def d_dve(ch):
            dve = ch.eng
            norm_dve(ch, "dn", xT, U[1], U[1])
            nc.vector.tensor_scalar(d_m2, U[1], -2.0, None, ALU.mult).then_inc(S["d_m2"], 1)
            dve.wait_ge(*S.at("d_bb", 1))
            ch.link(nc.vector.tensor_copy(d_bb, ps[:, 4, 0:TT]))

            def clip(g, j):
                dve.wait_ge(S["d_ab"], g + 1)
                if not isinstance(g, int) or g >= 2:
                    dve.wait_ge(S[f"d_out{j}"], 8 * (g - j))
                nc.vector.tensor_scalar(d_dt[j], ps[:, j, 0:SK], d_bb[:, bass.ds(g, 1)], 0.0, ALU.add,
                                        ALU.max).then_inc(S["d_clip"], 1)
            clip(0, 0)
            clip(1, 1)
            with dve.Fori(1, TT // 2) as i:
                for j in range(2):
                    clip(2 * i + j, j)
            R, least = d_R[0:B], d_t[0:B]
            lf, dg, up = d_from[0:B, :, 0], d_from[0:B, :, 1], d_up[0:B]
            E_, VD = d_E[0:B], d_VD[0:B]
            ch.link(nc.vector.memset(R[:, 0, :], BIG))
            ch.link(nc.vector.memset(R[:, 0, 0:1], 0.0))
            ch.link(nc.vector.memset(R[:, 1:L + 1, 0:1], BIG))
            ch.link(nc.vector.memset(up[:, :, 0:1], 0.0))
            ch.link(nc.vector.memset(E_, 0.0))
            ch.link(nc.vector.memset(VD[:, 1, 0:1], 0.0))
            ch.link(nc.vector.memset(E_[:, 0:1], 1.0))
            dve.wait_ge(S["d_back"], 16)

            def choice(j, part):
                if j < 0:
                    return
                dve.wait_ge(S["d_least"], j + 1)
                dst, src = ((up, R[:, j + 1, 0:SK]), (dg, R[:, j, 0:SK]))[part]
                nc.vector.tensor_tensor(dst[:, j, IP - 1:0:-1], src, least[:, j, :], ALU.is_le).then_inc(S["d_choice"], 1)

            def least_of(j):
                nc.vector.tensor_tensor(least[:, j, :], least[:, j, :], R[:, j + 1, 0:SK], ALU.min).then_inc(S["d_least"], 1)
            for j in range(L):
                prev, cur = R[:, j, :], R[:, j + 1, :]
                nc.vector.tensor_tensor(least[:, j, :], prev[:, 1:IP], prev[:, 0:SK], ALU.min).then_inc(S["d_fwd"], 1)
                if j:
                    least_of(j - 1)
                choice(j - 2, 0)
                dve.wait_ge(S["d_fwd"], 2 * j + 1)
                nc.vector.tensor_tensor_scan(cur[:, 1:IP], least[:, j, :], d_D[0:B, j, :], BIG,
                                             ALU.min, ALU.add).then_inc(S["d_fwd"], 1)
                choice(j - 2, 1)
                dve.wait_ge(S["d_fwd"], 2 * j + 2)
            least_of(L - 1)
            for j in range(L - 2, L):
                for part in range(2):
                    choice(j, part)
            dve.wait_ge(S["d_choice"], 2 * L)
            ch.link(nc.vector.memset(d_M[64:96, 2].rearrange("p b j -> p (b j)"), 0.0))

            def sort_left(j):
                nc.vector.scalar_tensor_tensor(out=lf[:, j, 1:IP], in0=dg[:, j, 1:IP], scalar=0.0, in1=up[:, j, 1:IP],
                                               op0=ALU.is_equal, op1=ALU.is_gt).then_inc(S["d_sort"], 1)

            def sort_up(j):
                dve.wait_ge(S["d_sort"], 2 * (L - 1 - j) + 1)
                nc.vector.tensor_tensor(up[:, j, 1:IP], up[:, j, 1:IP], dg[:, j, 1:IP],
                                        ALU.is_gt).then_inc(S["d_sort"], 1)
            sort_left(L - 1)
            sort_up(L - 1)
            for n in range(L):
                j = L - 1 - n
                dve.wait_ge(S["d_sort"], 2 * n + 2)
                v = d_V[0:B, j, :]
                nc.vector.tensor_tensor_scan(v[:, 0:SK], up[:, j, 0:SK], E_[:, 0:SK], 0.0,
                                             ALU.mult, ALU.add).then_inc(S["d_v"], 1)
                if j:
                    sort_left(j - 1)
                dve.wait_ge(S["d_v"], n + 1)
                nc.vector.tensor_tensor(VD[:, :, 1:IP], v[:, 0:SK].unsqueeze(1).broadcast_to([B, 2, SK]),
                                        d_from[0:B, j, :, 1:IP],
                                        ALU.mult).then_inc(S["d_bw"], 1)
                if j:
                    sort_up(j - 1)
                dve.wait_ge(S["d_bw"], 2 * n + 1)
                nc.vector.tensor_tensor(E_[:, 0:SK], VD[:, 0, 1:IP], VD[:, 1, 0:SK], ALU.add).then_inc(S["d_bw"], 1)
                dve.wait_ge(S["d_bw"], 2 * n + 2)

            def add(g, j):
                dve.wait_ge(S["d_tr"], g + 1)
                dst = xT[:, :, bass.ds(g * P, P)]
                nc.vector.tensor_tensor(dst, dst, ps[:, 6 + j, 0:D].rearrange("p (c j) -> p c j", c=DC),
                                        ALU.add).then_inc(S["d_add"], 1)
            with dve.Fori(0, TT // 2) as i:
                for j in range(2):
                    add(2 * i + j, j)
            dve.wait_ge(*S.at("d_add", TT))

        def d_pool(pool):
            def slot(g, j):
                if not isinstance(g, int) or g >= 2:
                    pool.wait_ge(S["d_ab"], g - 1)
                nc.gpsimd.tensor_copy(d_xs[j], d_m2[:, :, bass.ds(g * P, P)]).then_inc(S["d_xs"], 1)
                pool.wait_ge(S["d_sq"], g + 1)
                nc.gpsimd.tensor_tensor(d_ss[j], d_sq[j][:, 0, :], d_sq[j][:, 1, :], ALU.add).then_inc(S["d_ss"], 1)
            pool.wait_ge(*S.at("d_m2", 1))
            slot(0, 0)
            slot(1, 1)
            with pool.Fori(1, TT // 2) as i:
                for j in range(2):
                    slot(2 * i + j, j)

        t_raw = [U[2], U[3], U[4]]
        t_g = U[5]
        t_x = [U[6], U[7], U[8]]
        t_sq = [U[9], U[10]]
        t_v = view(22 * K, TT, D)
        t_o = view(24 * K, TT, D)
        t_osq = view(18 * K, TT, D)
        t_qm = [view(26 * K + 2048 * j, DC, HPC, P) for j in range(2)]
        t_S = [view(30 * K + 2048 * j, XH, P) for j in range(2)]
        t_w = [view(34 * K + 512 * n, DC, D) for n in range(5)]
        t_W0 = view(37 * K, DC, P)
        t_tril = view(37 * K + 256, P)
        t_cw = view(37 * K + 384, 3, DC, KW)
        t_gam, t_bet = view(37 * K + 512, DK), view(37 * K + 528, DK)
        t_ns = view(38 * K, 2, 2 * P)
        t_rep = view(39 * K, 2, TT, D)
        t_st = view(37 * K + 544, 2, TT * XH)

        TG = TT * XH // NH

        def t_load(sp):
            sp.wait_ge(*S.at("tn_in", 1))
            load(sp, "ld_t", *((t_w[n], A["L1_attn_W" + x]) for n, x in enumerate("qkvgo")), (t_cw, A["L1_attn_conv"]),
                 (t_W0, A["L1_attn_W_init"]), (t_tril, A["c_tril"]),
                 (t_gam, A["L1_attn_ln_gamma"]), (t_bet, A["L1_attn_ln_beta"]), shared="loads")

        def t_pe(pe):
            norm_pe(pe, "tn", xT, U[2])
            pe.wait_ge(*S.at("tn_out", 2))
            pe.wait_ge(*S.at("ld_t", dma_n["ld_t"]))
            dense_pe(pe, "tp", [(P, [(t_w[n][:, k, m * P:(m + 1) * P], half(U[1], k, h)) for k in range(DC)])
                                for n in range(4) for m in range(DC) for h in range(NH)], "a" * 16, list(range(8)))
            pe.wait_ge(*S.at("tp_ev_a", 16))
            for n in range(4):
                pe.wait_ge(S["t_sq"], n + 1)
                for t in range(TT):
                    o = (n // 2) * P + t * XH + (n % 2) * HPC
                    mm = nc.tensor.matmul(ps[:, 4, o:o + HPC], t_sq[n // 2][:, n % 2, t * P:(t + 1) * P], hmask,
                                          start=True, stop=True)
            mm.then_inc(S["t_ss"], 1)
            pe.wait_ge(*S.at("t_root", 1))
            pe.wait_ge(S["t_silu"], 6)
            for t in range(TT):
                for c in range(DC):
                    o = (t % 2) * D + c * P
                    mm = nc.tensor.transpose(ps[:, 4 + (t // 2 + 1) % 4, o:o + P], t_x[2][:, c, t * P:(t + 1) * P], ident)
                if t % 2:
                    mm.then_inc(S["t_vT"], 1)
            pe.wait_ge(S["t_rn"], 1)
            for g in range(8):
                n, c, h = g // 4, (g // 2) % 2, g % 2
                if g >= 4:
                    pe.wait_ge(S["t_qk"], g - 3)
                for t in range(4 * h, 4 * h + 4):
                    mm = nc.tensor.transpose(ps[:, g % 4, (t % 4) * P:(t % 4 + 1) * P],
                                             t_rep[:, n, t, c * P:(c + 1) * P], ident)
                mm.then_inc(S["t_nrm"], 1)
            pe.wait_ge(S["t_vev"], 4)
            pe.wait_ge(S["t_qk"], 8)

            def sc(t):
                for b in range(4):
                    if t:
                        pe.wait_ge(S["t_mask"], 4 * (t - 1) + b + 1)
                    pe.wait_ge(S["t_qm"], 2 * t + b // 2 + 1)
                    nc.tensor.matmul(ps[:, b, :], t_x[1][:, b // 2, t * P:(t + 1) * P],
                                     t_qm[t % 2][:, b // 2, 4 * (b % 2):4 * (b % 2) + 4, :].rearrange("p h q -> p (h q)"),
                                     start=True, stop=True).then_inc(S["t_s"], 1)

            sc(0)
            for t in range(TT):
                if t + 1 < TT:
                    sc(t + 1)
                if t >= 2:
                    pe.wait_ge(S["t_oev"], t - 1)
                for c in range(DC):
                    nc.tensor.matmul(ps[:, 4 + t % 2, c * P:(c + 1) * P], t_x[0][:, c, t * P:(t + 1) * P],
                                     t_W0[:, c, :], start=True, stop=False, skip_group_check=True)
                    for hd in range(HPC * c, HPC * (c + 1)):
                        if hd % 4 == 0:
                            pe.wait_ge(S["t_mask"], 4 * t + hd // 4 + 1)
                        mm = nc.tensor.matmul(ps[:, 4 + t % 2, hd * DK:(hd + 1) * DK], t_S[t % 2][:, hd, :],
                                              t_v[:, t, hd * DK:(hd + 1) * DK], start=False,
                                              stop=True, skip_group_check=True)
                mm.then_inc(S["t_om"], 1)
            def turn(h):
                pe.wait_ge(*S.at("t_ln", h + 1))
                for t in range(TT // NH * h, TT // NH * (h + 1)):
                    for c in range(DC):
                        mm = nc.tensor.transpose(ps[:, 2 * c + h, (t % 4) * P:(t % 4 + 1) * P],
                                                 t_o[:, t, c * P:(c + 1) * P], ident)
                mm.then_inc(S["t_oT"], 1)

            def project(h):
                pe.wait_ge(S["t_gate"], DC * (h + 1))
                for m in range(DC):
                    for k in range(DC):
                        mm = nc.tensor.matmul(ps[:, 4 + 2 * h + m, :], t_w[4][:, k, m * P:(m + 1) * P],
                                              half(t_x[0], k, h), start=(k == 0), stop=(k == 1))
                    mm.then_inc(S["to_mm"], 1)
            turn(0)
            pe.wait_ge(S["t_oev"], TT)
            project(0)
            turn(1)
            project(1)

        def t_act(act):
            norm_act(act, "tn", U[1], U[2], 0)
            for g in range(16):
                n, m, h = g // 4, (g // 2) % 2, g % 2
                act.wait_ge(*S.at("tp_mm", g + 1))
                dst = (t_raw + [t_g])[n]
                nc.scalar.copy(half(dst, m, h), ps[:, g % 8, :]).then_inc(S["tp_ev_a"], 1)

            def silu(n):
                act.wait_ge(S["t_conv"], n + 1)
                x = t_x[n // 2][:, n % 2, :]
                nc.scalar.activation(x, x, ACT.Silu).then_inc(S["t_silu"], 1)
            for n in range(4):
                silu(n)
                act.wait_ge(S["t_silu"], n + 1)
                nc.scalar.activation(t_sq[n // 2][:, n % 2, :], t_x[n // 2][:, n % 2, :],
                                     ACT.Square).then_inc(S["t_sq"], 1)
            act.wait_ge(*S.at("t_ss", 1))
            nc.scalar.activation(t_ns[:, 0, :], ps[:, 4, 0:2 * P], ACT.Sqrt, bias=eps[:, 3:4]).then_inc(S["t_root"], 1)
            silu(4)
            silu(5)
            for n in range(4):
                act.wait_ge(S["t_vT"], n + 1)
                nc.scalar.copy(t_v[:, 2 * n:2 * n + 2, :].rearrange("p a b -> p (a b)"), ps[:, 4 + (n + 1) % 4, :])\
                    .then_inc(S["t_vev"], 1)

            def evict(t):
                act.wait_ge(S["t_om"], t + 1)
                nc.scalar.copy(t_o[:, t, :], ps[:, 4 + t % 2, 0:D]).then_inc(S["t_oev"], 1)

            def squares(h):
                act.wait_ge(S["t_cen"], h + 1)
                own = slice(TT // NH * h, TT // NH * (h + 1))
                nc.scalar.activation(t_osq[:, own, :], t_o[:, own, :], ACT.Square).then_inc(S["t_osq"], 1)

            def deviation(h):
                act.wait_ge(S["t_var"], h + 1)
                nc.scalar.activation(t_st[:, 1, h * TG:(h + 1) * TG], t_st[:, 0, h * TG:(h + 1) * TG], ACT.Sqrt,
                                     bias=eps[:, 0:1], scale=1.0 / DK).then_inc(S["t_sd"], 1)
            for t in range(TT - 2):
                evict(t)
            squares(0)
            evict(TT - 2)
            deviation(0)
            evict(TT - 1)
            squares(1)
            deviation(1)

        def t_dve(ch):
            dve, ln = ch.eng, ch.link
            v = nc.vector
            norm_dve(ch, "tn", xT, U[1], U[1])
            dve.wait_ge(*S.at("ld_t", dma_n["ld_t"]))
            for n in range(6):
                w, c = n // 2, n % 2
                dve.wait_ge(*S.at("tp_ev_a", 2 * n + 2))
                x, y = t_raw[w][:, c, :], t_x[w][:, c, :]
                x3, y3 = (z.rearrange("p (b t) -> p b t", t=L) for z in (x, y))
                ln(v.scalar_tensor_tensor(out=y, in0=x, scalar=t_cw[:, w, c, KW - 1:KW], in1=x,
                                          op0=ALU.mult, op1=ALU.add))
                for s in range(1, KW):
                    ins = v.scalar_tensor_tensor(out=y3[:, :, s:], in0=x3[:, :, :L - s],
                                                 scalar=t_cw[:, w, c, KW - 1 - s:KW - s], in1=y3[:, :, s:],
                                                 op0=ALU.mult, op1=ALU.add)
                    if s < KW - 1:
                        ln(ins)
                ins.then_inc(S["t_conv"], 1)
            dve.wait_ge(*S.at("t_root", 1))
            ln(v.reciprocal(t_ns[:, 1, :], t_ns[:, 0, :]))
            v.tensor_copy(t_rep.rearrange("p n t (h d) -> p (n t h) d", d=DK),
                          t_ns[:, 1, :].unsqueeze(2).broadcast_to([P, 2 * P, DK])).then_inc(S["t_rn"], 1)
            for g in range(8):
                x = half(t_x[g // 4], (g // 2) % 2, g % 2)
                dve.wait_ge(S["t_nrm"], g + 1)
                v.tensor_tensor(x, x, ps[:, g % 4, :], ALU.mult).then_inc(S["t_qk"], 1)

            def masked(t):
                if t >= 2:
                    dve.wait_ge(S["t_om"], t - 1)
                for b in range(4):
                    dve.wait_ge(S["t_s"], 4 * t + b + 1)
                    v.tensor_tensor(t_S[t % 2][:, 4 * b:4 * b + 4, :],
                                    ps[:, b, :].rearrange("p (h q) -> p h q", h=4),
                                    t_tril.unsqueeze(1).broadcast_to([P, 4, P]), ALU.mult).then_inc(S["t_mask"], 1)

            def heads(x, h):
                return x[:, TT // NH * h:TT // NH * (h + 1), :].rearrange("p t (h d) -> p (t h) d", d=DK)

            def stat(n, h):
                return t_st[:, n, h * TG:(h + 1) * TG]

            def wide(s):
                return s.unsqueeze(2).broadcast_to([P, TG, DK])

            def centre(h):
                dve.wait_ge(S["t_oev"], TT // NH * (h + 1))
                o4 = heads(t_o, h)
                ln(v.tensor_reduce(stat(0, h), o4, AX.X, ALU.add))
                ln(v.tensor_scalar(stat(1, h), stat(0, h), 1.0 / DK, None, ALU.mult))
                v.tensor_tensor(o4, o4, wide(stat(1, h)), ALU.subtract).then_inc(S["t_cen"], 1)

            def variance(h):
                dve.wait_ge(S["t_osq"], h + 1)
                v.tensor_reduce(stat(0, h), heads(t_osq, h), AX.X, ALU.add).then_inc(S["t_var"], 1)

            def scaled(h):
                o4 = heads(t_o, h)
                dve.wait_ge(S["t_sd"], h + 1)
                ln(v.reciprocal(stat(0, h), stat(1, h)))
                ln(v.tensor_tensor(o4, o4, wide(stat(0, h)), ALU.mult))
                ln(v.tensor_tensor(o4, o4, t_gam.unsqueeze(1).broadcast_to([P, TG, DK]), ALU.mult))
                v.tensor_tensor(o4, o4, t_bet.unsqueeze(1).broadcast_to([P, TG, DK]), ALU.add).then_inc(S["t_ln"], 1)

            def gated(h):
                dve.wait_ge(*S.at("t_oT", h + 1))
                for c in range(DC):
                    v.tensor_tensor(half(t_x[0], c, h), ps[:, 2 * c + h, :], half(t_g, c, h),
                                    ALU.mult).then_inc(S["t_gate"], 1)
            for t in range(TT - 1):
                masked(t)
            centre(0)
            masked(TT - 1)
            variance(0)
            scaled(0)
            centre(1)
            gated(0)
            variance(1)
            scaled(1)
            gated(1)
            for g in range(4):
                m, h = g % 2, g // 2
                dve.wait_ge(*S.at("to_mm", g + 1))
                ln(v.tensor_tensor(half(xT, m, h), half(xT, m, h), ps[:, 4 + g, :], ALU.add))

        def t_pool(pool):
            pool.wait_ge(S["t_qk"], 4)
            for t in range(TT):
                for c in range(DC):
                    if t >= 2:
                        pool.wait_ge(S["t_s"], 4 * (t - 2) + 2 * c + 2)
                    nc.gpsimd.tensor_tensor(t_qm[t % 2][:, c],
                                            t_x[0][:, c, t * P:(t + 1) * P].unsqueeze(1).broadcast_to([P, HPC, P]),
                                            hmask.unsqueeze(2).broadcast_to([P, HPC, P]),
                                            ALU.mult).then_inc(S["t_qm"], 1)

        FC = FH // P
        g_w1 = [view(21 * K + 1024 * j, DC, FH) for j in range(2)]
        g_w2 = [view(23 * K + 1024 * j, FC, D) for j in range(2)]
        g_b1 = [view(25 * K + 16 * j, FC) for j in range(2)]
        g_b2 = view(25 * K + 64, D)
        g_sa = view(26 * K, 2, HALF)
        g_h = [view(27 * K + 2048 * j, FC, HALF) for j in range(2)]

        def g_load(sp):
            sp.wait_ge(*S.at("gn_in", 1))
            load(sp, "ld_g", (f_R["w"], A["L1_ffn_gate_w"]), (f_R["b"], A["L1_ffn_gate_b"]), (g_b2[0:E], A["L1_ffn_b2"]), shared="loads")

            def expert(e, j):
                for dst, src in ((g_w1[j], "w1"), (g_w2[j], "w2"), (g_b1[j].unsqueeze(1), "b1")):
                    sp.dma_start(dst, A["L1_ffn_" + src][:, bass.ds(e, 1)].rearrange("p a k f -> p (a k) f"))\
                        .then_inc(S[f"ge_wt{j}"], 16)
            expert(0, 0)
            expert(1, 1)
            with sp.Fori(1, E // 2) as i:
                for j in range(2):
                    sp.wait_ge(S["ge_w2"], 4 * i + 2 * j - 2)
                    expert(2 * i + j, j)

        def g_pe(pe):
            norm_pe(pe, "gn", xT, U[2])
            pe.wait_ge(*S.at("gn_out", 2))
            pe.wait_ge(*S.at("ld_g", dma_n["ld_g"]))
            route_pe(pe, "gr", f_R, U[1])

            def up(v, h, j, e):
                for f in range(FC):
                    r = 4 * v + f
                    if not isinstance(v, int) or r >= 2:
                        pe.wait_ge(S["ge_sa"], r - 1)
                    for k in range(DC):
                        mm = nc.tensor.matmul(ps[:, 4 + f % 2, :], g_w1[j][:, k, f * P:(f + 1) * P],
                                              half(U[1], k, h), start=(k == 0), stop=(k == 1))
                    mm.then_inc(S["ge_a"], 1)
                    if f == 0:
                        if not isinstance(v, int) or v >= 2:
                            pe.wait_ge(S["ge_h"], 4 * v - 4)
                        weight_pe(f_R, e, h).then_inc(S["ge_c"], 1)

            def down(v, h, j, stop):
                pe.wait_ge(S["ge_h"], 4 * v + 4)
                for m in range(DC):
                    for f in range(FC):
                        mm = nc.tensor.matmul(ps[:, 2 * m + h, :], g_w2[j][:, f, m * P:(m + 1) * P], g_h[h][:, f, :],
                                              start=False, stop=stop and f == FC - 1, skip_group_check=True)
                mm.then_inc(S["ge_w2"], 1)

            pe.wait_ge(S["gr_part"], 1)
            for m in range(DC):
                for h in range(NH):
                    nc.tensor.matmul(ps[:, 2 * m + h, :], g_b2[0:E, m * P:(m + 1) * P],
                                     f_R["cT"][0:E, h * HALF:(h + 1) * HALF], start=True, stop=False,
                                     skip_group_check=True)

            def expert_pair(i, first_pair):
                for j in range(2):
                    v = 4 * i + 2 * j
                    pe.wait_ge(*S.at(f"ge_wt{j}", 48 * i + 48))
                    up(v, 0, j, 2 * i + j)
                    if not (first_pair and j == 0):
                        down(v - 1, 1, 1 - j, False)
                    up(v + 1, 1, j, 2 * i + j)
                    down(v, 0, j, False)
            expert_pair(0, True)
            with pe.Fori(1, E // 2) as i:
                expert_pair(i, False)
            down(2 * E - 1, 1, 1, True)

        def g_act(act):
            norm_act(act, "gn", U[1], U[2], 0)
            route_act(act, "gr", f_R, False)

            def relu(r, f, j):
                act.wait_ge(S["ge_a"], r + 1)
                if not isinstance(r, int) or r >= 2:
                    act.wait_ge(S["ge_h"], r - 1)
                nc.scalar.activation(g_sa[:, f % 2, :], ps[:, 4 + f % 2, :], ACT.Relu,
                                     bias=g_b1[j][:, f:f + 1]).then_inc(S["ge_sa"], 1)

            def pair(i):
                for j in range(2):
                    act.wait_ge(*S.at(f"ge_wt{j}", 48 * i + 48))
                    for n in range(2 * FC):
                        relu(16 * i + 8 * j + n, n % FC, j)
            pair(0)
            with act.Fori(1, E // 2) as i:
                pair(i)

        def g_dve(ch):
            dve = ch.eng
            norm_dve(ch, "gn", xT, U[1], U[1])
            dve.wait_ge(*S.at("ld_g", dma_n["ld_g"]))
            route_dve(ch, "gr", f_R, False)
            route_parts(ch, "gr", f_R)

            def product(v, h):
                dve.wait_ge(S["ge_c"], v + 1)
                if not isinstance(v, int) or v >= 2:
                    dve.wait_ge(S["ge_w2"], v - 1)
                for f in range(FC):
                    dve.wait_ge(S["ge_sa"], 4 * v + f + 1)
                    nc.vector.tensor_tensor(g_h[h][:, f, :], g_sa[:, f % 2, :], ps[:, 6 + h, :],
                                            ALU.mult).then_inc(S["ge_h"], 1)
            product(0, 0)
            product(1, 1)
            with dve.Fori(1, E) as i:
                for h in range(NH):
                    product(2 * i + h, h)
            dve.wait_ge(S["ge_w2"], 2 * E)
            for g in range(4):
                ch.link(nc.vector.tensor_tensor(half(xT, g // 2, g % 2), half(xT, g // 2, g % 2),
                                                ps[:, g, :], ALU.add))

        def g_pool(pool):
            route_pool(pool, "gr", f_R, "gn_in")


        stages = {0: (x_loads, x_pe, x_act, x_dve, x_pool)}
        stages[1] = (m_load, m_pe, m_act, m_dve, m_pool)
        stages[2] = (f_load, f_pe, f_act, f_dve, f_pool)
        stages[3] = (d_load, d_pe, d_act, d_dve, d_pool)
        stages[4] = (t_load, t_pe, t_act, t_dve, t_pool)
        stages[5] = (g_load, g_pe, g_act, g_dve, g_pool)
        block = ctx.enter_context(nc.Block())

        @block.sync
        def _(sp):
            x_load(sp)
            for s in range(first, last + 1):
                stages[s][0](sp)
            sp.wait_ge(S["all_done"], 1)
            sp.dma_start(out, xT).then_inc(S["stored"], 16)
            sp.wait_ge(S["stored"], 16)

        @block.vector
        def _(dve):
            ch = Chain(dve, S["dve_own"])
            dve.wait_ge(S["ld_const"], dma_n["ld_const"])
            ch.link(nc.vector.tensor_copy(identb, ident))
            for s in range(first, last + 1):
                signal(("xn", "mn", "fn", "dn", "tn", "gn")[s] + "_in")
                stages[s][3](ch)
            signal("all_done")

        @block.scalar
        def _(act):
            for s in range(first, last + 1):
                stages[s][2](act)

        @block.gpsimd
        def _(pool):
            for s in range(first, last + 1):
                stages[s][4](pool)

        @block.tensor
        def _(pe):
            for s in range(first, last + 1):
                stages[s][1](pe)


def feat(w):
    w = np.asarray(w)
    return np.ascontiguousarray(w.T.reshape(w.shape[1] // P, P, w.shape[0]).transpose(1, 0, 2))


def cols(v):
    v = np.asarray(v)
    return np.ascontiguousarray(v.reshape(-1, P).T)


def constants():
    def split(v):
        parts = []
        for _ in range(3):
            parts.append((v.view(np.uint32) & np.uint32(0xFFFF0000)).view(np.float32))
            v = v - parts[-1]
        return parts

    p = np.arange(P)
    c = {
        "c_ident": np.eye(P, dtype=np.float32),
        "c_mean": np.full((P, P), 1.0 / D, np.float32),
        "c_hmask": (p[:, None] // DK == np.arange(HPC)[None]).astype(np.float32),
        "c_ones": np.ones((P, 32), np.float32),
        "c_eps": np.tile(np.array([1e-5, np.finfo(np.float32).eps, 1e-6, 1e-12], np.float32), (P, 1)),
        "c_iota8": np.tile(np.arange(E, dtype=np.float32), (P, 1)),
    }
    slopes = np.array([2.0 ** (-8.0 * (i + 1) / XH) for i in range(XH)], np.float32)
    sl = np.repeat(slopes.reshape(4, 4), L, axis=1)
    qs = -(sl * np.tile(np.arange(L, dtype=np.float32), 4)[None])
    c["c_slope"] = np.ascontiguousarray(np.stack(split(sl) + split(qs)))
    pos = np.arange(SK, dtype=np.float32)
    c["c_pos"] = np.stack([pos] * 3 + [np.ones_like(pos)] * 3)
    hq = np.repeat(np.arange(HPC), L)
    c["c_dmask"] = np.tile((p[:, None] // DK == hq[None]).astype(np.float32), (1, DC))
    head = np.arange(2)[None, :, None] * 4 + p[:, None, None] // L
    c["c_pick"] = np.ascontiguousarray(head == p[None, None, :] // DK).astype(np.float32)
    c["c_own"] = (p[:, None] % L == np.arange(L)[None]).astype(np.float32)
    tok = p // L
    c["c_neg"] = np.where(tok[:, None] == tok[None], 0.0, -BIG).astype(np.float32)
    c["c_tril"] = ((tok[:, None] == tok[None]) & (p[:, None] <= p[None])).astype(np.float32)
    return c


def layout(inputs):
    a = {}
    a["x"] = feat(np.asarray(inputs["x"]).reshape(T, D))
    ctx = np.asarray(inputs["ctx_1024"])
    a["ctxT"] = feat(ctx.reshape(B * SK, D))
    a["ctx_lastT"] = feat(ctx[:, SK - 1])
    for n in ("w_q", "w_k", "w_v", "w_o"):
        a["L0_xattn_" + n] = feat(inputs["L0_xattn_" + n])
    a["L0_xattn_b_o"] = cols(inputs["L0_xattn_b_o"])
    pre = "L0_attn_"
    a[pre + "norm_w"] = cols(inputs[pre + "norm_w"])
    for n in ("W_in", "W_out"):
        a[pre + n] = feat(inputs[pre + n])
    wx = np.asarray(inputs["L0_attn_W_x"])
    a["L0_attn_W_x"] = feat(np.concatenate([wx[:64], wx[64:128], wx[64:128], wx[128:], wx[128:]]))
    a[pre + "W_dt"] = np.ascontiguousarray(np.asarray(inputs[pre + "W_dt"]).T)
    for n in ("conv_b", "Dp", "b_dt"):
        a[pre + n] = cols(inputs[pre + n])
    a[pre + "conv_w"] = np.ascontiguousarray(np.asarray(inputs[pre + "conv_w"]).reshape(IC, P, KW).transpose(1, 0, 2))
    a[pre + "A_log"] = np.ascontiguousarray(np.asarray(inputs[pre + "A_log"]).reshape(IC, P, NS).transpose(1, 0, 2))
    pre = "L0_ffn_"
    a[pre + "Wq"], a[pre + "Wo"] = feat(inputs[pre + "Wq"]), feat(inputs[pre + "Wo"])
    k, v = feat(inputs[pre + "Wkc"]), feat(inputs[pre + "Wvc"])
    a[pre + "Wkv"] = np.concatenate([k, k, v, v], axis=2)
    a[pre + "g1"], a[pre + "g2"] = cols(inputs[pre + "g1"]), cols(inputs[pre + "g2"])
    a[pre + "Wr"] = feat(inputs[pre + "Wr"])
    a[pre + "expert_bias"] = np.ascontiguousarray(np.broadcast_to(np.asarray(inputs[pre + "expert_bias"]), (P, E)))
    a[pre + "sW13"] = np.concatenate([feat(inputs[pre + "sW1"]), feat(inputs[pre + "sW3"])], axis=2)
    a[pre + "sW2"] = feat(inputs[pre + "sW2"])
    a[pre + "eW13"] = np.stack([np.concatenate([feat(w1), feat(w3)], axis=2) for w1, w3 in
                                zip(np.asarray(inputs[pre + "eW1"]), np.asarray(inputs[pre + "eW3"]))], axis=1)
    a[pre + "eW2"] = np.stack([feat(w) for w in np.asarray(inputs[pre + "eW2"])], axis=1)
    rt = -(-SK // 3)
    back = np.concatenate([ctx[:, ::-1], np.zeros((B, 3 * rt - SK, D), np.float32)], axis=1)
    a["ctx_rows"] = np.ascontiguousarray(back.reshape(B, 3, rt, D).transpose(2, 0, 1, 3))
    pre = "L1_attn_"
    for x in "qkvgo":
        a[pre + "W" + x] = feat(inputs[pre + "W" + x])
    a[pre + "conv"] = np.stack([np.asarray(inputs[pre + "conv_" + x]).reshape(DC, P, KW).transpose(1, 0, 2)
                                for x in "qkv"], axis=1)
    w0 = np.zeros((P, DC, P), np.float32)
    for h in range(XH):
        r = DK * (h % HPC)
        w0[r:r + DK, h // HPC, r:r + DK] = np.asarray(inputs[pre + "W_init"])[0, h]
    a[pre + "W_init"] = w0
    for n in ("ln_gamma", "ln_beta"):
        a[pre + n] = np.ascontiguousarray(np.broadcast_to(np.asarray(inputs[pre + n]), (P, DK)))
    pre = "L1_ffn_"
    a[pre + "gate_w"] = feat(np.asarray(inputs[pre + "gate_w"]).T)
    a[pre + "gate_b"] = np.ascontiguousarray(np.broadcast_to(np.asarray(inputs[pre + "gate_b"]), (P, E)))
    a[pre + "w1"] = np.stack([feat(w.T) for w in np.asarray(inputs[pre + "w1"])], axis=1)
    a[pre + "w2"] = np.stack([feat(w.T) for w in np.asarray(inputs[pre + "w2"])], axis=1)
    a[pre + "b1"] = np.ascontiguousarray(np.asarray(inputs[pre + "b1"]).reshape(E, 1, FH // P, P).transpose(3, 0, 1, 2))
    a[pre + "b2"] = np.ascontiguousarray(np.asarray(inputs[pre + "b2"]))
    return a


def kernel(**inputs):
    import concourse.bacc as _bacc
    from concourse.bass_utils import run_bass_kernel_spmd as _run

    nc = _bacc.Bacc("TRN2", target_bir_lowering=False, num_devices=1)
    arrays = {**layout(inputs), **constants()}
    aps = {n: nc.dram_tensor(n, a.shape, mybir.dt.from_np(a.dtype), kind="ExternalInput").ap()
           for n, a in arrays.items()}
    out = nc.dram_tensor("out", (P, DC, T), F32, kind="ExternalOutput").ap()
    build(nc, aps, out)
    r = _run(nc, [arrays], core_ids=[0])
    got = np.asarray(r.results[0]["out"])
    return np.ascontiguousarray(got.transpose(2, 1, 0).reshape(B, L, D))
```
